# Optimizing a Trainium2 kernel written in Bass

```python
import numpy as np
import jax
import jax.numpy as jnp

def _softmax(x, axis=-1):
    return jax.nn.softmax(x, axis=axis)

def _gelu(x):
    return jax.nn.gelu(x, approximate=True)

def _silu(x):
    return jax.nn.silu(x)

def _sigmoid(x):
    return jax.nn.sigmoid(x)

def _layernorm(x, axis=-1, eps=1e-05):
    m = jnp.mean(x, axis=axis, keepdims=True)
    v = jnp.var(x, axis=axis, keepdims=True)
    return (x - m) / jnp.sqrt(v + eps)

def _scatter_add(tgt, idx, src, axis=0):
    return tgt.at[idx].add(src)

def _segment_sum(src, seg, n):
    return jax.ops.segment_sum(src, seg, n)
kernel_name = 'mk_gnn_preln_d2_gnn_r32_1f9c1e'

def setup_inputs(seed: int=0):
    np.random.seed(seed)
    _w = jnp.asarray

    def _rec_inputs():
        import jax
        import jax.numpy as jnp
        _gk = jax.random.key(seed)
        x = -0.000202 + 1 * jax.random.normal(jax.random.fold_in(_gk, 1), (3125, 64), jnp.float32)
        _s = jax.random.randint(jax.random.fold_in(_gk, 2), (25000,), 0, 3125, jnp.int32)
        _d = jax.random.randint(jax.random.fold_in(_gk, 3), (25000,), 0, 3125, jnp.int32)
        _loop = jnp.arange(3125, dtype=jnp.int32)
        src = jnp.concatenate([_s, _d, _loop])
        dst = jnp.concatenate([_d, _s, _loop])
        _o = jnp.argsort(dst, stable=True)
        src = src[_o]
        dst = dst[_o]
        edge_attr_16 = 0.000196303 + 1.00016 * jax.random.normal(jax.random.fold_in(_gk, 12), (53125, 16), jnp.float32)
        return (x, src, dst, edge_attr_16)
    x, src, dst, edge_attr_16 = _rec_inputs()

    def _L0_gnn_setup():
        import jax, jax.numpy as jnp
        import numpy as np
        N, E, HID, KEY, EDGE, H = (3125, 50000, 64, 64, 16, 4)
        DK, DH = (KEY // H, HID // H)
        LOG2 = float(np.log(2.0))

        def ssp(x):
            return jax.nn.softplus(x) - LOG2
        key = jax.random.key(seed)
        ks = jax.random.split(key, 24)
        s = 0.05
        inp = {'node_attr': jax.random.normal(ks[0], (N, HID), jnp.float32), 'edge_index': jax.random.randint(ks[1], (2, E), 0, N, jnp.int64), 'edge_attr': jax.random.normal(ks[2], (E, EDGE), jnp.float32), 'Wk': jax.random.normal(ks[3], (H, DK, DH), jnp.float32) * s, 'Wq': jax.random.normal(ks[4], (H, DK, DH), jnp.float32) * s, 'Wv': jax.random.normal(ks[5], (H, DH, DH), jnp.float32) * s, 'wk1_w': jax.random.normal(ks[6], (EDGE, DK), jnp.float32) * s, 'wk1_b': jnp.zeros((DK,), jnp.float32), 'wk2_w': jax.random.normal(ks[7], (DK, DK), jnp.float32) * s, 'wk2_b': jnp.zeros((DK,), jnp.float32), 'wkl_w': jax.random.normal(ks[8], (DK, DK), jnp.float32) * s, 'wkl_b': jnp.zeros((DK,), jnp.float32), 'wv1_w': jax.random.normal(ks[9], (EDGE, DH), jnp.float32) * s, 'wv1_b': jnp.zeros((DH,), jnp.float32), 'wv2_w': jax.random.normal(ks[10], (DH, DH), jnp.float32) * s, 'wv2_b': jnp.zeros((DH,), jnp.float32), 'wvl_w': jax.random.normal(ks[11], (DH, DH), jnp.float32) * s, 'wvl_b': jnp.zeros((DH,), jnp.float32), 'cen_w': jax.random.normal(ks[12], (HID, HID), jnp.float32) * s, 'cen_b': jnp.zeros((HID,), jnp.float32), 'out_w': jax.random.normal(ks[13], (HID, HID), jnp.float32) * s, 'out_b': jnp.zeros((HID,), jnp.float32), 'ln_g': jnp.ones((HID,), jnp.float32), 'ln_b': jnp.zeros((HID,), jnp.float32)}
        return inp
    _L0_gnn_all = _L0_gnn_setup()
    _L0_gnn_in = {k: v for k, v in _L0_gnn_all.items() if k in ('Wk', 'Wq', 'Wv', 'wk1_w', 'wk1_b', 'wk2_w', 'wk2_b', 'wkl_w', 'wkl_b', 'wv1_w', 'wv1_b', 'wv2_w', 'wv2_b', 'wvl_w', 'wvl_b', 'cen_w', 'cen_b', 'out_w', 'out_b', 'ln_g', 'ln_b')}
    del _L0_gnn_all

    def _L1_gnn_setup():
        import jax, jax.numpy as jnp
        import numpy as np
        N, E, D, H, HID = (50000, 12500, 64, 8, 1024)
        NEG_SLOPE = 0.2
        BN_EPS = 1e-05

        def _batchnorm(h, gamma, beta):
            mu = h.mean(axis=0)
            var = h.var(axis=0)
            return gamma * (h - mu) * jax.lax.rsqrt(var + BN_EPS) + beta
        key = jax.random.key(seed)
        ks = jax.random.split(key, 10)
        s = 0.05
        return {'x': jax.random.normal(ks[0], (N, D), jnp.float32), 'src': jax.random.randint(ks[1], (E,), 0, N, jnp.int32), 'dst': jax.random.randint(ks[2], (E,), 0, N, jnp.int32), 'fc_w': jax.random.normal(ks[3], (H * D, D), jnp.float32) * s, 'attn_l': jax.random.normal(ks[4], (H, D), jnp.float32) * s, 'attn_r': jax.random.normal(ks[5], (H, D), jnp.float32) * s, 'gat_bias': jnp.zeros((H * D,), jnp.float32), 'bn1_gamma': jnp.ones((H * D,), jnp.float32), 'bn1_beta': jnp.zeros((H * D,), jnp.float32), 'w1': jax.random.normal(ks[6], (HID, H * D), jnp.float32) * s, 'b1': jnp.zeros((HID,), jnp.float32), 'w2': jax.random.normal(ks[7], (D, HID), jnp.float32) * s, 'b2': jnp.zeros((D,), jnp.float32), 'bn2_gamma': jnp.ones((D,), jnp.float32), 'bn2_beta': jnp.zeros((D,), jnp.float32)}
    _L1_gnn_all = _L1_gnn_setup()
    _L1_gnn_in = {k: v for k, v in _L1_gnn_all.items() if k in ('fc_w', 'attn_l', 'attn_r', 'gat_bias', 'bn1_gamma', 'bn1_beta', 'w1', 'b1', 'w2', 'b2', 'bn2_gamma', 'bn2_beta')}
    del _L1_gnn_all
    return {'x': x, 'src': src, 'dst': dst, 'edge_attr_16': edge_attr_16, 'L0_gnn_Wk': _L0_gnn_in['Wk'], 'L0_gnn_Wq': _L0_gnn_in['Wq'], 'L0_gnn_Wv': _L0_gnn_in['Wv'], 'L0_gnn_wk1_w': _L0_gnn_in['wk1_w'], 'L0_gnn_wk1_b': _L0_gnn_in['wk1_b'], 'L0_gnn_wk2_w': _L0_gnn_in['wk2_w'], 'L0_gnn_wk2_b': _L0_gnn_in['wk2_b'], 'L0_gnn_wkl_w': _L0_gnn_in['wkl_w'], 'L0_gnn_wkl_b': _L0_gnn_in['wkl_b'], 'L0_gnn_wv1_w': _L0_gnn_in['wv1_w'], 'L0_gnn_wv1_b': _L0_gnn_in['wv1_b'], 'L0_gnn_wv2_w': _L0_gnn_in['wv2_w'], 'L0_gnn_wv2_b': _L0_gnn_in['wv2_b'], 'L0_gnn_wvl_w': _L0_gnn_in['wvl_w'], 'L0_gnn_wvl_b': _L0_gnn_in['wvl_b'], 'L0_gnn_cen_w': _L0_gnn_in['cen_w'], 'L0_gnn_cen_b': _L0_gnn_in['cen_b'], 'L0_gnn_out_w': _L0_gnn_in['out_w'], 'L0_gnn_out_b': _L0_gnn_in['out_b'], 'L0_gnn_ln_g': _L0_gnn_in['ln_g'], 'L0_gnn_ln_b': _L0_gnn_in['ln_b'], 'L1_gnn_fc_w': _L1_gnn_in['fc_w'], 'L1_gnn_attn_l': _L1_gnn_in['attn_l'], 'L1_gnn_attn_r': _L1_gnn_in['attn_r'], 'L1_gnn_gat_bias': _L1_gnn_in['gat_bias'], 'L1_gnn_bn1_gamma': _L1_gnn_in['bn1_gamma'], 'L1_gnn_bn1_beta': _L1_gnn_in['bn1_beta'], 'L1_gnn_w1': _L1_gnn_in['w1'], 'L1_gnn_b1': _L1_gnn_in['b1'], 'L1_gnn_w2': _L1_gnn_in['w2'], 'L1_gnn_b2': _L1_gnn_in['b2'], 'L1_gnn_bn2_gamma': _L1_gnn_in['bn2_gamma'], 'L1_gnn_bn2_beta': _L1_gnn_in['bn2_beta']}

def reference(x, src, dst, edge_attr_16, L0_gnn_Wk, L0_gnn_Wq, L0_gnn_Wv, L0_gnn_wk1_w, L0_gnn_wk1_b, L0_gnn_wk2_w, L0_gnn_wk2_b, L0_gnn_wkl_w, L0_gnn_wkl_b, L0_gnn_wv1_w, L0_gnn_wv1_b, L0_gnn_wv2_w, L0_gnn_wv2_b, L0_gnn_wvl_w, L0_gnn_wvl_b, L0_gnn_cen_w, L0_gnn_cen_b, L0_gnn_out_w, L0_gnn_out_b, L0_gnn_ln_g, L0_gnn_ln_b, L1_gnn_fc_w, L1_gnn_attn_l, L1_gnn_attn_r, L1_gnn_gat_bias, L1_gnn_bn1_gamma, L1_gnn_bn1_beta, L1_gnn_w1, L1_gnn_b1, L1_gnn_w2, L1_gnn_b2, L1_gnn_bn2_gamma, L1_gnn_bn2_beta):
    import jax
    import jax.numpy as jnp

    def _L0_gnn_ref(node_attr, edge_index, edge_attr, Wk, Wq, Wv, wk1_w, wk1_b, wk2_w, wk2_b, wkl_w, wkl_b, wv1_w, wv1_b, wv2_w, wv2_b, wvl_w, wvl_b, cen_w, cen_b, out_w, out_b, ln_g, ln_b):
        import jax, jax.numpy as jnp
        import numpy as np
        N, E, HID, KEY, EDGE, H = (3125, 50000, 64, 64, 16, 4)
        DK, DH = (KEY // H, HID // H)
        LOG2 = float(np.log(2.0))

        def ssp(x):
            return jax.nn.softplus(x) - LOG2
        row, col = (edge_index[0], edge_index[1])
        x = node_attr.reshape(N, H, DH)
        h_keys = jnp.einsum('nhd,hkd->nhk', x, Wk)
        h_queries = jnp.einsum('nhd,hkd->nhk', x, Wq)
        h_values = jnp.einsum('nhd,hvd->nhv', x, Wv)
        W_k = ssp(edge_attr @ wk1_w + wk1_b) @ wk2_w + wk2_b
        keys_j = W_k[:, None, :] * h_keys[col] @ wkl_w + wkl_b
        queries_i = h_queries[row]
        qk = jnp.sum(queries_i * keys_j, -1) / jnp.sqrt(jnp.float32(DK))
        seg_max = jax.ops.segment_max(qk, row, num_segments=N)
        ex = jnp.exp(qk - seg_max[row])
        seg_sum = jax.ops.segment_sum(ex, row, num_segments=N)
        alpha = ex / (seg_sum[row] + 1e-16)
        W_v = ssp(edge_attr @ wv1_w + wv1_b) @ wv2_w + wv2_b
        msg_j = W_v[:, None, :] * h_values[col] @ wvl_w + wvl_b
        msg_j = alpha[:, :, None] * msg_j
        aggr = jax.ops.segment_sum(msg_j, row, num_segments=N).reshape(N, HID)
        out = node_attr @ cen_w + cen_b + aggr
        out = ssp(out) @ out_w + out_b
        mu = jnp.mean(out, -1, keepdims=True)
        var = jnp.var(out, -1, keepdims=True)
        return (out - mu) / jnp.sqrt(var + 1e-05) * ln_g + ln_b

    def _L1_gnn_ref(x, src, dst, fc_w, attn_l, attn_r, gat_bias, bn1_gamma, bn1_beta, w1, b1, w2, b2, bn2_gamma, bn2_beta):
        import jax, jax.numpy as jnp
        import numpy as np
        N, E, D, H, HID = (50000, 12500, 64, 8, 1024)
        NEG_SLOPE = 0.2
        BN_EPS = 1e-05

        def _batchnorm(h, gamma, beta):
            mu = h.mean(axis=0)
            var = h.var(axis=0)
            return gamma * (h - mu) * jax.lax.rsqrt(var + BN_EPS) + beta
        n = x.shape[0]
        nh, dh = attn_l.shape
        feat = (x @ fc_w.T).reshape(n, nh, dh)
        el = jnp.einsum('nhd,hd->nh', feat, attn_l)
        er = jnp.einsum('nhd,hd->nh', feat, attn_r)
        e = jax.nn.leaky_relu(el[src] + er[dst], NEG_SLOPE)
        emax = jax.ops.segment_max(e, dst, num_segments=n)
        emax = jnp.where(jnp.isfinite(emax), emax, 0.0)
        ez = jnp.exp(e - emax[dst])
        denom = jax.ops.segment_sum(ez, dst, num_segments=n)
        alpha = ez / denom[dst]
        msg = alpha[:, :, None] * feat[src]
        rst = jax.ops.segment_sum(msg, dst, num_segments=n)
        rst = rst + gat_bias.reshape(nh, dh)
        h = rst.reshape(n, nh * dh)
        h = _batchnorm(h, bn1_gamma, bn1_beta)
        h = jax.nn.relu(h @ w1.T + b1)
        h = h @ w2.T + b2
        h = _batchnorm(h, bn2_gamma, bn2_beta)
        return h
    edge_index = jnp.stack([src, dst])
    h = jnp.maximum(_layernorm(x, axis=-1), 0.0)
    x = x + _L0_gnn_ref(h, edge_index, edge_attr_16, L0_gnn_Wk, L0_gnn_Wq, L0_gnn_Wv, L0_gnn_wk1_w, L0_gnn_wk1_b, L0_gnn_wk2_w, L0_gnn_wk2_b, L0_gnn_wkl_w, L0_gnn_wkl_b, L0_gnn_wv1_w, L0_gnn_wv1_b, L0_gnn_wv2_w, L0_gnn_wv2_b, L0_gnn_wvl_w, L0_gnn_wvl_b, L0_gnn_cen_w, L0_gnn_cen_b, L0_gnn_out_w, L0_gnn_out_b, L0_gnn_ln_g, L0_gnn_ln_b)
    h = jnp.maximum(_layernorm(x, axis=-1), 0.0)
    x = x + _L1_gnn_ref(h, src, dst, L1_gnn_fc_w, L1_gnn_attn_l, L1_gnn_attn_r, L1_gnn_gat_bias, L1_gnn_bn1_gamma, L1_gnn_bn1_beta, L1_gnn_w1, L1_gnn_b1, L1_gnn_w2, L1_gnn_b2, L1_gnn_bn2_gamma, L1_gnn_bn2_beta)
    return x

_drawn_inputs = setup_inputs


def setup_inputs(seed=0):
    import zlib

    import numpy as np

    out = dict(_drawn_inputs(seed))
    spreads = {'L0_gnn_wk1_b': (0.0, 0.8),
     'L0_gnn_wk2_b': (0.0, 0.8),
     'L0_gnn_wkl_b': (0.0, 2.0),
     'L0_gnn_wv1_b': (0.0, 0.8),
     'L0_gnn_wv2_b': (0.0, 0.8),
     'L0_gnn_wvl_b': (0.0, 2.0),
     'L0_gnn_cen_b': (0.0, 2.0),
     'L0_gnn_out_b': (0.0, 0.637),
     'L0_gnn_ln_g': (1.0, 0.2),
     'L0_gnn_ln_b': (0.0, 0.1),
     'L1_gnn_gat_bias': (0.0, 2.0),
     'L1_gnn_bn1_gamma': (1.0, 0.2),
     'L1_gnn_bn1_beta': (0.0, 0.1),
     'L1_gnn_b1': (0.0, 0.1),
     'L1_gnn_b2': (0.0, 2.0),
     'L1_gnn_bn2_gamma': (1.0, 0.2),
     'L1_gnn_bn2_beta': (0.0, 0.1)}
    factors = {'edge_attr_16': 8.0,
     'L0_gnn_Wk': 8.0,
     'L0_gnn_Wq': 8.0,
     'L0_gnn_Wv': 8.0,
     'L0_gnn_wk1_w': 8.0,
     'L0_gnn_wk2_w': 8.0,
     'L0_gnn_wkl_w': 8.0,
     'L0_gnn_wv1_w': 8.0,
     'L0_gnn_wv2_w': 8.0,
     'L0_gnn_wvl_w': 8.0,
     'L1_gnn_attn_r': 3.984,
     'L0_gnn_cen_w': 6.071}
    for name, (base, spread) in spreads.items():
        noise = np.random.default_rng([zlib.crc32(name.encode()), seed]).standard_normal(out[name].shape)
        drawn = base * np.exp(spread * noise) if base else spread * noise
        out[name] = jnp.asarray(drawn.astype(out[name].dtype))
    for name, factor in factors.items():
        out[name] = (out[name] * factor).astype(out[name].dtype)
    return out
```

```python
from contextlib import ExitStack

import numpy as np
import concourse.bass as bass
from concourse import mybir

F32 = mybir.dt.float32
I32 = mybir.dt.int32
ALU = mybir.AluOpType
ACT = mybir.ActivationFunctionType
AXX = mybir.AxisListType.X
PE = mybir.EngineType.PE
DVE = mybir.EngineType.DVE

P = 128
B = 64
G = 4
BIG = 3.0e38


def bc(ap, shape):
    return ap.to_broadcast(shape)


class Link:

    def __init__(self, eng, sem):
        self.eng, self.sem, self.base, self.n = eng, sem, 0, 0

    def __call__(self, ins):
        self.n += 1
        ins.then_inc(self.sem, 1)
        self.eng.wait_ge(self.sem, self.base + self.n)

    def loop(self, start, it, per):
        self.base, self.n = it * per + start, 0


def upto(it, par, k=1):
    return it * (2 * k) + k * (par + 1)


def tiles(it, par):
    return bass.ds(it * (2 * G) + par * G, G)


class Env:
    pass


def blocks_of(nc, engine, blk, it, NB):
    _, v = nc.values_load_multi_w_load_instructions(
        blk[0:1, bass.ds(it * (2 * G), 2 * G)], engines=[engine], min_val=0, max_val=NB - 1,
        skip_runtime_bounds_check_because="base_vector cuts them off at the last block")
    return v


BANK = 512


def banks(nc, st, name, shape):
    size = int(np.prod(shape[1:]))
    full = -(-size // BANK) * BANK
    t = st.enter_context(nc.psum_tensor(name, [P, full], F32))
    v = t[0:shape[0], 0:size]
    if len(shape) == 3:
        v = v.rearrange("p (a b) -> p a b", a=shape[1])
    return v


def masks(nc, E, sb, s_mask):
    E.ones = sb("ones", [P, P], F32)
    E.ident = sb("ident", [P, P], F32)
    E.before = sb("before", [P, P], F32)
    E.after = sb("after", [P, P], F32)
    E.iota_i = sb("iota_i", [P, E.NT], I32)
    E.iota = sb("iota", [P, E.NT], F32)


def masks_pool(nc, pool, E, s_ones, s_mask):
    nc.gpsimd.memset(E.ones[:, :], 1.0).then_inc(s_ones, 1)
    pool.wait_ge(s_ones, 1)
    for out, cmp, way in ((E.ident, ALU.is_equal, 1), (E.before, ALU.is_gt, 1), (E.after, ALU.is_gt, -1)):
        nc.gpsimd.affine_select(out=out[:, :], in_=E.ones[:, :], pattern=[[-way, P]], compare_op=cmp, fill=0.0,
                                base=0, channel_multiplier=way)
    nc.gpsimd.iota(E.iota_i[:, :], pattern=[[1, E.NT]], base=0, channel_multiplier=0).then_inc(s_mask, 1)


class Rank:

    def __init__(self, nc, sb, ps, sem, n):
        self.oh = sb(n + "_oh", [P, 2, 2, G, B], F32)
        self.kg = sb(n + "_kg", [P, 2, G], F32)
        self.ohT = sb(n + "_ohT", [B, 2, G, P], F32)
        self.T = sb(n + "_T", [B, 2, G, B], F32)
        self.tmp = sb(n + "_tmp", [P, G, B], F32)
        self.junk = sb(n + "_junk", [P, G, P], F32)
        self.r1 = sb(n + "_r1", [P, G], F32)
        self.r2 = sb(n + "_r2", [P, G], F32)
        self.posf = sb(n + "_posf", [P, G], F32)
        self.posi = sb(n + "_posi", [P, 3, G], I32)
        self.row = sb(n + "_row", [P, 2, G], I32)
        self.psH = ps(n + "_psH", [B, G, B], F32)
        self.psL = ps(n + "_psL", [P, G, B], F32)
        self.psHT = ps(n + "_psHT", [B, G, P], F32)
        self.psK = ps(n + "_psK", [P, G, P], F32)
        self.oh_ready = sem(n + "_oh_ready")
        self.hist_ready = sem(n + "_hist_ready")
        self.T_ready = sem(n + "_T_ready")
        self.hT_ready = sem(n + "_hT_ready")
        self.ohT_ready = sem(n + "_ohT_ready")
        self.keyrow_ready = sem(n + "_keyrow_ready")
        self.keyrow_free = sem(n + "_keyrow_free")
        self.look_ready = sem(n + "_look_ready")
        self.look_free = sem(n + "_look_free")
        self.row_ready = sem(n + "_row_ready")
        self.softplus = sem(n + "_softplus")


def rank_onehots(nc, dve, E, R, keys, tile0, par, g1):
    hi, lo, key = keys
    dve.wait_ge(R.keyrow_ready, g1)
    sl = bass.ds(tile0, G)
    for k, part in enumerate((hi, lo)):
        nc.vector.tensor_tensor(R.oh[:, par, k], bc(E.iota[:, None, 0:B], [P, G, B]),
                                bc(part[:, sl][:, :, None], [P, G, B]), ALU.is_equal)
    nc.vector.tensor_copy(R.kg[:, par, :], key[:, sl]).then_inc(R.oh_ready, 1)


def rank_tensor_first(nc, pe, E, R, it, par):
    g1 = upto(it, par)
    pe.wait_ge(R.oh_ready, g1)
    pe.wait_ge(R.T_ready, g1)
    for j in range(G):
        last = nc.tensor.matmul(R.psH[:, j, :], R.oh[:, par, 0, j, :], R.oh[:, par, 1, j, :], start=True, stop=True)
    last.then_inc(R.hist_ready, 1)
    pe.wait_ge(R.ohT_ready, g1)
    for j in range(G):
        last = nc.tensor.matmul(R.psHT[:, j, :], R.oh[:, par, 0, j, :], E.ident[:, :], start=True, stop=True)
    last.then_inc(R.hT_ready, 1)
    pe.wait_ge(R.keyrow_free, g1)
    for j in range(G):
        last = nc.tensor.matmul(R.psK[:, j, :], bc(R.kg[:, par, j:j + 1], [P, P]), E.ident[:, :], start=True, stop=True)
    last.then_inc(R.keyrow_ready, 1)


def rank_tensor_look(nc, pe, R, it, par):
    g1 = upto(it, par)
    pe.wait_ge(R.ohT_ready, g1 + 1)
    pe.wait_ge(R.T_ready, g1 + 1)
    pe.wait_ge(R.look_free, g1)
    for j in range(G):
        last = nc.tensor.matmul(R.psL[:, j, :], R.ohT[:, par, j, :], R.T[:, par, j, :], start=True, stop=True)
    last.then_inc(R.look_ready, 1)


def rank_tensor(nc, pe, E, R, it, par):
    rank_tensor_first(nc, pe, E, R, it, par)
    rank_tensor_look(nc, pe, R, it, par)


def rank_scalar(nc, act, R, it, par):
    g1 = upto(it, par)
    act.wait_ge(R.hT_ready, g1)
    act.wait_ge(R.look_ready, g1)
    nc.scalar.activation(R.ohT[:, par], R.psHT[:, :, :], ACT.Copy).then_inc(R.ohT_ready, 1)


RANK_LINKS = G - 1 + 6


def rank_rows(nc, dve, E, R, link, it, par, NT, scattered, padoff=None):
    g1 = upto(it, par)
    dve.wait_ge(R.hist_ready, g1)
    for j in range(G):
        out = R.T[:, par, j + 1] if j < G - 1 else R.T[:, 1 - par, 0]
        add = nc.vector.tensor_tensor(out, R.T[:, par, j], R.psH[:, j], ALU.add)
        if j < G - 1:
            link(add)
        else:
            add.then_inc(R.T_ready, 1)
    dve.wait_ge(R.keyrow_ready, g1 + 2)
    for j in range(G):
        last = nc.vector.scalar_tensor_tensor(R.junk[:, j], R.psK[:, j], R.kg[:, par, j:j + 1], E.before[:, :],
                                              ALU.is_equal, ALU.mult, accum_out=R.r2[:, j:j + 1])
    last.then_inc(R.keyrow_free, 1)
    dve.wait_ge(R.keyrow_free, g1 + 1)
    dve.wait_ge(R.look_ready, g1 + 2)
    nc.vector.tensor_tensor(R.tmp[:, :, :], R.psL[:, :, :], R.oh[:, par, 1], ALU.mult).then_inc(R.look_free, 1)
    dve.wait_ge(R.look_free, g1 + 1)
    link(nc.vector.tensor_reduce(R.r1[:, :], R.tmp[:, :, :], AXX, ALU.add))
    link(nc.vector.tensor_tensor(R.posf[:, :], R.r1[:, :], R.r2[:, :], ALU.add))
    if padoff is not None:
        link(nc.vector.tensor_tensor(R.posf[:, :], R.posf[:, :], padoff[:, tiles(it, par)], ALU.add))
    link(nc.vector.tensor_copy(R.posi[:, 0], R.posf[:, :]))
    link(nc.vector.tensor_scalar(R.posi[:, 1], R.posi[:, 0], 127, None, ALU.bitwise_and))
    link(nc.vector.tensor_scalar(R.posi[:, 2], R.posi[:, 0], 7, None, ALU.arith_shift_right))
    dve.wait_ge(scattered[par], 64 * it + 64)
    nc.vector.scalar_tensor_tensor(R.row[:, par], R.posi[:, 1], float(NT), R.posi[:, 2],
                                   ALU.mult, ALU.add).then_inc(R.row_ready, 1)


def split_keys(nc, link, keyf, keyi, hi, lo, ti):
    link(nc.vector.tensor_copy(keyf, keyi))
    link(nc.vector.tensor_scalar(ti, keyi, 6, None, ALU.arith_shift_right))
    link(nc.vector.tensor_copy(hi, ti))
    link(nc.vector.tensor_scalar(ti, keyi, B - 1, None, ALU.bitwise_and))
    link(nc.vector.tensor_copy(lo, ti))


def histogram_vector(nc, dve, E, H, hi, lo):
    def group(it, par):
        dve.wait_ge(H.counted, upto(it, par))
        for k, part in enumerate((hi, lo)):
            last = nc.vector.tensor_tensor(H.oh[:, par, k], bc(E.iota[:, None, 0:B], [P, G, B]),
                                           bc(part[:, tiles(it, par)][:, :, None], [P, G, B]), ALU.is_equal)
        last.then_inc(H.oh_ready, 1)
    with dve.Fori(0, H.n // (2 * G)) as it:
        for par in (0, 1):
            group(it, par)


def histogram_tensor(nc, pe, E, H):
    nc.tensor.matmul(H.ps[:, :], H.zero[:, 0:B], H.zero[:, 0:B], start=True, stop=False)
    with pe.Fori(0, H.n // (2 * G)) as it:
        for par in (0, 1):
            pe.wait_ge(H.oh_ready, upto(it, par))
            for j in range(G):
                last = nc.tensor.matmul(H.ps[:, :], H.oh[:, par, 0, j], H.oh[:, par, 1, j], start=False, stop=False)
            last.then_inc(H.counted, 1)
    nc.tensor.matmul(H.ps[:, :], H.zero[:, 0:B], H.zero[:, 0:B], start=False, stop=True).then_inc(H.done, 1)


class Hist:
    def __init__(self, nc, sb, ps, sem, n, tiles_n):
        self.n = tiles_n
        self.oh = sb(n + "_hoh", [P, 2, 2, G, B], F32)
        self.zero = sb(n + "_hzero", [P, B], F32)
        self.c = sb(n + "_hc", [B, 4, B], F32)
        self.i = sb(n + "_hi", [B, 2], I32)
        self.nt = sb(n + "_hnt", [B, 4], F32)
        self.M = sb(n + "_hM", [B, 512], F32)
        self.ps = ps(n + "_hps", [B, B], F32)
        self.psb = ps(n + "_hpsb", [B, 512], F32)
        self.oh_ready = sem(n + "_hoh_ready")
        self.counted = sem(n + "_hcounted")
        self.done = sem(n + "_hdone")
        self.s_nt = sem(n + "_hs_nt")
        self.s_first = sem(n + "_hs_first")
        self.s_M = sem(n + "_hs_M")
        self.s_blk = sem(n + "_hs_blk")


def base_vector(nc, dve, E, H, link, T0, blk):
    dve.wait_ge(H.done, 1)
    link(nc.vector.tensor_copy(H.c[:, 0], H.ps[:, :]))
    link(nc.vector.tensor_tensor_scan(H.c[:, 1], E.ones[0:B, 0:B], H.c[:, 0], 0.0, ALU.mult, ALU.add))
    link(nc.vector.tensor_scalar(H.nt[:, 0:1], H.c[:, 1, B - 1:B], float(P - 1), None, ALU.add))
    link(nc.vector.tensor_copy(H.i[:, 0:1], H.nt[:, 0:1]))
    link(nc.vector.tensor_scalar(H.i[:, 1:2], H.i[:, 0:1], 7, None, ALU.arith_shift_right))
    nc.vector.tensor_copy(H.nt[:, 1:2], H.i[:, 1:2]).then_inc(H.s_nt, 1)
    dve.wait_ge(H.s_first, 1)
    link(nc.vector.tensor_tensor(H.nt[:, 2:3], H.psb[:, 0:1], H.nt[:, 1:2], ALU.add))
    link(nc.vector.tensor_scalar(H.nt[:, 3:4], H.psb[:, 0:1], float(P), None, ALU.mult))
    link(nc.vector.tensor_tensor(H.c[:, 2], H.c[:, 1], H.c[:, 0], ALU.subtract))
    link(nc.vector.tensor_scalar(T0, H.c[:, 2], H.nt[:, 3:4], None, ALU.add))
    nc.vector.tensor_scalar(H.M[:, 0:E.NT], E.iota[0:B, :], H.nt[:, 2:3], None, ALU.is_ge).then_inc(H.s_M, 1)
    dve.wait_ge(H.s_blk, 1)
    link(nc.vector.tensor_scalar(blk, H.psb[0:1, 0:E.NT], float(E.NB - 1), None, ALU.min))


def base_tensor(nc, pe, E, H):
    pe.wait_ge(H.s_nt, 1)
    nc.tensor.matmul(H.psb[:, 0:1], E.after[0:B, 0:B], H.nt[:, 1:2], start=True, stop=True).then_inc(H.s_first, 1)
    pe.wait_ge(H.s_M, 1)
    nc.tensor.matmul(H.psb[0:1, 0:E.NT], E.ones[0:B, 0:1], H.M[:, 0:E.NT], start=True, stop=True).then_inc(H.s_blk, 1)


NC = 7


def load_nodes(sp, dst, x, N, sem):
    full = N // B
    sp.dma_start(dst[:, 0:full], x[0:full * B].rearrange("(b p) c -> p b c", p=B)).then_inc(sem, 16)
    sp.dma_start(dst[0:N - full * B, full:full + 1],
                 x[full * B:N].rearrange("(b p) c -> p b c", b=1)).then_inc(sem, 16)


def layernorm(nc, dve, act, link, x, s, sq, s_var, s_sd, n):
    D = x.shape[-1]
    mean, r = s[:, 0], s[:, 1]
    sh = list(x.shape)
    link(nc.vector.tensor_reduce(mean, x, AXX, ALU.add))
    link(nc.vector.tensor_scalar(mean, mean, 1.0 / D, None, ALU.mult))
    link(nc.vector.tensor_tensor(x, x, bc(mean[:, :, None], sh), ALU.subtract))
    link(nc.vector.tensor_tensor(sq, x, x, ALU.mult))
    link(nc.vector.tensor_reduce(r, sq, AXX, ALU.add))
    nc.vector.tensor_scalar(r, r, 1.0 / D, 1e-5, ALU.mult, ALU.add).then_inc(s_var, 1)
    dve.wait_ge(s_sd, n)
    link(nc.vector.reciprocal(r, r))
    link(nc.vector.tensor_tensor(x, x, bc(r[:, :, None], sh), ALU.mult))


def phase_nodes0(nc, E, a, sem):
    N, NB = E.N, E.NB
    CW = NC * B
    with ExitStack() as st:
        def tmp(name, shape, dt):
            return st.enter_context(nc.sbuf_tensor(name, shape, dt))

        def pst(name, shape, dt):
            return banks(nc, st, name, shape)

        x = tmp("n0_x", [B, NB, B], F32)
        sq = tmp("n0_sq", [B, NB, B], F32)
        s = tmp("n0_s", [B, 2, NB], F32)
        hs = tmp("n0_hs", [B, NC, B], F32)
        hTs = tmp("n0_hTs", [B, CW], F32)
        bd = tmp("n0_bd", [B, 4, B], F32)
        M = tmp("n0_M", [B, 68], F32)
        WKV = tmp("n0_WKV", [B, 2 * B], F32)
        WQ = tmp("n0_WQ", [B, 68], F32)
        psW = pst("n0_psW", [B, 4, B], F32)
        psT = pst("n0_psT", [B, CW], F32)
        psKV = pst("n0_psKV", [B, 8, 2 * B], F32)
        psQ = pst("n0_psQ", [B, NC, 68], F32)
        psB = pst("n0_psB", [1, P], F32)
        s_in, s_x, s_zero, s_link, s_var, s_sd, s_w, s_wc, s_M, s_q = (
            sem("n0_" + n) for n in ("in", "x", "zero", "link", "var", "sd", "w", "wc", "M", "q"))
        s_h, s_hs, s_T, s_Tc, s_tab, s_out, s_b, s_outa, s_id = (
            sem("n0_" + n) for n in ("h", "hs", "T", "Tc", "tab", "out", "b", "outa", "id"))
        s_taken = sem("n0_taken")
        H, D = 4, 16
        weights = 4 * H + H + 16 + 8 + 2 + 4 + H
        with nc.Block() as block:
            @block.sync
            def _(sp):
                sp.wait_ge(s_zero, 1)
                load_nodes(sp, x, a["x"], N, s_x)
                for h in range(H):
                    hd = slice(h * D, h * D + D)
                    for k, w in enumerate(("L0_gnn_Wk", "L0_gnn_Wv", "L0_gnn_Wq")):
                        sp.dma_start(bd[hd, k, hd], a[w][h]).then_inc(s_in, 16)
                    sp.dma_start(bd[hd, 3, hd], a["L0_gnn_wkl_w"]).then_inc(s_in, 16)
                    sp.dma_start(M[hd, B + h:B + h + 1], a["L0_gnn_wkl_b"].rearrange("(p c) -> p c", c=1)).then_inc(s_in, 16)
                    sp.dma_start(E.wvl[hd, hd], a["L0_gnn_wvl_w"]).then_inc(s_in, 16)
                for t in range(G):
                    for k, n in enumerate(("wk", "wv")):
                        o = 32 * t + 16 * k
                        sp.dma_start(E.W1[16 * t:16 * t + 16, o:o + 16], a[f"L0_gnn_{n}1_w"]).then_inc(s_in, 16)
                        sp.dma_start(E.W2[o:o + 16, o:o + 16], a[f"L0_gnn_{n}2_w"]).then_inc(s_in, 16)
                        sp.dma_start(E.b1[o:o + 16, :], a[f"L0_gnn_{n}1_b"].rearrange("(p c) -> p c", c=1)).then_inc(s_in, 16)
                        sp.dma_start(E.b2[0:1, o:o + 16], a[f"L0_gnn_{n}2_b"].rearrange("(p c) -> p c", p=1)).then_inc(s_in, 16)
                sp.wait_ge(s_in, 16 * (6 * H + 8 * G))
                sp.wait_ge(s_x, 32)

            @block.vector
            def _(dve):
                link = Link(dve, s_link)
                for t in (E.W1, E.W2, E.wvl, M):
                    nc.vector.memset(t[:, :], 0.0)
                nc.vector.memset(x[:, NB - 1], 0.0)
                nc.vector.memset(bd[:, :, :], 0.0).then_inc(s_zero, 1)
                dve.wait_ge(s_x, 32)
                layernorm(nc, dve, None, link, x[:, :, :], s, sq[:, :, :], s_var, s_sd, 1)
                nc.vector.tensor_scalar(x[:, :, :], x[:, :, :], 0.0, None, ALU.max).then_inc(s_h, 1)
                dve.wait_ge(s_w, 1)
                nc.vector.tensor_copy(WKV[:, 0:2 * B], psW[:, 0:2].rearrange("p k c -> p (k c)"))
                nc.vector.tensor_copy(M[:, 0:B], psW[:, 2]).then_inc(s_wc, 1)
                dve.wait_ge(s_q, 1)
                nc.vector.tensor_scalar(WQ[:, :], psQ[:, 0, :], 0.25, None, ALU.mult).then_inc(s_M, 1)
                dve.wait_ge(s_b, 1)
                nc.vector.scalar_tensor_tensor(E.b2[:, :], psB[:, :], -float(np.log(2.0)), E.b2[:, :],
                                               ALU.mult, ALU.add).then_inc(s_M, 1)
                dve.sem_inc(s_out, 1)
                with dve.Fori(0, NB // NC) as c:
                    dve.wait_ge(s_T, c + 1)
                    nc.vector.tensor_copy(hTs[:, :], psT[:, :]).then_inc(s_Tc, 1)
                    dve.wait_ge(s_tab, c + 1)
                    nc.vector.tensor_copy(E.kvtab[:, bass.ds(c * NC, NC), :], psKV[:, 0:NC, :]).then_inc(s_out, 1)

            @block.scalar
            def _(act):
                act.wait_ge(s_var, 1)
                nc.scalar.activation(s[:, 1], s[:, 1], ACT.Sqrt).then_inc(s_sd, 1)
                act.wait_ge(s_h, 1)
                act.sem_inc(s_outa, 1)
                with act.Fori(0, NB // NC) as c:
                    nc.scalar.activation(hs[:, :, :], x[:, bass.ds(c * NC, NC), :], ACT.Copy).then_inc(s_hs, 1)
                    act.wait_ge(s_Tc, c + 1)
                    nc.scalar.activation(E.h0T[:, bass.ds(c * CW, CW)], hTs[:, :], ACT.Copy)
                    act.wait_ge(s_tab, c + 1)
                    nc.scalar.activation(E.qtab[:, bass.ds(c * NC, NC), :], psQ[:, :, :], ACT.Copy).then_inc(s_outa, 1)

            @block.tensor
            def _(pe):
                pe.wait_ge(s_in, 16 * (6 * H + 8 * G))
                I = E.ident[0:B, 0:B]
                for k, w in enumerate((0, 1, 3)):
                    last = nc.tensor.matmul(psW[:, k], bd[:, w], I, start=True, stop=True)
                last.then_inc(s_w, 1)
                pe.wait_ge(s_wc, 1)
                nc.tensor.matmul(psQ[:, 0, :], bd[:, 2], M[:, :], start=True, stop=True).then_inc(s_q, 1)
                nc.tensor.matmul(psB[:, :], E.ones[:, 0:1], E.W2[:, :], start=True, stop=True).then_inc(s_b, 1)
                pe.wait_ge(s_M, 2)
                with pe.Fori(0, NB // NC) as c:
                    pe.wait_ge(s_hs, c + 1)
                    pe.sem_inc(s_taken, 1)
                    for j in range(NC):
                        last = nc.tensor.matmul(psT[:, j * B:j * B + B], hs[:, j], I, start=True, stop=True)
                    last.then_inc(s_T, 1)
                    pe.wait_ge(s_Tc, c + 1)
                    pe.wait_ge(s_out, c + 1)
                    pe.wait_ge(s_outa, c + 1)
                    pe.sem_inc(s_taken, 1)
                    for j in range(NC):
                        lhs = hTs[:, j * B:j * B + B]
                        nc.tensor.matmul(psKV[:, j, :], lhs, WKV[:, :], start=True, stop=True)
                        last = nc.tensor.matmul(psQ[:, j, :], lhs, WQ[:, :], start=True, stop=True)
                    last.then_inc(s_tab, 1)


def phase_sort_src(nc, E, sem):
    NT, EF = E.NT, E.EF
    with ExitStack() as st:
        def tmp(name, shape, dt):
            return st.enter_context(nc.sbuf_tensor(name, shape, dt))

        def pst(name, shape, dt):
            return banks(nc, st, name, shape)

        sd = tmp("sd", [P, NT, E.RD], F32)
        keyS = tmp("keyS", [P, NT + G], F32)
        hiS = tmp("hiS", [P, NT + G], F32)
        loS = tmp("loS", [P, NT + G], F32)
        pad = tmp("pad", [P, NT], F32)
        n = NT // (2 * G)
        with ExitStack() as st2:
            H = Hist(nc, lambda a, b, c: st2.enter_context(nc.sbuf_tensor(a, b, c)),
                     lambda a, b, c: banks(nc, st2, a, b), sem, "S", NT)
            ki = st2.enter_context(nc.sbuf_tensor("ki", [P, NT], I32))
            ti = st2.enter_context(nc.sbuf_tensor("tiS", [P, NT], I32))
            s_sd, s_link, s_hz = sem("s_sd"), sem("s_linkHS"), sem("s_hzS")
            with nc.Block() as block:
                @block.sync
                def _(sp):
                    sp.dma_start(sd[:, :, :], E.sd.rearrange("p (t f) -> p t f", f=E.RD)).then_inc(s_sd, 16)
                    sp.wait_ge(s_sd, 16)

                @block.vector
                def _(dve):
                    link = Link(dve, s_link)
                    nc.vector.memset(H.zero[:, :], 0.0).then_inc(s_hz, 1)
                    link(nc.vector.memset(keyS[:, NT:], -1.0))
                    link(nc.vector.memset(hiS[:, NT:], -1.0))
                    link(nc.vector.memset(loS[:, NT:], -1.0))
                    link(nc.vector.memset(E.loD[:, NT:], -1.0))
                    link(nc.vector.memset(E.srcI[:, NT:], 0))
                    dve.wait_ge(s_sd, 16)
                    link(nc.vector.tensor_copy(ki[:, :], sd[:, :, 1]))
                    split_keys(nc, link, E.keyD[:, :], ki[:, :], hiS[:, 0:NT], E.loD[:, 0:NT], ti[:, :])
                    link(nc.vector.tensor_scalar(pad[:, :], E.keyD[:, :], 0.0, 8388608.0, ALU.is_lt, ALU.mult))
                    link(nc.vector.tensor_tensor(E.loD[:, 0:NT], E.loD[:, 0:NT], pad[:, :], ALU.max))
                    link(nc.vector.tensor_copy(ki[:, :], sd[:, :, 0]))
                    split_keys(nc, link, keyS[:, 0:NT], ki[:, :], hiS[:, 0:NT], loS[:, 0:NT], ti[:, :])
                    link(nc.vector.tensor_scalar(E.srcI[:, 0:NT], keyS[:, 0:NT], 0.0, None, ALU.max))
                    histogram_vector(nc, dve, E, H, hiS, loS)
                    base_vector(nc, dve, E, H, link, E.T0S[:, :], E.blkS[:, :])

                @block.tensor
                def _(pe):
                    pe.wait_ge(s_hz, 1)
                    pe.sem_inc(H.counted, 2)
                    histogram_tensor(nc, pe, E, H)
                    base_tensor(nc, pe, E, H)

        R = Rank(nc, tmp, pst, sem, "RS")
        ohD = tmp("ohD", [P, 2, G, B], F32)
        ohDT = tmp("ohDT", [B, 2, G, P], F32)
        at = tmp("at", [P, 2, G * EF], F32)
        atT = tmp("atT", [G * EF, P], F32)
        net = tmp("net", [P, 3, P], F32)
        ssp = tmp("ssp", [P, P], F32)
        w = tmp("w", [P, G, 2, EF], F32)
        pay = tmp("payS", [P, 2, G, E.RS], F32)
        psDT = pst("psDT", [B, G, P], F32)
        psKV = pst("psKV", [P, G, 2 * B], F32)
        psN = pst("psN", [P, 4, P], F32)
        s_at, s_atp, s_atT, s_n1, s_act, s_ssp, s_n2, s_w, s_DT, s_ohDT, s_kv, s_pay, s_link, s_taken = (
            sem("es_" + k) for k in ("at", "atp", "atT", "n1", "act", "ssp", "n2", "w", "DT", "ohDT", "kv", "pay",
                                     "link", "taken"))
        s_taken2 = sem("es_taken2")
        keys = (hiS, loS, keyS)
        with nc.Block() as block:
            @block.tensor
            def _(pe):
                pe.sem_inc(R.keyrow_ready, 2)
                pe.sem_inc(R.look_ready, 2)
                with pe.Fori(0, n) as it:
                    blocks = blocks_of(nc, PE, E.blkD, it, E.NB)
                    for par in (0, 1):
                        g1 = upto(it, par)
                        pe.wait_ge(s_at, g1)
                        nc.tensor.matmul(psN[0:G * EF, 0], at[:, par], E.ident[:, :], start=True, stop=True).then_inc(s_atp, 1)
                        pe.wait_ge(R.oh_ready, g1)
                        pe.wait_ge(s_ohDT, g1)
                        for j in range(G):
                            last = nc.tensor.matmul(psDT[:, j], ohD[:, par, j], E.ident[:, :], start=True, stop=True)
                        last.then_inc(s_DT, 1)
                        rank_tensor_first(nc, pe, E, R, it, par)
                        pe.wait_ge(s_atT, g1)
                        nc.tensor.matmul(psN[:, 1], E.W1[:, :], atT[:, :], start=True, stop=True).then_inc(s_n1, 1)
                        rank_tensor_look(nc, pe, R, it, par)
                        pe.wait_ge(s_ssp, g1)
                        pe.wait_ge(s_w, g1)
                        nc.tensor.matmul(psN[:, 2], ssp[:, :], E.W2[:, :], start=True, stop=False)
                        nc.tensor.matmul(psN[:, 2], E.ones[0:1, :], E.b2[:, :], start=False, stop=True).then_inc(s_n2, 1)
                        pe.wait_ge(s_ohDT, g1 + 1)
                        pe.wait_ge(s_pay, g1)
                        pe.sem_inc(s_taken, 1)
                        for j in range(G):
                            b = blocks[par * G + j]
                            last = nc.tensor.matmul(psKV[:, j], ohDT[:, par, j], E.kvtab[:, bass.ds(b, 1), :],
                                                    start=True, stop=True)
                        last.then_inc(s_kv, 1)

            @block.scalar
            def _(act):
                act.sem_inc(R.ohT_ready, 1)
                act.sem_inc(s_ohDT, 1)
                act.sem_inc(s_w, 1)
                with act.Fori(0, n) as it:
                    for par in (0, 1):
                        g1 = upto(it, par)
                        nc.scalar.activation(at[:, par].rearrange("p (t f) -> p t f", f=EF), sd[:, tiles(it, par), 2:E.RD],
                                             ACT.Copy).then_inc(s_at, 1)
                        act.wait_ge(s_atp, g1)
                        nc.scalar.activation(atT[:, :], psN[0:G * EF, 0], ACT.Copy).then_inc(s_atT, 1)
                        rank_scalar(nc, act, R, it, par)
                        act.wait_ge(s_DT, g1)
                        nc.scalar.activation(ohDT[:, par], psDT[:, :, :], ACT.Copy).then_inc(s_ohDT, 1)
                        act.wait_ge(s_n1, g1)
                        nc.scalar.activation(net[:, 0], psN[:, 1], ACT.Abs, bias=E.b1[:, 0:1]).then_inc(s_act, 1)
                        act.wait_ge(s_act, it * 4 + 2 * par + 1)
                        nc.scalar.activation(net[:, 1], net[:, 0], ACT.Exp, scale=-1.0).then_inc(s_act, 1)
                        act.wait_ge(s_act, it * 4 + 2 * par + 2)
                        nc.scalar.activation(net[:, 1], net[:, 1], ACT.Ln, bias=1.0)
                        nc.scalar.activation(net[:, 2], psN[:, 1], ACT.Relu, bias=E.b1[:, 0:1]).then_inc(R.softplus, 1)
                        act.wait_ge(s_n2, g1)
                        act.wait_ge(s_pay, g1)
                        nc.scalar.activation(w[:, :, :, :], psN[:, 2].rearrange("p (t k j) -> p t k j", t=G, k=2),
                                             ACT.Copy).then_inc(s_w, 1)

            @block.vector
            def _(dve):
                link = Link(dve, s_link)
                dve.sem_inc(R.T_ready, 1)
                dve.sem_inc(R.keyrow_free, 1)
                dve.sem_inc(R.look_free, 1)
                dve.sem_inc(s_pay, 1)
                link(nc.vector.tensor_copy(R.T[:, 0, 0], E.T0S[:, :]))

                def onehots(tile0, par, g1):
                    dve.wait_ge(R.keyrow_ready, g1)
                    nc.vector.tensor_tensor(ohD[:, par], bc(E.iota[:, None, 0:B], [P, G, B]),
                                            bc(E.loD[:, bass.ds(tile0, G)][:, :, None], [P, G, B]), ALU.is_equal)
                    rank_onehots(nc, dve, E, R, keys, tile0, par, g1)

                onehots(0, 0, 1)
                with dve.Fori(0, n) as it:
                    link.loop(1, it, 2 * (RANK_LINKS + 1))
                    for par in (0, 1):
                        g1 = upto(it, par)
                        onehots(it * (2 * G) + (par + 1) * G, 1 - par, upto(it, par + 1))
                        dve.wait_ge(R.softplus, g1)
                        nc.vector.tensor_tensor(ssp[:, :], net[:, 1], net[:, 2], ALU.add).then_inc(s_ssp, 1)
                        rank_rows(nc, dve, E, R, link, it, par, NT, E.scatS, pad)
                        link(nc.vector.tensor_copy(pay[:, par, :, 2 * B:], R.kg[:, par, :, None]))
                        dve.wait_ge(s_w, g1 + 1)
                        dve.wait_ge(s_kv, g1)
                        for k in (0, 1):
                            last = nc.vector.tensor_tensor(
                                pay[:, par, :, k * B:(k + 1) * B].rearrange("p t (h j) -> p t h j", h=4),
                                psKV[:, :, k * B:(k + 1) * B].rearrange("p t (h j) -> p t h j", h=4),
                                bc(w[:, :, k, :][:, :, None, :], [P, G, 4, EF]), ALU.mult)
                        last.then_inc(s_pay, 1)
                    assert link.n == 2 * (RANK_LINKS + 1), link.n

            @block.gpsimd
            def _(pool):
                limit = pool.to_reg(P * NT - 1)
                with pool.Fori(0, n) as it:
                    for par in (0, 1):
                        pool.wait_ge(R.row_ready, upto(it, par))
                        pool.wait_ge(s_pay, upto(it, par) + 1)
                        pool.sem_inc(s_taken2, 1)
                        for j in range(G):
                            nc.gpsimd.indirect_dma_start(
                                out=E.ss_rows, out_offset=bass.IndirectOffsetOnAxis(ap=R.row[:, par, j:j + 1], axis=0),
                                in_=pay[:, par, j, :], in_offset=None,
                                bounds_check=limit, oob_is_err=False).then_inc(E.scatS[par], 16)
                for par in (0, 1):
                    pool.wait_ge(E.scatS[par], 64 * n + 64)


FAR = 1.0e30


def phase_logits0(nc, E, sem):
    NT, RS, H = E.NT, E.RS, 4
    with ExitStack() as st:
        def tmp(name, shape, dt):
            return st.enter_context(nc.sbuf_tensor(name, shape, dt))

        def pst(name, shape):
            return banks(nc, st, name, shape)

        rows = tmp("l0_rows", [P, 2, G, RS], F32)
        oh = tmp("l0_oh", [P, 2, G, B], F32)
        ohT = tmp("l0_ohT", [B, 2, G, P], F32)
        ki = tmp("l0_ki", [P, G], I32)
        kj = tmp("l0_kj", [P, G], I32)
        neg = tmp("l0_neg", [P, G], F32)
        prod = tmp("l0_prod", [P, G, B], F32)
        dot = tmp("l0_dot", [P, G, H], F32)
        psT = pst("l0_psT", [B, G, P])
        psQ = pst("l0_psQ", [P, G, B + H])
        s_in = [sem("l0_in0"), sem("l0_in1")]
        s_used, s_oh, s_T, s_ohT, s_q, s_link, s_taken = (
            sem("l0_" + k) for k in ("used", "oh", "T", "ohT", "q", "link", "taken"))
        n = NT // (2 * G)
        ss = E.ss.rearrange("p (t f) -> p t f", f=RS)
        with nc.Block() as block:
            @block.sync
            def _(sp):
                with sp.Fori(0, n) as it:
                    for par in (0, 1):
                        sp.wait_ge(s_used, upto(it, par))
                        sp.dma_start(rows[:, par], ss[:, tiles(it, par), :]).then_inc(s_in[par], 16)
                sp.wait_ge(s_used, 2 * n + 1)
                sp.dma_start(rows[:, 0], ss[:, 0:G, :]).then_inc(s_in[0], 16)
                sp.wait_ge(s_in[0], 16 * n + 16)

            @block.tensor
            def _(pe):
                with pe.Fori(0, n) as it:
                    blocks = blocks_of(nc, PE, E.blkS, it, E.NB)
                    for par in (0, 1):
                        g1 = upto(it, par)
                        pe.wait_ge(s_oh, g1)
                        pe.wait_ge(s_ohT, g1)
                        for j in range(G):
                            last = nc.tensor.matmul(psT[:, j], oh[:, par, j], E.ident[:, :], start=True, stop=True)
                        last.then_inc(s_T, 1)
                        pe.wait_ge(s_ohT, g1 + 1)
                        pe.wait_ge(s_used, g1 + 1)
                        pe.sem_inc(s_taken, 1)
                        for j in range(G):
                            b = blocks[par * G + j]
                            last = nc.tensor.matmul(psQ[:, j], ohT[:, par, j], E.qtab[:, bass.ds(b, 1), :],
                                                    start=True, stop=True)
                        last.then_inc(s_q, 1)

            @block.scalar
            def _(act):
                act.sem_inc(s_ohT, 1)
                with act.Fori(0, n) as it:
                    for par in (0, 1):
                        act.wait_ge(s_T, upto(it, par))
                        nc.scalar.activation(ohT[:, par], psT[:, :, :], ACT.Copy).then_inc(s_ohT, 1)

            @block.vector
            def _(dve):
                link = Link(dve, s_link)

                def onehots(tile0, par):
                    key = rows[:, par, :, 2 * B]
                    sl = bass.ds(tile0, G)
                    nc.vector.tensor_copy(E.keyS[:, sl], key)
                    nc.vector.tensor_scalar(neg[:, :], key, 0.0, 1000.0, ALU.is_lt, ALU.mult)
                    link(nc.vector.tensor_copy(ki[:, :], key))
                    link(nc.vector.tensor_scalar(kj[:, :], ki[:, :], B - 1, None, ALU.bitwise_and))
                    link(nc.vector.tensor_tensor(E.loS[:, sl], neg[:, :], kj[:, :], ALU.max))
                    nc.vector.tensor_tensor(oh[:, par], bc(E.iota[:, None, 0:B], [P, G, B]),
                                            bc(E.loS[:, sl][:, :, None], [P, G, B]), ALU.is_equal).then_inc(s_oh, 1)

                dve.sem_inc(s_used, 2)
                dve.wait_ge(s_in[0], 16)
                onehots(0, 0)
                with dve.Fori(0, n) as it:
                    link.loop(3, it, 2 * 6)
                    for par in (0, 1):
                        g1 = upto(it, par)
                        dve.wait_ge(s_in[1 - par], 16 * it + 16 * (par + 1))
                        onehots(it * (2 * G) + (par + 1) * G, 1 - par)
                        dve.wait_ge(s_q, g1)
                        link(nc.vector.tensor_tensor(prod[:, :, :], rows[:, par, :, 0:B], psQ[:, :, 0:B], ALU.mult))
                        link(nc.vector.tensor_reduce(dot[:, :, :], prod[:, :, :].rearrange("p t (h j) -> p t h j", h=H),
                                                     AXX, ALU.add))
                        link(nc.vector.tensor_tensor(E.lg0[:, tiles(it, par), :], dot[:, :, :], psQ[:, :, B:], ALU.add))
                        dve.sem_inc(s_used, 1)
                    assert link.n == 12, link.n


def phase_softmax(nc, E, sem, n, lg, key, H):
    NT = E.NT
    Q = NT // 4
    with ExitStack() as st:
        def tmp(name, shape, dt=F32):
            return st.enter_context(nc.sbuf_tensor(n + name, shape, dt))

        def pst(name, shape):
            return banks(nc, st, n + name, shape)

        X = tmp("X", [Q, 4, H, P])
        up = tmp("up", [Q, 4, H, P])
        down = tmp("down", [Q, 4, H, P])
        K = tmp("K", [Q, 4, P])
        Rup = tmp("Rup", [Q, 4, P])
        Rdown = tmp("Rdown", [Q, 4, P])
        e1 = tmp("e1", [Q, 4, H])
        e2 = tmp("e2", [Q, 4, H])
        ends = tmp("ends", [H, 4, NT])
        same = tmp("same", [H, 4, NT])
        run = tmp("run", [H, 2, NT])
        carry = tmp("carry", [H, 2, NT])
        cq = tmp("cq", [Q, 2, 4, H])
        psX = [pst("psX0", [Q, P * 4]), pst("psX1", [Q, P * 4])]
        psE = [pst(f"psE{k}", [H, NT]) for k in range(4)]
        psC = pst("psC", [Q, 2 * 4 * H])
        psMt = [pst("psMt", [P, 4 * Q])]
        s_X, s_Xc, s_link, s_ends, s_E, s_carry, s_C, s_M, s_Mt, s_sub, s_exp = (
            sem(n + k) for k in ("X", "Xc", "link", "ends", "E", "carry", "C", "M", "Mt", "sub", "exp"))
        HX = -(-H // 4)
        steps = [(c, k) for c in range(4) for k in range(HX + 1)]
        with nc.Block() as block:
            @block.tensor
            def _(pe):
                for i, (c, k) in enumerate(steps):
                    if i >= 2:
                        pe.wait_ge(s_Xc, i - 1)
                    if k < HX:
                        for h in range(4):
                            last = nc.tensor.matmul(psX[i % 2][:, h * P:(h + 1) * P], lg[:, c * Q:(c + 1) * Q, 4 * k + h],
                                                    E.ident[:, :], start=True, stop=True)
                    else:
                        last = nc.tensor.matmul(psX[i % 2][:, 0:P], key[:, c * Q:(c + 1) * Q], E.ident[:, :],
                                                start=True, stop=True)
                    last.then_inc(s_X, 1)
                pe.wait_ge(s_ends, 1)
                I = E.ident[0:Q, 0:Q]
                for c in range(4):
                    for k, src in enumerate((up[:, c, :, P - 1], down[:, c, :, 0], bc(K[:, c, 0:1], [Q, H]),
                                             bc(K[:, c, P - 1:P], [Q, H]))):
                        last = nc.tensor.matmul(psE[k][:, c * Q:(c + 1) * Q], src, I, start=True, stop=True)
                last.then_inc(s_E, 1)
                pe.wait_ge(s_carry, 1)
                for k in (0, 1):
                    for c in range(4):
                        last = nc.tensor.matmul(psC[:, (k * 4 + c) * H:(k * 4 + c + 1) * H], carry[:, k, c * Q:(c + 1) * Q],
                                                E.ident[0:H, 0:H], start=True, stop=True)
                last.then_inc(s_C, 1)
                pe.wait_ge(s_M, 1)
                for i, (c, k) in enumerate((c, k) for c in range(4) for k in range(HX)):
                    if i >= 1:
                        pe.wait_ge(s_sub, i)
                    for h in range(4):
                        last = nc.tensor.matmul(psMt[0][:, h * Q:(h + 1) * Q], up[:, c, 4 * k + h], I,
                                                start=True, stop=True)
                    last.then_inc(s_Mt, 1)

            @block.vector
            def _(dve):
                link = Link(dve, s_link)
                for i, (c, k) in enumerate(steps):
                    dve.wait_ge(s_X, i + 1)
                    if k < HX:
                        nc.vector.tensor_copy(X[:, c, 4 * k:4 * k + 4], psX[i % 2].rearrange("p (h e) -> p h e", h=4)).then_inc(s_Xc, 1)
                    else:
                        nc.vector.tensor_copy(K[:, c], psX[i % 2][:, 0:P]).then_inc(s_Xc, 1)
                dve.wait_ge(s_Xc, len(steps))
                nc.vector.memset(Rup[:, :, 0:1], 0.0)
                nc.vector.memset(Rdown[:, :, P - 1:P], 0.0)
                for c in range(4):
                    last = nc.vector.tensor_tensor(Rup[:, c, 1:P], K[:, c, 1:P], K[:, c, 0:P - 1], ALU.is_equal)
                link(last)
                link(nc.vector.tensor_scalar(Rup[:, :, 1:P], Rup[:, :, 1:P], FAR, -FAR, ALU.mult, ALU.add))
                link(nc.vector.tensor_copy(Rdown[:, :, 0:P - 1], Rup[:, :, 1:P]))
                for c in range(4):
                    for h in range(H):
                        nc.vector.tensor_tensor_scan(up[:, c, h], Rup[:, c], X[:, c, h], -FAR, ALU.add, ALU.max)
                        last = nc.vector.tensor_tensor_scan(down[:, c, h, ::-1], Rdown[:, c, ::-1], X[:, c, h, ::-1],
                                                            -FAR, ALU.add, ALU.max)
                last.then_inc(s_ends, 1)
                dve.wait_ge(s_E, 1)
                for k in range(4):
                    nc.vector.tensor_copy(ends[:, k], psE[k][:, :])
                link(nc.vector.memset(carry[:, :, :], -FAR))
                first, final = ends[:, 2], ends[:, 3]
                link(nc.vector.tensor_tensor(same[:, 0, 1:NT], first[:, 1:NT], final[:, 0:NT - 1], ALU.is_equal))
                link(nc.vector.tensor_tensor(same[:, 1], first, final, ALU.is_equal))
                link(nc.vector.memset(same[:, 2:4], -FAR))
                link(nc.vector.memset(same[:, 0, 0:1], 0.0))
                link(nc.vector.tensor_tensor(same[:, 2, 1:NT], same[:, 0, 1:NT], same[:, 1, 1:NT], ALU.mult))
                link(nc.vector.tensor_tensor(same[:, 3, 0:NT - 1], same[:, 0, 1:NT], same[:, 1, 0:NT - 1], ALU.mult))
                link(nc.vector.tensor_scalar(same[:, 0], same[:, 0], FAR, -FAR, ALU.mult, ALU.add))
                link(nc.vector.tensor_scalar(same[:, 2, 1:NT], same[:, 2, 1:NT], FAR, -FAR, ALU.mult, ALU.add))
                link(nc.vector.tensor_scalar(same[:, 3, 0:NT - 1], same[:, 3, 0:NT - 1], FAR, -FAR, ALU.mult, ALU.add))
                link(nc.vector.tensor_tensor_scan(run[:, 0], same[:, 2], ends[:, 0], -FAR, ALU.add, ALU.max))
                link(nc.vector.tensor_tensor_scan(run[:, 1, ::-1], same[:, 3, ::-1], ends[:, 1, ::-1], -FAR, ALU.add, ALU.max))
                nc.vector.tensor_tensor(carry[:, 0, 1:NT], run[:, 0, 0:NT - 1], same[:, 0, 1:NT], ALU.add)
                nc.vector.tensor_tensor(carry[:, 1, 0:NT - 1], run[:, 1, 1:NT], same[:, 0, 1:NT], ALU.add).then_inc(s_carry, 1)
                dve.wait_ge(s_C, 1)
                link(nc.vector.tensor_copy(cq[:, :, :, :].rearrange("p k c h -> p (k c h)"), psC))
                for c in range(4):
                    nc.vector.tensor_scalar(Rup[:, c], K[:, c], K[:, c, 0:1], None, ALU.is_equal)
                    link(nc.vector.tensor_scalar(Rdown[:, c], K[:, c], K[:, c, P - 1:P], None, ALU.is_equal))
                link(nc.vector.tensor_scalar(Rup[:, :, :], Rup[:, :, :], FAR, -FAR, ALU.mult, ALU.add))
                link(nc.vector.tensor_scalar(Rdown[:, :, :], Rdown[:, :, :], FAR, -FAR, ALU.mult, ALU.add))
                for k, (R, m) in enumerate(((Rup, up), (Rdown, down))):
                    for c in range(4):
                        for h in range(H):
                            last = nc.vector.scalar_tensor_tensor(m[:, c, h], R[:, c], cq[:, k, c, h:h + 1], m[:, c, h],
                                                                  ALU.add, ALU.max)
                link(last)
                nc.vector.tensor_tensor(up[:, :, :, :], up[:, :, :, :], down[:, :, :, :], ALU.max).then_inc(s_M, 1)
                for i, (c, k) in enumerate((c, k) for c in range(4) for k in range(HX)):
                    dve.wait_ge(s_Mt, i + 1)
                    v = lg[:, c * Q:(c + 1) * Q, 4 * k:4 * k + 4]
                    nc.vector.tensor_tensor(v, v, psMt[0].rearrange("p (h q) -> p q h", h=4), ALU.subtract).then_inc(s_sub, 1)

            @block.scalar
            def _(act):
                act.wait_ge(s_sub, 4 * HX)
                nc.scalar.activation(lg[:, 0:NT, :], lg[:, 0:NT, :], ACT.Exp)


def phase_sum0(nc, E, sem):
    NT, RS, H = E.NT, E.RS, 4
    V = B + H
    with ExitStack() as st:
        def tmp(name, shape, dt):
            return st.enter_context(nc.sbuf_tensor(name, shape, dt))

        rows = tmp("a0_rows", [P, 2, G, RS], F32)
        oh = tmp("a0_oh", [P, 2, G, B], F32)
        val = tmp("a0_val", [P, 2, G, V], F32)
        psA = [banks(nc, st, f"a0_ps{k}", [V, G, B]) for k in (0, 1)]
        s_in = [sem("a0_in0"), sem("a0_in1")]
        s_link, s_val, s_sum, s_acc = (sem("a0_" + k) for k in ("link", "val", "sum", "acc"))
        n = NT // (2 * G)
        ss = E.ss.rearrange("p (t f) -> p t f", f=RS)
        with nc.Block() as block:
            @block.sync
            def _(sp):
                with sp.Fori(0, n) as it:
                    for par in (0, 1):
                        sp.wait_ge(s_val, upto(it, par))
                        sp.dma_start(rows[:, par], ss[:, tiles(it, par), :]).then_inc(s_in[par], 16)
                for par in (0, 1):
                    sp.wait_ge(s_in[par], 16 * n)

            @block.tensor
            def _(pe):
                with pe.Fori(0, n) as it:
                    for par in (0, 1):
                        g1 = upto(it, par)
                        pe.wait_ge(s_val, g1 + 2)
                        pe.wait_ge(s_acc, g1)
                        for j in range(G):
                            last = nc.tensor.matmul(psA[par][:, j], val[:, par, j], oh[:, par, j], start=True, stop=True)
                        last.then_inc(s_sum, 1)

            @block.vector
            def _(dve):
                link = Link(dve, s_link)
                dve.sem_inc(s_val, 2)
                dve.sem_inc(s_acc, 2)
                link(nc.vector.memset(E.acc0[:, :], 0.0))

                def values(it, par, g1):
                    sl = tiles(it, par)
                    nc.vector.tensor_tensor(oh[:, par], bc(E.iota[:, None, 0:B], [P, G, B]),
                                            bc(E.loS[:, sl][:, :, None], [P, G, B]), ALU.is_equal)
                    nc.vector.tensor_copy(val[:, par, :, B:], E.lg0[:, sl, :])
                    dve.wait_ge(s_in[par], 16 * it + 16)
                    nc.vector.tensor_tensor(val[:, par, :, 0:B].rearrange("p t (h j) -> p t h j", h=H),
                                            rows[:, par, :, B:2 * B].rearrange("p t (h j) -> p t h j", h=H),
                                            bc(E.lg0[:, sl, :][:, :, :, None], [P, G, H, B // H]),
                                            ALU.mult).then_inc(s_val, 1)

                def add(it, par, blocks):
                    dve.wait_ge(s_sum, upto(it, par))
                    for j in range(G):
                        b = blocks[par * G + j]
                        a = E.acc0[:, bass.ds(b * B, B)]
                        ins = nc.vector.tensor_tensor(a, a, psA[par][:, j], ALU.add)
                        if j < G - 1:
                            link(ins)
                        else:
                            ins.then_inc(s_acc, 1)

                with dve.Fori(0, n) as it:
                    blocks = blocks_of(nc, DVE, E.blkS, it, E.NB)
                    link.loop(1, it, 2 * (G - 1))
                    values(it, 0, None)
                    values(it, 1, None)
                    add(it, 0, blocks)
                    dve.wait_ge(s_acc, upto(it, 0) + 2)
                    add(it, 1, blocks)
                    dve.wait_ge(s_acc, upto(it, 1) + 2)
                    assert link.n == 2 * (G - 1)


def row(v):
    return v.rearrange("(p c) -> p c", p=1)


def col(v, p):
    return v.rearrange("(c p) -> p c", p=p)


def phase_nodes1(nc, E, a, sem):
    N, NB = E.N, E.NB
    CW = NC * B
    H = 4
    H1 = 8
    with ExitStack() as st:
        def tmp(name, shape, dt=F32):
            return st.enter_context(nc.sbuf_tensor("n1_" + name, shape, dt))

        def pst(name, shape):
            return banks(nc, st, "n1_" + name, shape)

        sq = tmp("sq", [B, NB, B])
        h1 = tmp("h1", [B, NB, B + H1])
        s = tmp("s", [B, 2, NB])
        sel = tmp("sel", [B + H, B])
        cen = tmp("cen", [B, P])
        outw = tmp("outw", [B, B])
        rows = tmp("rows", [1, 2, B])
        lnrow = tmp("lnrow", [B, 2, B])
        cols = tmp("cols", [B, 2])
        fcw = tmp("fcw", [B, H1, B])
        attn = tmp("attn", [H1, 2, B])
        attnT = tmp("attnT", [B, 2, H1])
        WLR = tmp("WLR", [B, 2 * H1])
        Sb = tmp("Sb", [B, CW])
        r = tmp("r", [B, CW])
        Gn = tmp("Gn", [B, CW])
        z = tmp("z", [B, CW])
        net = tmp("net", [B, 3, CW])
        ssp = tmp("ssp", [B, CW])
        hs = tmp("hs", [B, NC, B])
        hTs = tmp("hTs", [B, CW])
        psS = pst("psS", [B, CW])
        psO = pst("psO", [P, CW])
        psY = pst("psY", [B, NC, B])
        psT = pst("psT", [B, CW])
        psA = pst("psA", [B, 2 * H1])
        psL = pst("psL", [B, 2 * H1])
        psE = pst("psE", [B, NC, 2 * H1])
        names = ("zero", "in", "link", "S", "G", "O", "z", "act", "soft", "ssp", "Y", "y", "var", "sd", "h", "at", "atc",
                 "L", "w", "hs", "T", "Tc", "E", "Ec", "b", "bc", "out", "taken", "x")
        (s_zero, s_in, s_link, s_S, s_G, s_O, s_z, s_act, s_soft, s_ssp, s_Y, s_y, s_var, s_sd, s_h, s_at, s_atc,
         s_L, s_w, s_hs, s_T, s_Tc, s_E, s_Ec, s_b, s_bc, s_out, s_taken, s_x) = (sem("n1_" + k) for k in names)
        s_fill = sem("n1_fill")
        loads = 1 + 1 + 1 + 2 + H + 1 + 1 + 2
        n = NB // NC
        with nc.Block() as block:
            @block.sync
            def _(sp):
                sp.wait_ge(s_fill, 1)
                load_nodes(sp, E.x1, a["x"], N, s_x)
                sp.dma_start(cen[:, 0:B], a["L0_gnn_cen_w"]).then_inc(s_in, 16)
                sp.dma_start(outw[:, :], a["L0_gnn_out_w"]).then_inc(s_in, 16)
                sp.dma_start(rows[:, 0], row(a["L0_gnn_out_b"])).then_inc(s_in, 16)
                for k, v in enumerate(("L0_gnn_ln_g", "L0_gnn_ln_b")):
                    sp.dma_start(lnrow[:, k], bc(row(a[v]), [B, B])).then_inc(s_in, 16)
                for h in range(H):
                    sp.dma_start(cols[16 * h:16 * h + 16, 0:1], col(a["L0_gnn_wvl_b"], 16)).then_inc(s_in, 16)
                sp.dma_start(cols[:, 1:2], col(a["L0_gnn_cen_b"], B)).then_inc(s_in, 16)
                sp.dma_start(fcw[:, :, :], a["L1_gnn_fc_w"].rearrange("(h o) c -> o h c", h=H1)).then_inc(s_in, 16)
                for k, v in enumerate(("L1_gnn_attn_l", "L1_gnn_attn_r")):
                    sp.dma_start(attn[:, k], a[v]).then_inc(s_in, 16)
                sp.wait_ge(s_in, 16 * loads)
                sp.wait_ge(s_h, 2)
                sp.dma_start(E.table1.rearrange("(b p) c -> p b c", p=B), h1[:, :, :]).then_inc(s_out, 16)
                sp.wait_ge(s_out, 16)
                sp.wait_ge(s_x, 32)

            @block.gpsimd
            def _(pool):
                nc.gpsimd.memset(sel[:, :], 0.0).then_inc(s_zero, 1)
                pool.wait_ge(s_zero, 1)
                nc.gpsimd.affine_select(out=sel[:, :].rearrange("p (h j) -> p h j", h=H),
                                        in_=sel[:, :].rearrange("p (h j) -> p h j", h=H),
                                        pattern=[[-1, H], [0, B // H]], compare_op=ALU.not_equal, fill=1.0,
                                        base=-B, channel_multiplier=1).then_inc(s_zero, 1)

            @block.tensor
            def _(pe):
                I = E.ident[0:B, 0:B]
                pe.wait_ge(s_zero, 2)
                pe.wait_ge(s_in, 16 * loads)
                nc.tensor.matmul(psA[0:1, 0:1], E.ones[:, 0:1], E.ones[:, 0:1], start=True, stop=True)
                for k in (0, 1):
                    last = nc.tensor.matmul(psA[:, k * H1:(k + 1) * H1], attn[:, k], E.ident[0:H1, 0:H1], start=True, stop=True)
                last.then_inc(s_at, 1)
                pe.wait_ge(s_atc, 1)
                for k in (0, 1):
                    for h in range(H1):
                        last = nc.tensor.matmul(psL[:, k * H1 + h:k * H1 + h + 1], fcw[:, h], attnT[:, k, h:h + 1],
                                                start=True, stop=True)
                last.then_inc(s_L, 1)
                nc.tensor.matmul(psY[0:1, 0, :], E.ones[0:B, 0:1], outw[:, :], start=True, stop=True).then_inc(s_b, 1)
                pe.wait_ge(s_bc, 1)
                with pe.Fori(0, n) as c:
                    ds = bass.ds(c * CW, CW)
                    pe.wait_ge(s_G, c + 1)
                    pe.sem_inc(s_taken, 1)
                    nc.tensor.matmul(psS[:, :], sel[:, :], E.acc0[:, ds], start=True, stop=True).then_inc(s_S, 1)
                    pe.wait_ge(s_G, c + 2)
                    pe.wait_ge(s_z, c + 1)
                    pe.sem_inc(s_taken, 1)
                    nc.tensor.matmul(psO[:, :], E.wvl[:, :], Gn[:, :], start=True, stop=False)
                    nc.tensor.matmul(psO[:, :], cen[:, :], E.h0T[:, ds], start=False, stop=True).then_inc(s_O, 1)
                    pe.wait_ge(s_ssp, c + 1)
                    pe.wait_ge(s_y, c + 1)
                    pe.sem_inc(s_taken, 1)
                    for j in range(NC):
                        nc.tensor.matmul(psY[:, j], ssp[:, j * B:(j + 1) * B], outw[:, :], start=True, stop=False)
                        last = nc.tensor.matmul(psY[:, j], E.ones[0:1, 0:B], rows[:, 1], start=False, stop=True)
                    last.then_inc(s_Y, 1)
                with pe.Fori(0, n) as c:
                    pe.wait_ge(s_hs, c + 1)
                    pe.sem_inc(s_taken, 1)
                    for j in range(NC):
                        last = nc.tensor.matmul(psT[:, j * B:(j + 1) * B], hs[:, j], I, start=True, stop=True)
                    last.then_inc(s_T, 1)
                    pe.wait_ge(s_Tc, c + 1)
                    pe.wait_ge(s_Ec, c + 1)
                    pe.sem_inc(s_taken, 1)
                    for j in range(NC):
                        last = nc.tensor.matmul(psE[:, j], hTs[:, j * B:(j + 1) * B], WLR[:, :], start=True, stop=True)
                    last.then_inc(s_E, 1)

            @block.scalar
            def _(act):
                act.wait_ge(s_in, 16 * loads)
                act.sem_inc(s_y, 1)
                with act.Fori(0, n) as c:
                    act.wait_ge(s_z, c + 2)
                    nc.scalar.activation(net[:, 0], z[:, :], ACT.Abs, bias=cols[:, 1:2]).then_inc(s_act, 1)
                    act.wait_ge(s_act, c * 2 + 1)
                    nc.scalar.activation(net[:, 1], net[:, 0], ACT.Exp, scale=-1.0).then_inc(s_act, 1)
                    act.wait_ge(s_act, c * 2 + 2)
                    nc.scalar.activation(net[:, 1], net[:, 1], ACT.Ln, bias=1.0)
                    nc.scalar.activation(net[:, 2], z[:, :], ACT.Relu, bias=cols[:, 1:2]).then_inc(s_soft, 1)
                    act.wait_ge(s_Y, c + 1)
                    nc.scalar.activation(h1[:, bass.ds(c * NC, NC), 0:B], psY[:, :, :], ACT.Copy).then_inc(s_y, 1)
                for k in (1, 2):
                    act.wait_ge(s_var, k)
                    nc.scalar.activation(s[:, 1], s[:, 1], ACT.Sqrt).then_inc(s_sd, 1)
                act.wait_ge(s_h, 1)
                with act.Fori(0, n) as c:
                    nc.scalar.activation(hs[:, :, :], h1[:, bass.ds(c * NC, NC), 0:B], ACT.Copy).then_inc(s_hs, 1)
                    act.wait_ge(s_T, c + 1)

            @block.vector
            def _(dve):
                link = Link(dve, s_link)
                nc.vector.memset(E.x1[:, NB - 1], 0.0)
                nc.vector.memset(cen[:, :], 0.0).then_inc(s_fill, 1)
                dve.wait_ge(s_at, 1)
                nc.vector.tensor_copy(attnT[:, :, :].rearrange("p k h -> p (k h)"), psA[:, :]).then_inc(s_atc, 1)
                dve.wait_ge(s_L, 1)
                nc.vector.tensor_copy(WLR[:, :], psL[:, :]).then_inc(s_w, 1)
                dve.wait_ge(s_b, 1)
                nc.vector.scalar_tensor_tensor(rows[:, 1], psY[0:1, 0, :], -float(np.log(2.0)), rows[:, 0],
                                               ALU.mult, ALU.add).then_inc(s_bc, 1)
                dve.sem_inc(s_G, 1)
                dve.sem_inc(s_z, 1)
                with dve.Fori(0, n) as c:
                    ds = bass.ds(c * CW, CW)
                    link.loop(0, c, 4)
                    dve.wait_ge(s_S, c + 1)
                    link(nc.vector.tensor_copy(Sb[:, :], psS[:, :]))
                    link(nc.vector.tensor_scalar(r[:, :], Sb[:, :], 1e-16, None, ALU.add))
                    link(nc.vector.reciprocal(r[:, :], r[:, :]))
                    nc.vector.tensor_tensor(Gn[:, :], E.acc0[0:B, ds], r[:, :], ALU.mult).then_inc(s_G, 1)
                    link(nc.vector.scalar_tensor_tensor(r[:, :], Sb[:, :], cols[:, 0:1], r[:, :], ALU.mult, ALU.mult))
                    dve.wait_ge(s_O, c + 1)
                    nc.vector.tensor_tensor(z[:, :], psO[0:B, :], r[:, :], ALU.add).then_inc(s_z, 1)
                    dve.wait_ge(s_soft, c + 1)
                    nc.vector.tensor_tensor(ssp[:, :], net[:, 1], net[:, 2], ALU.add).then_inc(s_ssp, 1)
                link.loop(0, n, 4)
                dve.wait_ge(s_y, n + 1)
                dve.wait_ge(s_x, 32)
                y = h1[:, :, 0:B]
                layernorm(nc, dve, None, link, y, s, sq[:, :, :], s_var, s_sd, 1)
                link(nc.vector.tensor_tensor(y, y, bc(lnrow[:, 0][:, None, :], [B, NB, B]), ALU.mult))
                link(nc.vector.tensor_tensor(y, y, bc(lnrow[:, 1][:, None, :], [B, NB, B]), ALU.add))
                link(nc.vector.tensor_tensor(E.x1[:, :, :], E.x1[:, :, :], y, ALU.add))
                link(nc.vector.tensor_copy(y, E.x1[:, :, :]))
                layernorm(nc, dve, None, link, y, s, sq[:, :, :], s_var, s_sd, 2)
                nc.vector.tensor_scalar(y, y, 0.0, None, ALU.max).then_inc(s_h, 1)
                dve.sem_inc(s_Ec, 1)
                with dve.Fori(0, n) as c:
                    dve.wait_ge(s_T, c + 1)
                    nc.vector.tensor_copy(hTs[:, :], psT[:, :]).then_inc(s_Tc, 1)
                    dve.wait_ge(s_E, c + 1)
                    nc.vector.tensor_copy(h1[:, bass.ds(c * NC, NC), B:B + H1], psE[:, :, 0:H1])
                    nc.vector.tensor_copy(E.ertab[:, bass.ds(c * NC, NC), :], psE[:, :, H1:]).then_inc(s_Ec, 1)
                dve.wait_ge(s_Ec, n + 1)
                dve.sem_inc(s_h, 1)


def phase_gather1(nc, E, sem):
    NT, H, W = E.NT, 8, B + 8
    with ExitStack() as st:
        def tmp(name, shape, dt=F32):
            return st.enter_context(nc.sbuf_tensor("g1_" + name, shape, dt))

        g = tmp("g", [P, 2, G, W])
        idx = tmp("idx", [P, 2, G], I32)
        oh = tmp("oh", [P, 2, G, B])
        ohT = tmp("ohT", [B, 2, G, P])
        sum_ = tmp("sum", [P, G, H])
        psT = banks(nc, st, "g1_psT", [B, G, P])
        psR = banks(nc, st, "g1_psR", [P, G, H])
        s_g = [sem("g1_g0"), sem("g1_g1")]
        s_st = [sem("g1_st0"), sem("g1_st1")]
        s_oh, s_T, s_ohT, s_r, s_lg, s_link, s_free, s_taken, s_taken2 = (
            sem("g1_" + k) for k in ("oh", "T", "ohT", "r", "lg", "link", "free", "taken", "taken2"))
        n = NT // (2 * G)
        hd = E.hg.rearrange("p (t f) -> p t f", f=W)
        with nc.Block() as block:
            @block.gpsimd
            def _(pool):
                with pool.Fori(0, n) as it:
                    for par in (0, 1):
                        pool.wait_ge(s_oh, upto(it, par))
                        pool.wait_ge(s_free, upto(it, par))
                        pool.wait_ge(s_lg, upto(it, par))
                        pool.sem_inc(s_taken2, 1)
                        for j in range(G):
                            nc.gpsimd.indirect_dma_start(
                                out=g[:, par, j, :], out_offset=None, in_=E.table1,
                                in_offset=bass.IndirectOffsetOnAxis(ap=idx[:, par, j:j + 1], axis=0)).then_inc(s_g[par], 16)
                for par in (0, 1):
                    pool.wait_ge(s_g[par], 64 * n)

            @block.sync
            def _(sp):
                sp.sem_inc(s_free, 1)
                sp.dma_start(E.hg[0:1, 0:W], E.table1[0:1, :]).then_inc(s_st[1], 16)
                with sp.Fori(0, n) as it:
                    for par in (0, 1):
                        sp.wait_ge(s_st[1 - par], it * 16 + 16)
                        sp.sem_inc(s_free, 1)
                        sp.wait_ge(s_g[par], it * 64 + 64)
                        sp.dma_start(hd[:, tiles(it, par), :], g[:, par]).then_inc(s_st[par], 16)
                sp.wait_ge(s_st[0], 16 * n)
                sp.wait_ge(s_st[1], 16 * n + 16)

            @block.tensor
            def _(pe):
                with pe.Fori(0, n) as it:
                    blocks = blocks_of(nc, PE, E.blkD, it, E.NB)
                    for par in (0, 1):
                        g1 = upto(it, par)
                        pe.wait_ge(s_oh, g1)
                        pe.wait_ge(s_ohT, g1)
                        for j in range(G):
                            last = nc.tensor.matmul(psT[:, j], oh[:, par, j], E.ident[:, :], start=True, stop=True)
                        last.then_inc(s_T, 1)
                        pe.wait_ge(s_ohT, g1 + 1)
                        pe.wait_ge(s_lg, g1 + 1)
                        pe.sem_inc(s_taken, 1)
                        for j in range(G):
                            b = blocks[par * G + j]
                            last = nc.tensor.matmul(psR[:, j], ohT[:, par, j], E.ertab[:, bass.ds(b, 1), :],
                                                    start=True, stop=True)
                        last.then_inc(s_r, 1)

            @block.scalar
            def _(act):
                act.sem_inc(s_ohT, 1)
                with act.Fori(0, n) as it:
                    for par in (0, 1):
                        act.wait_ge(s_T, upto(it, par))
                        nc.scalar.activation(ohT[:, par], psT[:, :, :], ACT.Copy).then_inc(s_ohT, 1)

            @block.vector
            def _(dve):
                link = Link(dve, s_link)
                dve.sem_inc(s_lg, 2)

                def onehots(tile0, par):
                    sl = bass.ds(tile0, G)
                    nc.vector.tensor_copy(idx[:, par], E.srcI[:, sl])
                    nc.vector.tensor_tensor(oh[:, par], bc(E.iota[:, None, 0:B], [P, G, B]),
                                            bc(E.loD[:, sl][:, :, None], [P, G, B]), ALU.is_equal).then_inc(s_oh, 1)

                nc.vector.memset(E.lg1[:, NT:], 0.0)
                onehots(0, 0)
                with dve.Fori(0, n) as it:
                    link.loop(0, it, 2)
                    for par in (0, 1):
                        if par == 1:
                            dve.wait_ge(s_g[0], it * 64 + 64)
                        else:
                            dve.wait_ge(s_oh, it * 2 + 1)
                        onehots(it * (2 * G) + (par + 1) * G, 1 - par)
                        dve.wait_ge(s_r, upto(it, par))
                        dve.wait_ge(s_g[par], it * 64 + 64)
                        link(nc.vector.tensor_tensor(sum_[:, :, :], g[:, par, :, B:], psR[:, :, :], ALU.add))
                        nc.vector.scalar_tensor_tensor(E.lg1[:, tiles(it, par), :], sum_[:, :, :], 0.2, sum_[:, :, :],
                                                       ALU.mult, ALU.max).then_inc(s_lg, 1)
                    assert link.n == 2


def phase_sum1(nc, E, sem):
    NT, H, W = E.NT, 8, B + 8
    with ExitStack() as st:
        def tmp(name, shape, dt=F32):
            return st.enter_context(nc.sbuf_tensor("a1_" + name, shape, dt))

        rows = tmp("rows", [P, 2, G, W])
        oh = tmp("oh", [P, 2, G, B])
        val = tmp("val", [P, 2, G, 5, P])
        psA = [[banks(nc, st, f"a1_ps{k}{j}", [P, 5, B]) for j in range(G)] for k in (0, 1)]
        s_in = [sem("a1_in0"), sem("a1_in1")]
        s_link, s_ez, s_val, s_valA, s_valP, s_sum, s_acc, s_taken, s_free = (
            sem("a1_" + k) for k in ("link", "ez", "val", "valA", "valP", "sum", "acc", "taken", "free"))
        n = NT // (2 * G)
        hd = E.hg.rearrange("p (t f) -> p t f", f=W)
        of_act, of_pool = (2,), (3,)
        of_dve = tuple(j for j in range(G) if j not in of_act + of_pool)

        def product(par, j):
            return (val[:, par, j, 0:4].rearrange("p k (h c) -> p (k h) c", h=2), bc(rows[:, par, j, None, 0:B], [P, H, B]),
                    bc(val[:, par, j, 4, 0:H][:, :, None], [P, H, B]))

        with nc.Block() as block:
            @block.sync
            def _(sp):
                with sp.Fori(0, n) as it:
                    for par in (0, 1):
                        sp.wait_ge(s_val, upto(it, par))
                        sp.wait_ge(s_valA, upto(it, par))
                        sp.wait_ge(s_valP, upto(it, par))
                        sp.dma_start(rows[:, par], hd[:, tiles(it, par), :]).then_inc(s_in[par], 16)
                for s in (s_val, s_valA, s_valP):
                    sp.wait_ge(s, 2 * n + 1)
                sp.dma_start(rows[:, 0], hd[:, 0:G, :]).then_inc(s_in[0], 16)
                sp.wait_ge(s_in[0], 16 * n + 16)
                sp.wait_ge(s_in[1], 16 * n)

            @block.tensor
            def _(pe):
                with pe.Fori(0, n) as it:
                    for par in (0, 1):
                        g1 = upto(it, par)
                        pe.wait_ge(s_val, g1 + 2)
                        pe.wait_ge(s_acc, g1)
                        for j in of_dve:
                            for k in range(5):
                                nc.tensor.matmul(psA[par][j][:, k], val[:, par, j, k], oh[:, par, j], start=True, stop=True)
                        pe.wait_ge(s_valA, g1 + 2)
                        pe.wait_ge(s_valP, g1 + 2)
                        for j in of_act + of_pool:
                            for k in range(5):
                                last = nc.tensor.matmul(psA[par][j][:, k], val[:, par, j, k], oh[:, par, j],
                                                        start=True, stop=True)
                        last.then_inc(s_sum, 1)

            @block.scalar
            def _(act):
                def values(par, ez, loaded):
                    act.wait_ge(s_ez, ez)
                    act.wait_ge(s_in[par], loaded)
                    for j in of_act:
                        for h in range(H):
                            last = nc.scalar.activation(val[:, par, j, h // 2, (h % 2) * B:(h % 2 + 1) * B],
                                                        rows[:, par, j, 0:B], ACT.Copy,
                                                        scale=val[:, par, j, 4, h:h + 1])
                    last.then_inc(s_valA, 1)

                act.sem_inc(s_valA, 2)
                with act.Fori(0, n) as it:
                    for par in (0, 1):
                        values(par, upto(it, par), 16 * it + 16)
                values(0, 2 * n + 1, 16 * n + 16)

            @block.gpsimd
            def _(pool):
                def values(par, ez, loaded):
                    pool.wait_ge(s_ez, ez)
                    pool.wait_ge(s_in[par], loaded)
                    for j in of_pool:
                        out, h, e = product(par, j)
                        last = nc.gpsimd.tensor_tensor(out, h, e, ALU.mult)
                    last.then_inc(s_valP, 1)

                pool.sem_inc(s_valP, 2)
                with pool.Fori(0, n) as it:
                    for par in (0, 1):
                        values(par, upto(it, par), 16 * it + 16)
                values(0, 2 * n + 1, 16 * n + 16)

            @block.vector
            def _(dve):
                link = Link(dve, s_link)
                nc.vector.memset(val[:, :, :, 4], 0.0)
                link(nc.vector.memset(E.acc1[:, :, :], 0.0))
                dve.sem_inc(s_val, 2)
                dve.sem_inc(s_acc, 2)

                def values(tile0, par, free, loaded):
                    if free is not None:
                        dve.wait_ge(s_sum, free)
                    sl = bass.ds(tile0, G)
                    nc.vector.tensor_copy(val[:, par, :, 4, 0:H], E.lg1[:, sl, :]).then_inc(s_ez, 1)
                    nc.vector.tensor_tensor(oh[:, par], bc(E.iota[:, None, 0:B], [P, G, B]),
                                            bc(E.loD[:, sl][:, :, None], [P, G, B]), ALU.is_equal)
                    dve.wait_ge(s_in[par], loaded)
                    dve.wait_ge(s_ez, free + 1 if free is not None else 1)
                    for j in of_dve:
                        out, h, e = product(par, j)
                        last = nc.vector.tensor_tensor(out, h, e, ALU.mult)
                    last.then_inc(s_val, 1)

                def add(it, par, blocks):
                    dve.wait_ge(s_sum, upto(it, par) + 1)
                    for j in range(G):
                        v = E.acc1[:, :, bass.ds(blocks[par * G + j] * B, B)]
                        ins = nc.vector.tensor_tensor(v, v, psA[par][j][:, :, :], ALU.add)
                        if j < G - 1:
                            link(ins)
                        else:
                            ins.then_inc(s_acc, 1)
                    dve.wait_ge(s_acc, upto(it, par) + 2)

                dve.sem_inc(s_sum, 1)
                values(0, 0, None, 16)
                with dve.Fori(0, n) as it:
                    blocks = blocks_of(nc, DVE, E.blkD, it, E.NB)
                    link.loop(1, it, 2 * (G - 1))
                    for par in (0, 1):
                        values(it * (2 * G) + (par + 1) * G, 1 - par, upto(it, par), 16 * it + 16 * (par + 1))
                        add(it, par, blocks)
                    assert link.n == 2 * (G - 1)


def phase_dense1(nc, E, a, out, sem):
    N, NB = E.N, E.NB
    CW = NC * B
    n = NB // NC
    FM = a["L1_gnn_w1"].shape[0] // P
    with ExitStack() as st:
        def tmp(name, shape, dt=F32):
            return st.enter_context(nc.sbuf_tensor("d_" + name, shape, dt))

        def pst(name, shape):
            return banks(nc, st, "d_" + name, shape)

        fcs = tmp("fcs", [B, 8, B])
        FC = tmp("FC", [P, 4, P])
        selR = tmp("selR", [8, 4, P])
        rec = tmp("rec", [8, NB * B])
        rb = tmp("rb", [P, 2, CW])
        w1s = tmp("w1s", [P, 2, 4 * P])
        w1T = tmp("w1T", [P, 4, FM * P])
        w2s = tmp("w2s", [B, FM, P])
        w2T = tmp("w2T", [P, FM, B])
        c1 = tmp("c1", [P, 4, 3])
        bb1 = tmp("bb1", [P, FM])
        c2 = tmp("c2", [B, 3])
        st1 = tmp("st1", [P, 4, n, 6])
        mv1 = tmp("mv1", [P, 4, 2])
        sc1 = tmp("sc1", [P, 4, 3])
        st2 = tmp("st2", [B, n, 6])
        mv2 = tmp("mv2", [B, 2])
        sc2 = tmp("sc2", [B, 3])
        hn = tmp("hn", [P, 4, CW])
        h2 = tmp("h2", [P, 2, CW])
        yT = tmp("yT", [B, NB * B])
        yn = tmp("yn", [B, CW])
        fin = tmp("fin", [B, NC, B])
        pw = [pst(f"ps{k}", [P, BANK]) for k in range(4)]
        ps = [v[:, 0:CW] for v in pw]
        psY = pst("psY", [B, CW])
        psZ = pst("psZ", [B, NC, B])
        names = ("zero", "in", "link", "w1", "tp", "tpc", "R", "Rb", "rbc", "Rw", "bn", "sd", "sdd", "hn", "h", "h2",
                 "Y", "y", "yn", "Z", "fin", "out", "taken", "w1f", "rec", "hn1", "last", "fcc", "bn2")
        (s_zero, s_in, s_link, s_w1, s_tp, s_tpc, s_R, s_Rb, s_rbc, s_Rw, s_bn, s_sd, s_sdd, s_hn, s_h, s_h2,
         s_Y, s_y, s_yn, s_Z, s_fin, s_out, s_taken, s_w1f, s_rec, s_hn1, s_last, s_fcc, s_bn2) = (sem("d_" + k) for k in names)
        s_w1d = [sem("d_w1d0"), sem("d_w1d1")]
        s_outd = sem("d_outd")
        loads = 1 + 1 + 3 + 1 + 3
        ntp = FM + 2 + 4
        edge = [CW] * (n - 1) + [N - (n - 1) * CW]
        with nc.Block() as block:
            @block.sync
            def _(sp):
                sp.dma_start(fcs[:, :, :], a["L1_gnn_fc_w"].rearrange("(h o) c -> o h c", h=8)).then_inc(s_in, 16)
                sp.dma_start(w2s[:, :, :], a["L1_gnn_w2"].rearrange("o (m p) -> o m p", p=P)).then_inc(s_in, 16)
                for k, v in enumerate(("L1_gnn_gat_bias", "L1_gnn_bn1_gamma", "L1_gnn_bn1_beta")):
                    sp.dma_start(c1[:, :, k:k + 1], a[v].rearrange("(k p c) -> p k c", p=P, c=1),
                                 allow_slow_non_contiguous=True).then_inc(s_in, 16)
                sp.dma_start(bb1[:, :, None], a["L1_gnn_b1"].rearrange("(k p c) -> p k c", p=P, c=1),
                                 allow_slow_non_contiguous=True).then_inc(s_in, 16)
                for k, v in enumerate(("L1_gnn_b2", "L1_gnn_bn2_gamma", "L1_gnn_bn2_beta")):
                    sp.dma_start(c2[:, k:k + 1], col(a[v], B)).then_inc(s_in, 16)
                for m in range(FM):
                    if m >= 2:
                        sp.wait_ge(s_tp, m - 1)
                    sp.dma_start(w1s[:, m % 2], a["L1_gnn_w1"][m * P:(m + 1) * P]).then_inc(s_w1d[m % 2], 16)
                sp.wait_ge(s_in, 16 * loads)
                sp.sem_inc(s_out, 1)
                full = N // B
                ov = out[0:full * B].rearrange("(b p) c -> p b c", p=B)
                with sp.Fori(0, n - 1) as c:
                    sp.wait_ge(s_fin, c + 1)
                    sp.dma_start(ov[:, bass.ds(c * NC, NC), :], fin[:, :, :]).then_inc(s_outd, 16)
                    sp.wait_ge(s_outd, c * 16 + 16)
                    sp.sem_inc(s_out, 1)
                sp.wait_ge(s_fin, n)
                sp.dma_start(ov[:, (n - 1) * NC:full, :], fin[:, 0:full - (n - 1) * NC]).then_inc(s_outd, 16)
                sp.dma_start(out[full * B:N], fin[0:N - full * B, NC - 1]).then_inc(s_outd, 16)
                sp.wait_ge(s_outd, 16 * (n + 1))

            @block.gpsimd
            def _(pool):
                nc.gpsimd.memset(selR[:, :, :], 0.0).then_inc(s_zero, 1)
                pool.wait_ge(s_zero, 1)
                v = selR[:, :, :].rearrange("p k (h c) -> p (k h) c", h=2)
                nc.gpsimd.affine_select(out=v, in_=v, pattern=[[-1, 8], [0, B]], compare_op=ALU.not_equal, fill=1.0,
                                        base=0, channel_multiplier=1).then_inc(s_zero, 1)

            def second(pe, c, m):
                if m == 0:
                    pe.wait_ge(s_y, c + 1)
                pe.wait_ge(s_h, c * FM + m + 5)
                last = nc.tensor.matmul(psY[:, :], w2T[:, m], h2[:, m % 2], start=(m == 0), stop=(m == FM - 1))
                last.then_inc(s_Y, 1)

            @block.tensor
            def _(pe):
                I = E.ident[0:B, 0:B]
                pe.wait_ge(s_in, 16 * loads)
                pe.wait_ge(s_zero, 2)
                for m in range(ntp):
                    if m >= 4:
                        pe.wait_ge(s_tpc, m - 3)
                    b = pw[m % 4]
                    if m < FM:
                        pe.wait_ge(s_w1d[m % 2], 16 * (m // 2 + 1))
                        for k in range(4):
                            last = nc.tensor.matmul(b[:, k * P:(k + 1) * P], w1s[:, m % 2, k * P:(k + 1) * P], E.ident[:, :],
                                                    start=True, stop=True)
                    elif m < FM + 2:
                        for k in range(4):
                            last = nc.tensor.matmul(b[:, k * B:(k + 1) * B], w2s[:, (m - FM) * 4 + k], I, start=True, stop=True)
                    else:
                        for k in (0, 1):
                            last = nc.tensor.matmul(b[64 * k:64 * k + 64, 64 * k:64 * k + 64], fcs[:, 2 * (m - FM - 2) + k],
                                                    I, start=True, stop=True)
                    last.then_inc(s_tp, 1)
                pe.wait_ge(s_tpc, ntp)
                pe.wait_ge(s_rec, 1)
                with pe.Fori(0, n) as c:
                    ds = bass.ds(c * CW, CW)
                    for k in range(4):
                        q = k % 2
                        pe.wait_ge(s_Rw, c * 4 + k + 1)
                        pe.sem_inc(s_taken, 1)
                        nc.tensor.matmul(ps[2 + q][:, :], selR[:, k], rec[:, ds], start=True, stop=True).then_inc(s_Rb, 1)
                        nc.tensor.matmul(ps[q][:, :], FC[:, k], E.acc1[:, k, ds], start=True, stop=True).then_inc(s_R, 1)
                pe.sem_inc(s_Y, 2)
                with pe.Fori(0, n) as c:
                    pe.wait_ge(s_hn, c + 1)
                    for m in range(FM):
                        pe.wait_ge(s_h, c * FM + m + 1)
                        for k in range(4):
                            last = nc.tensor.matmul(ps[m % 4][:, :], w1T[:, k, m * P:(m + 1) * P], hn[:, k],
                                                    start=(k == 0), stop=(k == 3))
                        last.then_inc(s_h2, 1)
                        if m >= 1:
                            second(pe, c, m - 1)
                    second(pe, c, FM - 1)
                pe.wait_ge(s_bn2, 1)
                with pe.Fori(0, n) as c:
                    pe.wait_ge(s_yn, c + 1)
                    pe.sem_inc(s_taken, 1)
                    for j in range(NC):
                        last = nc.tensor.matmul(psZ[:, j], yn[:, j * B:(j + 1) * B], I, start=True, stop=True)
                    last.then_inc(s_Z, 1)

            @block.scalar
            def _(act):
                with act.Fori(0, n) as c:
                    for k in range(4):
                        act.wait_ge(s_Rb, c * 4 + k + 1)
                        act.wait_ge(s_Rw, c * 4 + k + 1)
                        nc.scalar.activation(rb[:, k % 2], ps[2 + k % 2][:, :], ACT.Copy).then_inc(s_rbc, 1)
                act.wait_ge(s_sd, 1)
                nc.scalar.activation(sc1[:, :, 0], sc1[:, :, 0], ACT.Sqrt).then_inc(s_sdd, 1)
                act.wait_ge(s_hn1, 1)
                act.sem_inc(s_h, 4)
                with act.Fori(0, n) as c:
                    for k in range(4):
                        last = nc.scalar.activation(hn[:, k], E.acc1[:, k, bass.ds(c * CW, CW)], ACT.Identity,
                                                    bias=sc1[:, k, 2:3], scale=sc1[:, k, 1:2])
                    last.then_inc(s_hn, 1)
                    for m in range(FM):
                        act.wait_ge(s_h2, c * FM + m + 1)
                        act.wait_ge(s_Y, c * FM + m + 1)
                        nc.scalar.activation(h2[:, m % 2], ps[m % 4][:, :], ACT.Relu, bias=bb1[:, m:m + 1]).then_inc(s_h, 1)
                act.wait_ge(s_sd, 2)
                nc.scalar.activation(sc2[:, 0:1], sc2[:, 0:1], ACT.Sqrt).then_inc(s_sdd, 1)
                act.wait_ge(s_bn2, 1)
                with act.Fori(0, n) as c:
                    nc.scalar.activation(yn[:, :], yT[:, bass.ds(c * CW, CW)], ACT.Identity, bias=sc2[:, 2:3],
                                         scale=sc2[:, 1:2]).then_inc(s_yn, 1)
                    act.wait_ge(s_fin, c + 1)

            @block.vector
            def _(dve):
                link = Link(dve, s_link)
                link(nc.vector.memset(FC[:, :, :], 0.0))
                for m in range(ntp):
                    dve.wait_ge(s_tp, m + 1)
                    b = pw[m % 4]
                    if m < FM:
                        nc.vector.tensor_copy(w1T[:, :, m * P:(m + 1) * P], b.rearrange("p (k c) -> p k c", k=4)).then_inc(s_tpc, 1)
                    elif m < FM + 2:
                        nc.vector.tensor_copy(w2T[:, (m - FM) * 4:(m - FM) * 4 + 4], b[:, 0:4 * B].rearrange("p (k c) -> p k c", k=4)).then_inc(s_tpc, 1)
                    else:
                        for k in (0, 1):
                            q = slice(64 * k, 64 * k + 64)
                            last = nc.vector.tensor_copy(FC[q, m - FM - 2, q], b[q, q])
                        last.then_inc(s_tpc, 1)
                link(nc.vector.tensor_scalar(rec[:, :], E.acc1[0:8, 4, :], 1e-30, None, ALU.max))
                nc.vector.reciprocal(rec[:, :], rec[:, :]).then_inc(s_rec, 1)
                dve.sem_inc(s_Rw, 2)
                with dve.Fori(0, n) as c:
                    link.loop(2, c, 4)
                    for k in range(4):
                        v = E.acc1[:, k, bass.ds(c * CW, CW)]
                        dve.wait_ge(s_R, c * 4 + k + 1)
                        dve.wait_ge(s_rbc, c * 4 + k + 1)
                        link(nc.vector.tensor_tensor(v, ps[k % 2][:, :], rb[:, k % 2], ALU.mult))
                        nc.vector.tensor_scalar(v, v, c1[:, k, 0:1], None, ALU.add).then_inc(s_Rw, 1)
                link.loop(2, n, 4)
                dve.wait_ge(s_Rw, 4 * n + 2)
                for k in range(4):
                    for c in range(n):
                        last = nc.vector.bn_stats(st1[:, k, c], E.acc1[:, k, c * CW:c * CW + edge[c]])
                link(last)
                for k in range(4):
                    last = nc.vector.bn_aggr(mv1[:, k], st1[:, k].rearrange("p a b -> p (a b)"))
                link(last)
                batchnorm_scale(nc, dve, link, mv1[:, :, 0], mv1[:, :, 1], sc1[:, :, 0], sc1[:, :, 1], sc1[:, :, 2],
                                c1[:, :, 1], c1[:, :, 2], s_sd, s_sdd, 1)
                dve.sem_inc(s_hn1, 1)
                dve.sem_inc(s_y, 1)
                with dve.Fori(0, n) as c:
                    dve.wait_ge(s_Y, c * FM + FM + 2)
                    nc.vector.tensor_scalar(yT[:, bass.ds(c * CW, CW)], psY[:, :], c2[:, 0:1], None, ALU.add).then_inc(s_y, 1)
                dve.wait_ge(s_y, n + 1)
                for c in range(n):
                    last = nc.vector.bn_stats(st2[:, c], yT[:, c * CW:c * CW + edge[c]])
                link(last)
                link(nc.vector.bn_aggr(mv2[:, :], st2[:, :, :].rearrange("p a b -> p (a b)")))
                batchnorm_scale(nc, dve, link, mv2[:, 0:1], mv2[:, 1:2], sc2[:, 0:1], sc2[:, 1:2], sc2[:, 2:3],
                                c2[:, 1:2], c2[:, 2:3], s_sd, s_sdd, 2)
                dve.sem_inc(s_bn2, 1)
                with dve.Fori(0, n) as c:
                    dve.wait_ge(s_Z, c + 1)
                    dve.wait_ge(s_out, c + 1)
                    nc.vector.tensor_tensor(fin[:, :, :], psZ[:, :, :], E.x1[:, bass.ds(c * NC, NC), :],
                                            ALU.add).then_inc(s_fin, 1)


def batchnorm_scale(nc, dve, link, mean, var, sd, scale, shift, gamma, beta, s_sd, s_sdd, n):
    nc.vector.tensor_scalar(sd, var, 1e-5, None, ALU.add).then_inc(s_sd, 1)
    dve.wait_ge(s_sdd, n)
    link(nc.vector.reciprocal(sd, sd))
    link(nc.vector.tensor_tensor(scale, sd, gamma, ALU.mult))
    link(nc.vector.tensor_tensor(shift, mean, scale, ALU.mult))
    link(nc.vector.tensor_tensor(shift, beta, shift, ALU.subtract))


class LinkLoop:
    pass


def phase_setup(nc, E, a, sb, ps, sem, stack):
    N, NT, NT0 = E.N, E.NT, E.NT0
    with ExitStack() as st:
        def tmp(name, shape, dt):
            return st.enter_context(nc.sbuf_tensor(name, shape, dt))

        def pst(name, shape, dt):
            return banks(nc, st, name, shape)

        H = Hist(nc, tmp, pst, sem, "D", NT0)
        idx = tmp("idx", [P, 2, NT0], I32)
        ti = tmp("ti", [P, NT0], I32)
        unset = tmp("unset", [P, 2 * max(E.RD, E.RS)], F32)
        s_ones, s_mask, s_fill, s_in, s_dve, s_low = (sem(n) for n in
                                                      ("s_ones", "s_mask", "s_fill", "s_in", "s_dve", "s_low"))
        s_hz = sem("s_hz")
        full = P - 1
        last = E.E - full * NT0
        with nc.Block() as block:
            @block.gpsimd
            def _(pool):
                masks_pool(nc, pool, E, s_ones, s_mask)
                pool.wait_ge(s_low, 1)
                for table, width, done in ((E.sd, E.RD, E.scatD), (E.ss, E.RS, E.scatS)):
                    w = NT * width // 8
                    for k in range(8):
                        pool.dma_start(table[:, k * w:(k + 1) * w].rearrange("p (n w) -> p n w", w=2 * width),
                                       bc(unset[:, None, 0:2 * width], [P, NT // 16, 2 * width])).then_inc(done[k % 2], 16)
                for par in (0, 1):
                    pool.wait_ge(E.scatD[par], 64)

            @block.sync
            def _(sp):
                sp.wait_ge(s_fill, 1)
                for k, v in enumerate((a["src"], a["dst"])):
                    sp.dma_start(idx[0:full, k], v[0:full * NT0].rearrange("(p t) -> p t", p=full)).then_inc(s_in, 16)
                    sp.dma_start(idx[full:P, k, 0:last], v[full * NT0:E.E].rearrange("(p t) -> p t", p=1)).then_inc(s_in, 16)
                ea = a["edge_attr_16"]
                sp.dma_start(E.attr[0:full], ea[0:full * NT0].rearrange("(p t) f -> p t f", p=full)).then_inc(s_in, 16)
                sp.dma_start(E.attr[full:P, 0:last], ea[full * NT0:E.E].rearrange("(p t) f -> p t f", p=1)).then_inc(s_in, 16)
                sp.wait_ge(s_in, 96)

            @block.vector
            def _(dve):
                link = Link(dve, s_dve)
                nc.vector.memset(E.attr[96:P], 0.0)
                nc.vector.memset(idx[96:P], E.NB * B - 1).then_inc(s_fill, 1)
                nc.vector.memset(unset[:, :], -1.0).then_inc(s_low, 1)
                nc.vector.memset(H.zero[:, :], 0.0).then_inc(s_hz, 1)
                link(nc.vector.memset(E.key0[:, :, NT0:], -1.0))
                link(nc.vector.memset(E.hi0[:, NT0:], -1.0))
                link(nc.vector.memset(E.lo0[:, NT0:], -1.0))
                dve.wait_ge(s_mask, 1)
                link(nc.vector.tensor_copy(E.iota[:, :], E.iota_i[:, :]))
                dve.wait_ge(s_in, 96)
                link(nc.vector.tensor_copy(E.key0[:, 0, 0:NT0], idx[:, 0]))
                split_keys(nc, link, E.key0[:, 1, 0:NT0], idx[:, 1], E.hi0[:, 0:NT0], E.lo0[:, 0:NT0], ti[:, :])
                histogram_vector(nc, dve, E, H, E.hi0, E.lo0)
                base_vector(nc, dve, E, H, link, E.T0D[:, :], E.blkD[:, :])

            @block.tensor
            def _(pe):
                pe.wait_ge(s_hz, 1)
                pe.sem_inc(H.counted, 2)
                histogram_tensor(nc, pe, E, H)
                base_tensor(nc, pe, E, H)


def phase_sort_dst(nc, E, sem):
    NT, NT0 = E.NT, E.NT0
    with ExitStack() as st:
        def tmp(name, shape, dt):
            return st.enter_context(nc.sbuf_tensor(name, shape, dt))

        def pst(name, shape, dt):
            return banks(nc, st, name, shape)

        R = Rank(nc, tmp, pst, sem, "RD")
        pay = tmp("payD", [P, 2, G, E.RD], F32)
        s_link, s_pay, s_taken = sem("s_linkD"), sem("s_payD"), sem("s_takenD")
        n = NT0 // (2 * G)
        keys = (E.hi0, E.lo0, E.key0[:, 1])
        with nc.Block() as block:
            @block.tensor
            def _(pe):
                pe.sem_inc(R.keyrow_ready, 2)
                pe.sem_inc(R.look_ready, 2)
                with pe.Fori(0, n) as it:
                    for par in (0, 1):
                        rank_tensor(nc, pe, E, R, it, par)

            @block.scalar
            def _(act):
                act.sem_inc(R.ohT_ready, 1)
                with act.Fori(0, n) as it:
                    for par in (0, 1):
                        act.wait_ge(E.scatD[par], 64 * it + 64)
                        nc.scalar.activation(pay[:, par, :, 0:2], E.key0[:, :, tiles(it, par)].rearrange("p k t -> p t k"), ACT.Copy)
                        nc.scalar.activation(pay[:, par, :, 2:E.RD], E.attr[:, tiles(it, par), :],
                                             ACT.Copy).then_inc(s_pay, 1)
                        rank_scalar(nc, act, R, it, par)

            @block.vector
            def _(dve):
                link = Link(dve, s_link)
                dve.sem_inc(R.T_ready, 1)
                dve.sem_inc(R.keyrow_free, 1)
                dve.sem_inc(R.look_free, 1)
                link(nc.vector.tensor_copy(R.T[:, 0, 0], E.T0D[:, :]))
                rank_onehots(nc, dve, E, R, keys, 0, 0, 1)
                with dve.Fori(0, n) as it:
                    link.loop(1, it, 2 * (RANK_LINKS - 1))
                    for par in (0, 1):
                        rank_onehots(nc, dve, E, R, keys, it * (2 * G) + (par + 1) * G, 1 - par, upto(it, par + 1))
                        rank_rows(nc, dve, E, R, link, it, par, NT, E.scatD)
                    assert link.n == 2 * (RANK_LINKS - 1), link.n

            @block.gpsimd
            def _(pool):
                with pool.Fori(0, n) as it:
                    for par in (0, 1):
                        pool.wait_ge(R.row_ready, upto(it, par))
                        pool.wait_ge(s_pay, upto(it, par))
                        pool.sem_inc(s_taken, 1)
                        for j in range(G):
                            nc.gpsimd.indirect_dma_start(
                                out=E.sd_rows, out_offset=bass.IndirectOffsetOnAxis(ap=R.row[:, par, j:j + 1], axis=0),
                                in_=pay[:, par, j, :], in_offset=None).then_inc(E.scatD[par], 16)
                for par in (0, 1):
                    pool.wait_ge(E.scatD[par], 64 * n + 64)


def build(nc, a, out, dbg=None):
    E = Env()
    E.N, E.E, E.EF = a["x"].shape[0], a["src"].shape[0], a["edge_attr_16"].shape[1]
    E.NB = -(-E.N // B)
    per = 2 * G * P
    E.NT0 = -(-E.E // per) * 2 * G
    most = (E.NT0 * P + E.NB * (P - 1)) // P
    E.NT = -(-most // (2 * G)) * 2 * G
    E.RD = 2 + E.EF
    E.RS = 2 * B + 1
    sdt = nc.dram_tensor("by_dst", (P, E.NT * E.RD), F32, kind="Internal").ap()
    E.sd = sdt
    sst = nc.dram_tensor("by_src", (P, E.NT * E.RS), F32, kind="Internal").ap()
    E.ss = sst
    E.ss_rows = sst.rearrange("p (t f) -> (p t) f", f=E.RS)
    E.table1 = nc.dram_tensor("table1", (E.NB * B, B + 8), F32, kind="Internal").ap()
    E.hg = nc.dram_tensor("by_dst_h", (P, E.NT * (B + 8)), F32, kind="Internal").ap()
    E.sd_rows = sdt.rearrange("p (t f) -> (p t) f", f=E.RD)
    with ExitStack() as top:
        def sb(name, shape, dt):
            return top.enter_context(nc.sbuf_tensor(name, shape, dt))

        taken = []

        def sem(name):
            taken.append(nc.alloc_semaphore(name))
            return taken[-1]

        masks(nc, E, sb, None)
        E.T0D = sb("T0D", [B, B], F32)
        E.blkD = sb("blkD", [1, E.NT], I32)
        E.T0S = sb("T0S", [B, B], F32)
        E.blkS = sb("blkS", [1, E.NT], I32)
        E.loD = sb("loD", [P, E.NT + G], F32)
        E.keyD = sb("keyD", [P, E.NT], F32)
        E.srcI = sb("srcI", [P, E.NT + G], I32)
        E.x1 = sb("x1", [B, E.NB, B], F32)
        E.ertab = sb("ertab", [B, E.NB, 8], F32)
        E.scatD = [sem("scatD0"), sem("scatD1")]
        E.scatS = [sem("scatS0"), sem("scatS1")]

        def stack(st):
            return lambda name, shape, dt: st.enter_context(nc.sbuf_tensor(name, shape, dt))

        with ExitStack() as first:
            sb1 = stack(first)
            E.h0T = sb1("h0T", [B, E.NB * B], F32)
            E.wvl = sb1("wvl", [B, P], F32)
            E.qtab = sb1("qtab", [B, E.NB, B + 4], F32)
            E.acc0 = sb1("acc0", [B + 4, E.NB * B], F32)
            with ExitStack() as st:
                sb2 = stack(st)
                E.attr = sb2("attr", [P, E.NT0, E.EF], F32)
                E.key0 = sb2("key0", [P, 2, E.NT0 + G], F32)
                E.hi0 = sb2("hi0", [P, E.NT0 + G], F32)
                E.lo0 = sb2("lo0", [P, E.NT0 + G], F32)
                phase_setup(nc, E, a, sb, None, sem, top)
                phase_sort_dst(nc, E, sem)
            with ExitStack() as st:
                sb2 = stack(st)
                E.kvtab = sb2("kvtab", [B, E.NB, 2 * B], F32)
                E.W1 = sb2("W1", [B, P], F32)
                E.W2 = sb2("W2", [P, P], F32)
                E.b1 = sb2("b1", [P, 1], F32)
                E.b2 = sb2("b2", [1, P], F32)
                phase_nodes0(nc, E, a, sem)
                phase_sort_src(nc, E, sem)
            with ExitStack() as st:
                sb2 = stack(st)
                E.lg0 = sb2("lg0", [P, E.NT, 4], F32)
                E.loS = sb2("loS0", [P, E.NT + G], F32)
                E.keyS = sb2("keyS0", [P, E.NT + G], F32)
                phase_logits0(nc, E, sem)
                phase_softmax(nc, E, sem, "m0_", E.lg0, E.keyS, 4)
                phase_sum0(nc, E, sem)
            phase_nodes1(nc, E, a, sem)
        nc.clear_and_free_semaphores(taken)
        nc.all_engine_barrier()
        with ExitStack() as second:
            sb1 = stack(second)
            E.acc1 = sb1("acc1", [P, 5, E.NB * B], F32)
            with ExitStack() as st:
                E.lg1 = stack(st)("lg1", [P, E.NT + G, 8], F32)
                phase_gather1(nc, E, sem)
                phase_softmax(nc, E, sem, "m1_", E.lg1, E.keyD, 8)
                phase_sum1(nc, E, sem)
            phase_dense1(nc, E, a, out, sem)


_OUTS = [((3125, 64), 'float32')]


def kernel(**inputs):
    import numpy as _np
    import concourse.bacc as _bacc
    from concourse import mybir as _mybir
    from concourse.bass_utils import run_bass_kernel_spmd as _run

    nc = _bacc.Bacc("TRN2", target_bir_lowering=False, num_devices=1)
    arrays, aps = {}, {}
    for name in inputs:
        a = _np.ascontiguousarray(inputs[name])
        arrays[f"in_{name}"] = a
        aps[name] = nc.dram_tensor(f"in_{name}", a.shape, _mybir.dt.from_np(a.dtype), kind="ExternalInput").ap()
    shape, dtype = _OUTS[0]
    out = nc.dram_tensor("out_0", shape, _mybir.dt.from_np(_np.dtype(dtype)), kind="ExternalOutput").ap()
    build(nc, aps, out)
    r = _run(nc, [arrays], core_ids=[0])
    return r.results[0]["out_0"]
```

```python
from contextlib import ExitStack

import numpy as np
import concourse.bass as bass
from concourse import mybir

F32 = mybir.dt.float32
BF16 = mybir.dt.bfloat16
BF16 = mybir.dt.bfloat16
I32 = mybir.dt.int32
ALU = mybir.AluOpType
ACT = mybir.ActivationFunctionType
AXX = mybir.AxisListType.X
PE = mybir.EngineType.PE
DVE = mybir.EngineType.DVE

P = 128
B = 64
G = 4
BIG = 3.0e38


def bc(ap, shape):
    return ap.to_broadcast(shape)


class Link:

    def __init__(self, eng, sem):
        self.eng, self.sem, self.base, self.n = eng, sem, 0, 0

    def __call__(self, ins):
        self.n += 1
        ins.then_inc(self.sem, 1)
        self.eng.wait_ge(self.sem, self.base + self.n)

    def loop(self, start, it, per):
        self.base, self.n = it * per + start, 0


def upto(it, par, k=1):
    return it * (2 * k) + k * (par + 1)


def tiles(it, par):
    return bass.ds(it * (2 * G) + par * G, G)


class Env:
    pass


def blocks_of(nc, engine, blk, it, NB, groups=2):
    _, v = nc.values_load_multi_w_load_instructions(
        blk[0:1, bass.ds(it * (groups * G), groups * G)], engines=[engine], min_val=0, max_val=NB - 1,
        skip_runtime_bounds_check_because="base_vector cuts them off at the last block")
    return v


BANK = 512


def banks(nc, st, name, shape):
    size = int(np.prod(shape[1:]))
    full = -(-size // BANK) * BANK
    t = st.enter_context(nc.psum_tensor(name, [P, full], F32))
    v = t[0:shape[0], 0:size]
    if len(shape) == 3:
        v = v.rearrange("p (a b) -> p a b", a=shape[1])
    return v


def masks(nc, E, sb, s_mask):
    E.ones = sb("ones", [P, P], F32)
    E.ident = sb("ident", [P, P], F32)
    E.identb = sb("identb", [P, P], BF16)
    E.after = sb("after", [P, P], F32)
    E.iota_i = sb("iota_i", [P, E.NT], I32)
    E.iota = sb("iota", [P, E.NT], F32)


def masks_pool(nc, pool, E, s_ones, s_mask):
    nc.gpsimd.memset(E.ones[:, :], 1.0).then_inc(s_ones, 1)
    pool.wait_ge(s_ones, 1)
    for out, cmp, way in ((E.ident, ALU.is_equal, 1), (E.after, ALU.is_gt, -1)):
        nc.gpsimd.affine_select(out=out[:, :], in_=E.ones[:, :], pattern=[[-way, P]], compare_op=cmp, fill=0.0,
                                base=0, channel_multiplier=way)
    nc.gpsimd.iota(E.iota_i[:, :], pattern=[[1, E.NT]], base=0, channel_multiplier=0).then_inc(s_mask, 1)


class Rank:

    def __init__(self, nc, sb, ps, sem, n):
        self.oh = sb(n + "_oh", [P, 2, 2, G, B], BF16)
        self.ohT = sb(n + "_ohT", [B, 2, G, P], BF16)
        self.Hb = sb(n + "_Hb", [B, 2, G, B], BF16)
        self.T = sb(n + "_T", [B, 2, 2, B], BF16)
        self.M = sb(n + "_M", [P, G, P], BF16)
        self.zero = sb(n + "_zero", [1, G * B], BF16)
        self.tmp = sb(n + "_tmp", [P, G, B], F32)
        self.posf = sb(n + "_posf", [P, G], F32)
        self.posi = sb(n + "_posi", [P, 3, G], I32)
        self.row = sb(n + "_row", [P, 2, G], I32)
        self.psH = ps(n + "_psH", [B, G, B], F32)
        self.psT = ps(n + "_psT", [B, B], F32)
        self.psHT = ps(n + "_psHT", [B, G, P], F32)
        self.psE = ps(n + "_psE", [P, G, P], F32)
        self.psL = ps(n + "_psL", [P, G, B], F32)
        self.oh_ready = sem(n + "_oh_ready")
        self.hist_ready = sem(n + "_hist_ready")
        self.T_ready = sem(n + "_T_ready")
        self.hT_ready = sem(n + "_hT_ready")
        self.ohT_ready = sem(n + "_ohT_ready")
        self.same_ready = sem(n + "_same_ready")
        self.M_ready = sem(n + "_M_ready")
        self.look_ready = sem(n + "_look_ready")
        self.before_ready = sem(n + "_before_ready")
        self.look_free = sem(n + "_look_free")
        self.row_ready = sem(n + "_row_ready")
        self.taken = sem(n + "_taken")


def onehot(nc, E, out, part, tile0, n=B):
    return nc.vector.tensor_tensor(out, bc(E.iota[:, None, 0:n], [P, G, n]),
                                   bc(part[:, bass.ds(tile0, G)][:, :, None], [P, G, n]), ALU.is_equal)


def rank_onehots_hi(nc, E, R, keys, tile0, par):
    onehot(nc, E, R.oh[:, par, 0], keys[0], tile0)


def rank_zero(nc, R, link):
    link(nc.vector.memset(R.zero[:, :], 0.0))


def rank_onehots_lo(nc, E, R, keys, tile0, par):
    onehot(nc, E, R.oh[:, par, 1], keys[1], tile0).then_inc(R.oh_ready, 1)


def rank_tensor_hist(nc, pe, E, R, par):
    I = E.identb[0:B, 0:B]
    pe.sem_inc(R.taken, 1)
    for k in (0, 1):
        nc.tensor.matmul(R.psT[:, :], I, R.T[:, par, k], start=(k == 0), stop=False)
    for j in range(G):
        nc.tensor.matmul(R.psH[:, j, :], R.oh[:, par, 0, j, :], R.oh[:, par, 1, j, :], start=True, stop=True)
        last = nc.tensor.matmul(R.psT[:, :], R.oh[:, par, 0, j, :], R.oh[:, par, 1, j, :], start=False, stop=(j == G - 1))
    last.then_inc(R.hist_ready, 1)
    for j in range(G):
        last = nc.tensor.matmul(R.psHT[:, j, :], R.oh[:, par, 0, j, :], E.identb[:, :], start=True, stop=True)
    last.then_inc(R.hT_ready, 1)


def rank_tensor_same(nc, pe, R, it, par):
    g1 = upto(it, par)
    pe.wait_ge(R.ohT_ready, g1)
    pe.wait_ge(R.M_ready, g1)
    for j in range(G):
        last = nc.tensor.matmul(R.psE[:, j, :], R.ohT[:, par, j, :], R.ohT[:, par, j, :], start=True, stop=True)
    last.then_inc(R.same_ready, 1)


def rank_tensor_next(nc, pe, E, R, it, par):
    g1 = upto(it, par)
    pe.wait_ge(R.oh_ready, g1 + 1)
    pe.wait_ge(R.T_ready, g1 + 1)
    rank_tensor_hist(nc, pe, E, R, 1 - par)


def rank_tensor_look(nc, pe, R, it, par):
    pe.wait_ge(R.look_free, upto(it, par))
    nc.tensor.matmul(R.psL[:, :, :], R.zero[0:1, 0:P], R.zero[0:1, :], start=True, stop=False)
    for j in range(G):
        nc.tensor.matmul(R.psL[:, j, :], R.ohT[:, par, j, :], R.T[:, par, 0, :], start=False, stop=False)
        last = nc.tensor.matmul(R.psL[:, j, :], R.ohT[:, par, j, :], R.T[:, par, 1, :], start=False, stop=False)
        for i in range(j):
            last = nc.tensor.matmul(R.psL[:, j, :], R.ohT[:, par, j, :], R.Hb[:, par, i, :], start=False, stop=False)
    last.then_inc(R.before_ready, 1)


def rank_tensor_look_tile(nc, pe, R, it, par):
    pe.wait_ge(R.M_ready, upto(it, par) + 1)
    for j in range(G):
        last = nc.tensor.matmul(R.psL[:, j, :], R.M[:, j, :], R.oh[:, par, 1, j, :], start=False,
                                stop=(j == G - 1))
    last.then_inc(R.look_ready, 1)


def rank_scalar(nc, act, R, it, par):
    g1 = upto(it, par)
    act.wait_ge(R.hist_ready, g1)
    act.wait_ge(R.look_ready, g1)
    nc.scalar.activation(R.Hb[:, par], R.psH[:, :, :], ACT.Copy)
    act.wait_ge(R.hT_ready, g1)
    nc.scalar.activation(R.ohT[:, par], R.psHT[:, :, :], ACT.Copy).then_inc(R.ohT_ready, 1)


def rank_positions(nc, link, R, par, pos):
    link(nc.vector.tensor_copy(R.T[:, par, 0], pos))
    nc.vector.tensor_tensor(R.T[:, par, 1], pos, R.T[:, par, 0], ALU.subtract).then_inc(R.T_ready, 1)


def rank_vector_next(nc, dve, R, link, it, par):
    dve.wait_ge(R.hist_ready, upto(it, par) + 1)
    dve.wait_ge(R.before_ready, upto(it, par))
    rank_positions(nc, link, R, par, R.psT[:, :])


def rank_vector_same(nc, dve, E, R, it, par):
    dve.wait_ge(R.same_ready, upto(it, par))
    nc.vector.tensor_tensor(R.M[:, :, :], R.psE[:, :, :], bc(E.after[:, None, :], [P, G, P]),
                            ALU.mult).then_inc(R.M_ready, 1)


RANK_LINKS = 1 + 4


def rank_rows(nc, dve, E, R, keys, link, it, par, NT, scattered, padoff=None):
    g1 = upto(it, par)
    dve.wait_ge(R.look_ready, g1 + 2)
    nc.vector.tensor_tensor(R.tmp[:, :, :], R.psL[:, :, :], R.oh[:, par, 1], ALU.mult).then_inc(R.look_free, 1)
    dve.wait_ge(R.look_free, g1 + 1)
    rank_onehots_lo(nc, E, R, keys, it * (2 * G) + (par + 2) * G, par)
    link(nc.vector.tensor_reduce(R.posf[:, :], R.tmp[:, :, :], AXX, ALU.add))
    if padoff is not None:
        link(nc.vector.tensor_tensor(R.posi[:, 0], R.posf[:, :], padoff[:, tiles(it, par)], ALU.add))
    else:
        link(nc.vector.tensor_copy(R.posi[:, 0], R.posf[:, :]))
    link(nc.vector.tensor_scalar(R.posi[:, 1], R.posi[:, 0], 127, None, ALU.bitwise_and))
    link(nc.vector.tensor_scalar(R.posi[:, 2], R.posi[:, 0], 7, None, ALU.arith_shift_right))
    dve.wait_ge(scattered[par], 64 * it + 64)
    nc.vector.scalar_tensor_tensor(R.row[:, par], R.posi[:, 1], float(NT), R.posi[:, 2],
                                   ALU.mult, ALU.add).then_inc(R.row_ready, 1)


def split_keys(nc, link, keyf, keyi, hi, lo, ti):
    link(nc.vector.tensor_copy(keyf, keyi))
    link(nc.vector.tensor_scalar(ti, keyi, 6, None, ALU.arith_shift_right))
    link(nc.vector.tensor_copy(hi, ti))
    link(nc.vector.tensor_scalar(ti, keyi, B - 1, None, ALU.bitwise_and))
    link(nc.vector.tensor_copy(lo, ti))


def histogram_vector(nc, dve, E, H, hi, lo):
    def group(it, par):
        dve.wait_ge(H.counted, upto(it, par))
        for k, part in enumerate((hi, lo)):
            last = nc.vector.tensor_tensor(H.oh[:, par, k], bc(E.iota[:, None, 0:B], [P, G, B]),
                                           bc(part[:, tiles(it, par)][:, :, None], [P, G, B]), ALU.is_equal)
        last.then_inc(H.oh_ready, 1)
    with dve.Fori(0, H.n // (2 * G)) as it:
        for par in (0, 1):
            group(it, par)


def histogram_tensor(nc, pe, E, H):
    nc.tensor.matmul(H.ps[:, :], H.zero[:, 0:B], H.zero[:, 0:B], start=True, stop=False)
    with pe.Fori(0, H.n // (2 * G)) as it:
        for par in (0, 1):
            pe.wait_ge(H.oh_ready, upto(it, par))
            for j in range(G):
                last = nc.tensor.matmul(H.ps[:, :], H.oh[:, par, 0, j], H.oh[:, par, 1, j], start=False, stop=False)
            last.then_inc(H.counted, 1)
    nc.tensor.matmul(H.ps[:, :], H.zero[:, 0:B], H.zero[:, 0:B], start=False, stop=True).then_inc(H.done, 1)


class Hist:
    def __init__(self, nc, sb, ps, sem, n, tiles_n):
        self.n = tiles_n
        self.oh = sb(n + "_hoh", [P, 2, 2, G, B], BF16)
        self.zero = sb(n + "_hzero", [P, B], BF16)
        self.c = sb(n + "_hc", [B, 4, B], F32)
        self.i = sb(n + "_hi", [B, 2], I32)
        self.nt = sb(n + "_hnt", [B, 4], F32)
        self.M = sb(n + "_hM", [B, 512], F32)
        self.ps = ps(n + "_hps", [B, B], F32)
        self.psb = ps(n + "_hpsb", [B, 512], F32)
        self.oh_ready = sem(n + "_hoh_ready")
        self.counted = sem(n + "_hcounted")
        self.done = sem(n + "_hdone")
        self.s_nt = sem(n + "_hs_nt")
        self.s_first = sem(n + "_hs_first")
        self.s_M = sem(n + "_hs_M")
        self.s_blk = sem(n + "_hs_blk")


def base_vector(nc, dve, E, H, link, T0, blk):
    dve.wait_ge(H.done, 1)
    link(nc.vector.tensor_copy(H.c[:, 0], H.ps[:, :]))
    link(nc.vector.tensor_tensor_scan(H.c[:, 1], E.ones[0:B, 0:B], H.c[:, 0], 0.0, ALU.mult, ALU.add))
    link(nc.vector.tensor_scalar(H.nt[:, 0:1], H.c[:, 1, B - 1:B], float(P - 1), None, ALU.add))
    link(nc.vector.tensor_copy(H.i[:, 0:1], H.nt[:, 0:1]))
    link(nc.vector.tensor_scalar(H.i[:, 1:2], H.i[:, 0:1], 7, None, ALU.arith_shift_right))
    nc.vector.tensor_copy(H.nt[:, 1:2], H.i[:, 1:2]).then_inc(H.s_nt, 1)
    dve.wait_ge(H.s_first, 1)
    link(nc.vector.tensor_tensor(H.nt[:, 2:3], H.psb[:, 0:1], H.nt[:, 1:2], ALU.add))
    link(nc.vector.tensor_scalar(H.nt[:, 3:4], H.psb[:, 0:1], float(P), None, ALU.mult))
    link(nc.vector.tensor_tensor(H.c[:, 2], H.c[:, 1], H.c[:, 0], ALU.subtract))
    link(nc.vector.tensor_scalar(T0, H.c[:, 2], H.nt[:, 3:4], None, ALU.add))
    nc.vector.tensor_scalar(H.M[:, 0:E.NT], E.iota[0:B, :], H.nt[:, 2:3], None, ALU.is_ge).then_inc(H.s_M, 1)
    dve.wait_ge(H.s_blk, 1)
    link(nc.vector.tensor_scalar(blk, H.psb[0:1, 0:E.NT], float(E.NB - 1), None, ALU.min))


def base_tensor(nc, pe, E, H):
    pe.wait_ge(H.s_nt, 1)
    nc.tensor.matmul(H.psb[:, 0:1], E.after[0:B, 0:B], H.nt[:, 1:2], start=True, stop=True).then_inc(H.s_first, 1)
    pe.wait_ge(H.s_M, 1)
    nc.tensor.matmul(H.psb[0:1, 0:E.NT], E.ones[0:B, 0:1], H.M[:, 0:E.NT], start=True, stop=True).then_inc(H.s_blk, 1)


NC = 7


def load_nodes(sp, dst, x, N, sem):
    full = N // B
    sp.dma_start(dst[:, 0:full], x[0:full * B].rearrange("(b p) c -> p b c", p=B)).then_inc(sem, 16)
    sp.dma_start(dst[0:N - full * B, full:full + 1],
                 x[full * B:N].rearrange("(b p) c -> p b c", b=1)).then_inc(sem, 16)


def layernorm(nc, dve, act, link, x, s, sq, s_var, s_sd, n):
    D = x.shape[-1]
    mean, r = s[:, 0], s[:, 1]
    sh = list(x.shape)
    link(nc.vector.tensor_reduce(mean, x, AXX, ALU.add))
    link(nc.vector.tensor_scalar(mean, mean, 1.0 / D, None, ALU.mult))
    link(nc.vector.tensor_tensor(x, x, bc(mean[:, :, None], sh), ALU.subtract))
    link(nc.vector.tensor_tensor(sq, x, x, ALU.mult))
    link(nc.vector.tensor_reduce(r, sq, AXX, ALU.add))
    nc.vector.tensor_scalar(r, r, 1.0 / D, 1e-5, ALU.mult, ALU.add).then_inc(s_var, 1)
    dve.wait_ge(s_sd, n)
    link(nc.vector.reciprocal(r, r))
    link(nc.vector.tensor_tensor(x, x, bc(r[:, :, None], sh), ALU.mult))


def phase_nodes0(nc, E, a, sem):
    N, NB = E.N, E.NB
    CW = NC * B
    with ExitStack() as st:
        def tmp(name, shape, dt):
            return st.enter_context(nc.sbuf_tensor(name, shape, dt))

        def pst(name, shape, dt):
            return banks(nc, st, name, shape)

        x = tmp("n0_x", [B, NB, B], F32)
        sq = tmp("n0_sq", [B, NB, B], F32)
        s = tmp("n0_s", [B, 2, NB], F32)
        hs = tmp("n0_hs", [B, NC, B], F32)
        hTs = tmp("n0_hTs", [B, CW], F32)
        bd = tmp("n0_bd", [B, 4, B], F32)
        M = tmp("n0_M", [B, 68], F32)
        WKV = tmp("n0_WKV", [B, 2 * B], F32)
        WQ = tmp("n0_WQ", [B, 68], F32)
        psW = pst("n0_psW", [B, 4, B], F32)
        psT = pst("n0_psT", [B, CW], F32)
        psKV = pst("n0_psKV", [B, 8, 2 * B], F32)
        psQ = pst("n0_psQ", [B, NC, 68], F32)
        s_in, s_x, s_zero, s_link, s_var, s_sd, s_w, s_wc, s_M, s_q = (
            sem("n0_" + n) for n in ("in", "x", "zero", "link", "var", "sd", "w", "wc", "M", "q"))
        s_h, s_hs, s_T, s_Tc, s_tab, s_out, s_outa = (
            sem("n0_" + n) for n in ("h", "hs", "T", "Tc", "tab", "out", "outa"))
        s_taken = sem("n0_taken")
        H, D = 4, 16
        with nc.Block() as block:
            @block.sync
            def _(sp):
                sp.wait_ge(s_zero, 1)
                load_nodes(sp, x, a["x"], N, s_x)
                for h in range(H):
                    hd = slice(h * D, h * D + D)
                    for k, w in enumerate(("L0_gnn_Wk", "L0_gnn_Wv", "L0_gnn_Wq")):
                        sp.dma_start(bd[hd, k, hd], a[w][h]).then_inc(s_in, 16)
                    sp.dma_start(bd[hd, 3, hd], a["L0_gnn_wkl_w"]).then_inc(s_in, 16)
                    sp.dma_start(M[hd, B + h:B + h + 1], a["L0_gnn_wkl_b"].rearrange("(p c) -> p c", c=1)).then_inc(s_in, 16)
                    sp.dma_start(E.wvl[hd, hd], a["L0_gnn_wvl_w"]).then_inc(s_in, 16)
                sp.wait_ge(s_in, 16 * (6 * H))
                sp.wait_ge(s_x, 32)

            @block.vector
            def _(dve):
                link = Link(dve, s_link)
                for t in (E.wvl, M):
                    nc.vector.memset(t[:, :], 0.0)
                nc.vector.memset(x[:, NB - 1], 0.0)
                nc.vector.memset(bd[:, :, :], 0.0).then_inc(s_zero, 1)
                dve.wait_ge(s_x, 32)
                layernorm(nc, dve, None, link, x[:, :, :], s, sq[:, :, :], s_var, s_sd, 1)
                nc.vector.tensor_scalar(x[:, :, :], x[:, :, :], 0.0, None, ALU.max).then_inc(s_h, 1)
                dve.wait_ge(s_w, 1)
                nc.vector.tensor_copy(WKV[:, 0:2 * B], psW[:, 0:2].rearrange("p k c -> p (k c)"))
                nc.vector.tensor_copy(M[:, 0:B], psW[:, 2]).then_inc(s_wc, 1)
                dve.wait_ge(s_q, 1)
                nc.vector.tensor_scalar(WQ[:, :], psQ[:, 0, :], 0.25, None, ALU.mult).then_inc(s_M, 1)
                dve.sem_inc(s_out, 1)
                with dve.Fori(0, NB // NC) as c:
                    dve.wait_ge(s_T, c + 1)
                    nc.vector.tensor_copy(hTs[:, :], psT[:, :]).then_inc(s_Tc, 1)
                    dve.wait_ge(s_tab, c + 1)
                    nc.vector.tensor_copy(E.kvtab[:, bass.ds(c * NC, NC), :], psKV[:, 0:NC, :]).then_inc(s_out, 1)

            @block.scalar
            def _(act):
                act.wait_ge(s_var, 1)
                nc.scalar.activation(s[:, 1], s[:, 1], ACT.Sqrt).then_inc(s_sd, 1)
                act.wait_ge(s_h, 1)
                act.sem_inc(s_outa, 1)
                with act.Fori(0, NB // NC) as c:
                    nc.scalar.activation(hs[:, :, :], x[:, bass.ds(c * NC, NC), :], ACT.Copy).then_inc(s_hs, 1)
                    act.wait_ge(s_Tc, c + 1)
                    nc.scalar.activation(E.h0T[:, bass.ds(c * CW, CW)], hTs[:, :], ACT.Copy)
                    act.wait_ge(s_tab, c + 1)
                    nc.scalar.activation(E.qtab[:, bass.ds(c * NC, NC), :], psQ[:, :, :], ACT.Copy).then_inc(s_outa, 1)

            @block.tensor
            def _(pe):
                pe.wait_ge(s_in, 16 * (6 * H))
                I = E.ident[0:B, 0:B]
                for k, w in enumerate((0, 1, 3)):
                    last = nc.tensor.matmul(psW[:, k], bd[:, w], I, start=True, stop=True)
                last.then_inc(s_w, 1)
                pe.wait_ge(s_wc, 1)
                nc.tensor.matmul(psQ[:, 0, :], bd[:, 2], M[:, :], start=True, stop=True).then_inc(s_q, 1)
                pe.wait_ge(s_M, 1)
                with pe.Fori(0, NB // NC) as c:
                    pe.wait_ge(s_hs, c + 1)
                    pe.sem_inc(s_taken, 1)
                    for j in range(NC):
                        last = nc.tensor.matmul(psT[:, j * B:j * B + B], hs[:, j], I, start=True, stop=True)
                    last.then_inc(s_T, 1)
                    pe.wait_ge(s_Tc, c + 1)
                    pe.wait_ge(s_out, c + 1)
                    pe.wait_ge(s_outa, c + 1)
                    pe.sem_inc(s_taken, 1)
                    for j in range(NC):
                        lhs = hTs[:, j * B:j * B + B]
                        nc.tensor.matmul(psKV[:, j, :], lhs, WKV[:, :], start=True, stop=True)
                        last = nc.tensor.matmul(psQ[:, j, :], lhs, WQ[:, :], start=True, stop=True)
                    last.then_inc(s_tab, 1)


def phase_sort_src(nc, E, sem):
    NT, EF = E.NT, E.EF
    with ExitStack() as st:
        def tmp(name, shape, dt):
            return st.enter_context(nc.sbuf_tensor(name, shape, dt))

        def pst(name, shape, dt):
            return banks(nc, st, name, shape)

        sd = tmp("sd", [P, NT, E.RD], F32)
        KL = tmp("KL", [P, 2, NT + 2 * G], F32)
        hiS = tmp("hiS", [P, NT + 2 * G], F32)
        keyS, loS = KL[:, 0], KL[:, 1]
        pad = tmp("pad", [P, NT], F32)
        n = NT // (2 * G)
        with ExitStack() as st2:
            ki = st2.enter_context(nc.sbuf_tensor("ki", [P, NT], I32))
            ti = st2.enter_context(nc.sbuf_tensor("tiS", [P, NT], I32))
            s_sd, s_link = sem("s_sd"), sem("s_linkHS")
            with nc.Block() as block:
                @block.sync
                def _(sp):
                    sp.dma_start(sd[:, :, :], E.sd.rearrange("p (t f) -> p t f", f=E.RD)).then_inc(s_sd, 16)
                    sp.wait_ge(s_sd, 16)

                @block.vector
                def _(dve):
                    link = Link(dve, s_link)
                    link(nc.vector.memset(keyS[:, NT:], -1.0))
                    link(nc.vector.memset(hiS[:, NT:], -1.0))
                    link(nc.vector.memset(loS[:, NT:], -1.0))
                    link(nc.vector.memset(E.loD[:, NT:], -1.0))
                    link(nc.vector.memset(E.srcI[:, NT:], 0))
                    dve.wait_ge(s_sd, 16)
                    link(nc.vector.tensor_copy(ki[:, :], sd[:, :, 1]))
                    split_keys(nc, link, E.keyD[:, :], ki[:, :], hiS[:, 0:NT], E.loD[:, 0:NT], ti[:, :])
                    link(nc.vector.tensor_scalar(pad[:, :], E.keyD[:, :], 0.0, 8388608.0, ALU.is_lt, ALU.mult))
                    link(nc.vector.tensor_tensor(E.loD[:, 0:NT], E.loD[:, 0:NT], pad[:, :], ALU.max))
                    link(nc.vector.tensor_copy(ki[:, :], sd[:, :, 0]))
                    split_keys(nc, link, keyS[:, 0:NT], ki[:, :], hiS[:, 0:NT], loS[:, 0:NT], ti[:, :])
                    link(nc.vector.tensor_scalar(E.srcI[:, 0:NT], keyS[:, 0:NT], 0.0, None, ALU.max))

        R = Rank(nc, tmp, pst, sem, "RS")
        ohD = tmp("ohD", [P, 2, G, B], BF16)
        ohDT = tmp("ohDT", [B, 2, G, P], F32)
        pay = tmp("payS", [P, 2, G, E.RS], F32)
        psDT = pst("psDT", [B, G, P], F32)
        psKV = pst("psKV", [P, G, 2 * B], F32)
        s_DT, s_ohDT, s_kv, s_pay, s_link, s_taken, s_taken2, s_key = (
            sem("es_" + k) for k in ("DT", "ohDT", "kv", "pay", "link", "taken", "taken2", "key"))
        keys = (hiS, loS)

        def dst_transposed(par):
            for j in range(G):
                last = nc.tensor.matmul(psDT[:, j], ohD[:, par, j], E.identb[:, :], start=True, stop=True)
            last.then_inc(s_DT, 1)

        with nc.Block() as block:
            @block.tensor
            def _(pe):
                pe.sem_inc(R.look_ready, 2)
                pe.wait_ge(R.oh_ready, 1)
                pe.wait_ge(R.T_ready, 1)
                rank_tensor_hist(nc, pe, E, R, 0)
                dst_transposed(0)
                with pe.Fori(0, n) as it:
                    blocks = blocks_of(nc, PE, E.blkD, it, E.NB)
                    for par in (0, 1):
                        g1 = upto(it, par)
                        rank_tensor_same(nc, pe, R, it, par)
                        rank_tensor_look(nc, pe, R, it, par)
                        rank_tensor_next(nc, pe, E, R, it, par)
                        pe.wait_ge(s_ohDT, g1)
                        dst_transposed(1 - par)
                        pe.wait_ge(s_pay, g1)
                        pe.sem_inc(s_taken, 1)
                        for j in range(G):
                            b = blocks[par * G + j]
                            last = nc.tensor.matmul(psKV[:, j], ohDT[:, par, j], E.kvtab[:, bass.ds(b, 1), :],
                                                    start=True, stop=True)
                        last.then_inc(s_kv, 1)
                        rank_tensor_look_tile(nc, pe, R, it, par)

            @block.scalar
            def _(act):
                with act.Fori(0, n) as it:
                    for par in (0, 1):
                        g1 = upto(it, par)
                        rank_scalar(nc, act, R, it, par)
                        act.wait_ge(s_DT, g1)
                        nc.scalar.activation(ohDT[:, par], psDT[:, :, :], ACT.Copy).then_inc(s_ohDT, 1)
                        act.wait_ge(E.scatS[par], 64 * it + 64)
                        nc.scalar.activation(pay[:, par, :, 2 * B:],
                                             KL[:, :, tiles(it, par)].rearrange("p k t -> p t k"), ACT.Copy).then_inc(s_key, 1)

            @block.vector
            def _(dve):
                link = Link(dve, s_link)
                dve.sem_inc(R.M_ready, 1)
                dve.sem_inc(R.look_free, 1)
                dve.sem_inc(s_pay, 1)

                def onehots(tile0, par):
                    onehot(nc, E, ohD[:, par], E.loD, tile0)
                    rank_onehots_hi(nc, E, R, keys, tile0, par)

                rank_zero(nc, R, link)
                onehots(0, 0)
                rank_onehots_lo(nc, E, R, keys, 0, 0)
                rank_positions(nc, link, R, 0, E.T0S[:, :])
                onehots(G, 1)
                rank_onehots_lo(nc, E, R, keys, G, 1)
                dve.wait_ge(R.hist_ready, 1)
                rank_positions(nc, link, R, 1, R.psT[:, :])
                with dve.Fori(0, n) as it:
                    link.loop(3, it, 2 * RANK_LINKS)
                    for par in (0, 1):
                        g1 = upto(it, par)
                        rank_vector_same(nc, dve, E, R, it, par)
                        onehots(it * (2 * G) + (par + 2) * G, par)
                        rank_vector_next(nc, dve, R, link, it, par)
                        dve.wait_ge(E.scatS[par], 64 * it + 64)
                        dve.wait_ge(s_kv, g1)
                        for k in (0, 1):
                            w = sd[:, tiles(it, par), 2 + k * EF:2 + (k + 1) * EF]
                            last = nc.vector.tensor_tensor(
                                pay[:, par, :, k * B:(k + 1) * B].rearrange("p t (h j) -> p t h j", h=4),
                                psKV[:, :, k * B:(k + 1) * B].rearrange("p t (h j) -> p t h j", h=4),
                                bc(w[:, :, None, :], [P, G, 4, EF]), ALU.mult)
                        last.then_inc(s_pay, 1)
                        rank_rows(nc, dve, E, R, keys, link, it, par, NT, E.scatS, pad)
                    assert link.n == 2 * RANK_LINKS, link.n

            @block.gpsimd
            def _(pool):
                limit = pool.to_reg(P * NT - 1)
                with pool.Fori(0, n) as it:
                    for par in (0, 1):
                        pool.wait_ge(R.row_ready, upto(it, par))
                        pool.wait_ge(s_pay, upto(it, par) + 1)
                        pool.wait_ge(s_key, upto(it, par))
                        pool.sem_inc(s_taken2, 1)
                        for j in range(G):
                            nc.gpsimd.indirect_dma_start(
                                out=E.ss_rows, out_offset=bass.IndirectOffsetOnAxis(ap=R.row[:, par, j:j + 1], axis=0),
                                in_=pay[:, par, j, :], in_offset=None,
                                bounds_check=limit, oob_is_err=False).then_inc(E.scatS[par], 16)
                for par in (0, 1):
                    pool.wait_ge(E.scatS[par], 64 * n + 64)


U = 4
FAR = 1.0e30


def phase_logits0(nc, E, sem):
    NT, RS, H = E.NT, E.RS, 4
    with ExitStack() as st:
        def tmp(name, shape, dt):
            return st.enter_context(nc.sbuf_tensor(name, shape, dt))

        def pst(name, shape):
            return banks(nc, st, name, shape)

        rows = tmp("l0_rows", [P, U, G, RS], F32)
        oh = tmp("l0_oh", [P, 2, G, B], BF16)
        ohT = tmp("l0_ohT", [B, 2, G, P], F32)
        prod = tmp("l0_prod", [P, G, B], F32)
        dot = tmp("l0_dot", [P, G, H], F32)
        psT = pst("l0_psT", [B, G, P])
        psQ = [pst(f"l0_psQ{k}", [P, G, B + H]) for k in (0, 1)]
        s_in = [sem(f"l0_in{u}") for u in range(U)]
        s_used, s_keys, s_oh, s_T, s_ohT, s_q, s_link, s_taken = (
            sem("l0_" + k) for k in ("used", "keys", "oh", "T", "ohT", "q", "link", "taken"))
        n = NT // (U * G)
        assert NT % (U * G) == 0
        ss = E.ss.rearrange("p (t f) -> p t f", f=RS)

        def group(it, u):
            return bass.ds(it * (U * G) + u * G, G)

        with nc.Block() as block:
            @block.sync
            def _(sp):
                with sp.Fori(0, n) as it:
                    for u in range(U):
                        sp.wait_ge(s_used, it * U + u + 1)
                        sp.wait_ge(s_keys, it * U + u + 1)
                        sp.dma_start(rows[:, u], ss[:, group(it, u), :]).then_inc(s_in[u], 16)
                sp.wait_ge(s_used, U * (n - 1) + 1 + U)
                sp.wait_ge(s_keys, U * (n - 1) + 1 + U)
                sp.dma_start(rows[:, 0], ss[:, 0:G, :]).then_inc(s_in[0], 16)
                sp.wait_ge(s_used, U * (n - 1) + 2 + U)
                sp.wait_ge(s_keys, U * (n - 1) + 2 + U)
                sp.dma_start(rows[:, 1], ss[:, G:2 * G, :]).then_inc(s_in[1], 16)
                for u in range(U):
                    sp.wait_ge(s_in[u], 16 * n + 16 * (u < 2))

            @block.tensor
            def _(pe):
                def transposed(par):
                    for j in range(G):
                        last = nc.tensor.matmul(psT[:, j], oh[:, par, j], E.identb[:, :], start=True, stop=True)
                    last.then_inc(s_T, 1)

                pe.sem_inc(s_q, 2)
                pe.wait_ge(s_oh, 1)
                transposed(0)
                with pe.Fori(0, n) as it:
                    blocks = blocks_of(nc, PE, E.blkS, it, E.NB, U)
                    for u in range(U):
                        par, g1 = u % 2, it * U + u + 1
                        pe.wait_ge(s_oh, g1 + 1)
                        pe.wait_ge(s_ohT, g1)
                        transposed(1 - par)
                        pe.wait_ge(s_used, g1 + U - 2)
                        pe.sem_inc(s_taken, 1)
                        for j in range(G):
                            b = blocks[u * G + j]
                            last = nc.tensor.matmul(psQ[par][:, j], ohT[:, par, j], E.qtab[:, bass.ds(b, 1), :],
                                                    start=True, stop=True)
                        last.then_inc(s_q, 1)

            @block.scalar
            def _(act):
                act.sem_inc(s_keys, U)
                with act.Fori(0, n) as it:
                    for u in range(U):
                        par, g1 = u % 2, it * U + u + 1
                        act.wait_ge(s_T, g1)
                        act.wait_ge(s_q, g1)
                        nc.scalar.activation(ohT[:, par], psT[:, :, :], ACT.Copy).then_inc(s_ohT, 1)
                        act.wait_ge(s_in[u], 16 * it + 16)
                        nc.scalar.activation(E.keyS[:, group(it, u)], rows[:, u, :, 2 * B], ACT.Copy)
                        nc.scalar.activation(E.loS[:, group(it, u)], rows[:, u, :, 2 * B + 1], ACT.Copy).then_inc(s_keys, 1)

            @block.vector
            def _(dve):
                link = Link(dve, s_link)

                def onehots(u, par):
                    nc.vector.tensor_tensor(oh[:, par], bc(E.iota[:, None, 0:B], [P, G, B]),
                                            bc(rows[:, u, :, 2 * B + 1:2 * B + 2], [P, G, B]), ALU.is_equal).then_inc(s_oh, 1)

                dve.sem_inc(s_used, U)
                nc.vector.memset(E.loS[:, NT:], -1.0)
                link(nc.vector.memset(E.lg0[:, NT:], 0.0))
                for u in (0, 1):
                    dve.wait_ge(s_in[u], 16)
                    onehots(u, u)
                with dve.Fori(0, n) as it:
                    link.loop(1, it, 3 * U)
                    for u in range(U):
                        par, g1 = u % 2, it * U + u + 1
                        dve.wait_ge(s_T, g1)
                        dve.wait_ge(s_in[(u + 2) % U], 16 * it + 16 * (1 + (u + 2) // U))
                        onehots((u + 2) % U, par)
                        dve.wait_ge(s_q, g1 + 2)
                        link(nc.vector.tensor_tensor(prod[:, :, :], rows[:, u, :, 0:B], psQ[par][:, :, 0:B], ALU.mult))
                        link(nc.vector.tensor_reduce(dot[:, :, :], prod[:, :, :].rearrange("p t (h j) -> p t h j", h=H),
                                                     AXX, ALU.add))
                        link(nc.vector.tensor_tensor(E.lg0[:, group(it, u), :], dot[:, :, :], psQ[par][:, :, B:], ALU.add))
                        dve.sem_inc(s_used, 1)
                    assert link.n == 3 * U, link.n


def phase_softmax(nc, E, sem, n, lg, key, H):
    NT = E.NT
    Q = NT // 4
    with ExitStack() as st:
        def tmp(name, shape, dt=F32):
            return st.enter_context(nc.sbuf_tensor(n + name, shape, dt))

        def pst(name, shape):
            return banks(nc, st, n + name, shape)

        X = tmp("X", [Q, 4, H, P])
        up = tmp("up", [Q, 4, H, P])
        down = tmp("down", [Q, 4, H, P])
        K = tmp("K", [Q, 4, P])
        Rup = tmp("Rup", [Q, 4, P])
        Rdown = tmp("Rdown", [Q, 4, P])
        e1 = tmp("e1", [Q, 4, H])
        e2 = tmp("e2", [Q, 4, H])
        ends = tmp("ends", [H, 4, NT])
        same = tmp("same", [H, 4, NT])
        run = tmp("run", [H, 2, NT])
        carry = tmp("carry", [H, 2, NT])
        cq = tmp("cq", [Q, 2, 4, H])
        psX = [pst("psX0", [Q, P * 4]), pst("psX1", [Q, P * 4])]
        psE = [pst(f"psE{k}", [H, NT]) for k in range(4)]
        psC = pst("psC", [Q, 2 * 4 * H])
        psMt = [pst("psMt", [P, 4 * Q])]
        s_X, s_Xc, s_link, s_ends, s_E, s_carry, s_C, s_M, s_Mt, s_sub, s_exp = (
            sem(n + k) for k in ("X", "Xc", "link", "ends", "E", "carry", "C", "M", "Mt", "sub", "exp"))
        HX = -(-H // 4)
        steps = [(c, k) for c in range(4) for k in range(HX + 1)]
        with nc.Block() as block:
            @block.tensor
            def _(pe):
                for i, (c, k) in enumerate(steps):
                    if i >= 2:
                        pe.wait_ge(s_Xc, i - 1)
                    if k < HX:
                        for h in range(4):
                            last = nc.tensor.matmul(psX[i % 2][:, h * P:(h + 1) * P], lg[:, c * Q:(c + 1) * Q, 4 * k + h],
                                                    E.ident[:, :], start=True, stop=True)
                    else:
                        last = nc.tensor.matmul(psX[i % 2][:, 0:P], key[:, c * Q:(c + 1) * Q], E.ident[:, :],
                                                start=True, stop=True)
                    last.then_inc(s_X, 1)
                pe.wait_ge(s_ends, 1)
                I = E.ident[0:Q, 0:Q]
                for c in range(4):
                    for k, src in enumerate((up[:, c, :, P - 1], down[:, c, :, 0], bc(K[:, c, 0:1], [Q, H]),
                                             bc(K[:, c, P - 1:P], [Q, H]))):
                        last = nc.tensor.matmul(psE[k][:, c * Q:(c + 1) * Q], src, I, start=True, stop=True)
                last.then_inc(s_E, 1)
                pe.wait_ge(s_carry, 1)
                for k in (0, 1):
                    for c in range(4):
                        last = nc.tensor.matmul(psC[:, (k * 4 + c) * H:(k * 4 + c + 1) * H], carry[:, k, c * Q:(c + 1) * Q],
                                                E.ident[0:H, 0:H], start=True, stop=True)
                last.then_inc(s_C, 1)
                pe.wait_ge(s_M, 1)
                for i, (c, k) in enumerate((c, k) for c in range(4) for k in range(HX)):
                    if i >= 1:
                        pe.wait_ge(s_sub, i)
                    for h in range(4):
                        last = nc.tensor.matmul(psMt[0][:, h * Q:(h + 1) * Q], up[:, c, 4 * k + h], I,
                                                start=True, stop=True)
                    last.then_inc(s_Mt, 1)

            @block.vector
            def _(dve):
                link = Link(dve, s_link)
                for i, (c, k) in enumerate(steps):
                    dve.wait_ge(s_X, i + 1)
                    if k < HX:
                        nc.vector.tensor_copy(X[:, c, 4 * k:4 * k + 4], psX[i % 2].rearrange("p (h e) -> p h e", h=4)).then_inc(s_Xc, 1)
                    else:
                        nc.vector.tensor_copy(K[:, c], psX[i % 2][:, 0:P]).then_inc(s_Xc, 1)
                dve.wait_ge(s_Xc, len(steps))
                nc.vector.memset(Rup[:, :, 0:1], 0.0)
                nc.vector.memset(Rdown[:, :, P - 1:P], 0.0)
                for c in range(4):
                    last = nc.vector.tensor_tensor(Rup[:, c, 1:P], K[:, c, 1:P], K[:, c, 0:P - 1], ALU.is_equal)
                link(last)
                link(nc.vector.tensor_scalar(Rup[:, :, 1:P], Rup[:, :, 1:P], FAR, -FAR, ALU.mult, ALU.add))
                link(nc.vector.tensor_copy(Rdown[:, :, 0:P - 1], Rup[:, :, 1:P]))
                for c in range(4):
                    for h in range(H):
                        nc.vector.tensor_tensor_scan(up[:, c, h], Rup[:, c], X[:, c, h], -FAR, ALU.add, ALU.max)
                        last = nc.vector.tensor_tensor_scan(down[:, c, h, ::-1], Rdown[:, c, ::-1], X[:, c, h, ::-1],
                                                            -FAR, ALU.add, ALU.max)
                last.then_inc(s_ends, 1)
                dve.wait_ge(s_E, 1)
                for k in range(4):
                    nc.vector.tensor_copy(ends[:, k], psE[k][:, :])
                link(nc.vector.memset(carry[:, :, :], -FAR))
                first, final = ends[:, 2], ends[:, 3]
                link(nc.vector.tensor_tensor(same[:, 0, 1:NT], first[:, 1:NT], final[:, 0:NT - 1], ALU.is_equal))
                link(nc.vector.tensor_tensor(same[:, 1], first, final, ALU.is_equal))
                link(nc.vector.memset(same[:, 2:4], -FAR))
                link(nc.vector.memset(same[:, 0, 0:1], 0.0))
                link(nc.vector.tensor_tensor(same[:, 2, 1:NT], same[:, 0, 1:NT], same[:, 1, 1:NT], ALU.mult))
                link(nc.vector.tensor_tensor(same[:, 3, 0:NT - 1], same[:, 0, 1:NT], same[:, 1, 0:NT - 1], ALU.mult))
                link(nc.vector.tensor_scalar(same[:, 0], same[:, 0], FAR, -FAR, ALU.mult, ALU.add))
                link(nc.vector.tensor_scalar(same[:, 2, 1:NT], same[:, 2, 1:NT], FAR, -FAR, ALU.mult, ALU.add))
                link(nc.vector.tensor_scalar(same[:, 3, 0:NT - 1], same[:, 3, 0:NT - 1], FAR, -FAR, ALU.mult, ALU.add))
                link(nc.vector.tensor_tensor_scan(run[:, 0], same[:, 2], ends[:, 0], -FAR, ALU.add, ALU.max))
                link(nc.vector.tensor_tensor_scan(run[:, 1, ::-1], same[:, 3, ::-1], ends[:, 1, ::-1], -FAR, ALU.add, ALU.max))
                nc.vector.tensor_tensor(carry[:, 0, 1:NT], run[:, 0, 0:NT - 1], same[:, 0, 1:NT], ALU.add)
                nc.vector.tensor_tensor(carry[:, 1, 0:NT - 1], run[:, 1, 1:NT], same[:, 0, 1:NT], ALU.add).then_inc(s_carry, 1)
                dve.wait_ge(s_C, 1)
                link(nc.vector.tensor_copy(cq[:, :, :, :].rearrange("p k c h -> p (k c h)"), psC))
                for c in range(4):
                    nc.vector.tensor_scalar(Rup[:, c], K[:, c], K[:, c, 0:1], None, ALU.is_equal)
                    link(nc.vector.tensor_scalar(Rdown[:, c], K[:, c], K[:, c, P - 1:P], None, ALU.is_equal))
                link(nc.vector.tensor_scalar(Rup[:, :, :], Rup[:, :, :], FAR, -FAR, ALU.mult, ALU.add))
                link(nc.vector.tensor_scalar(Rdown[:, :, :], Rdown[:, :, :], FAR, -FAR, ALU.mult, ALU.add))
                for k, (R, m) in enumerate(((Rup, up), (Rdown, down))):
                    for c in range(4):
                        for h in range(H):
                            last = nc.vector.scalar_tensor_tensor(m[:, c, h], R[:, c], cq[:, k, c, h:h + 1], m[:, c, h],
                                                                  ALU.add, ALU.max)
                link(last)
                nc.vector.tensor_tensor(up[:, :, :, :], up[:, :, :, :], down[:, :, :, :], ALU.max).then_inc(s_M, 1)
                for i, (c, k) in enumerate((c, k) for c in range(4) for k in range(HX)):
                    dve.wait_ge(s_Mt, i + 1)
                    v = lg[:, c * Q:(c + 1) * Q, 4 * k:4 * k + 4]
                    nc.vector.tensor_tensor(v, v, psMt[0].rearrange("p (h q) -> p q h", h=4), ALU.subtract).then_inc(s_sub, 1)

            @block.scalar
            def _(act):
                act.wait_ge(s_sub, 4 * HX)
                nc.scalar.activation(lg[:, 0:NT, :], lg[:, 0:NT, :], ACT.Exp)


def phase_sum0(nc, E, sem):
    NT, RS, H = E.NT, E.RS, 4
    V = B + H
    with ExitStack() as st:
        def tmp(name, shape, dt):
            return st.enter_context(nc.sbuf_tensor(name, shape, dt))

        rows = tmp("a0_rows", [P, U, G, RS], F32)
        oh = tmp("a0_oh", [P, 2, G, B], F32)
        val = tmp("a0_val", [P, 2, G, V], F32)
        psA = [banks(nc, st, f"a0_ps{k}", [V, G, B]) for k in (0, 1)]
        s_in = [sem(f"a0_in{u}") for u in range(U)]
        s_link, s_val, s_sum, s_acc = (sem("a0_" + k) for k in ("link", "val", "sum", "acc"))
        n = NT // (U * G)
        ss = E.ss.rearrange("p (t f) -> p t f", f=RS)
        with nc.Block() as block:
            @block.sync
            def _(sp):
                with sp.Fori(0, n) as it:
                    for u in range(U):
                        sp.wait_ge(s_val, it * U + u + 1)
                        sp.dma_start(rows[:, u], ss[:, bass.ds(it * (U * G) + u * G, G), :]).then_inc(s_in[u], 16)
                sp.wait_ge(s_val, U * (n - 1) + 1 + U)
                sp.dma_start(rows[:, 0], ss[:, 0:G, :]).then_inc(s_in[0], 16)
                for u in range(U):
                    sp.wait_ge(s_in[u], 16 * n + 16 * (u == 0))

            @block.tensor
            def _(pe):
                with pe.Fori(0, n) as it:
                    for u in range(U):
                        par, g1 = u % 2, it * U + u + 1
                        pe.wait_ge(s_val, g1 + U)
                        pe.wait_ge(s_acc, g1)
                        for j in range(G):
                            last = nc.tensor.matmul(psA[par][:, j], val[:, par, j], oh[:, par, j], start=True, stop=True)
                        last.then_inc(s_sum, 1)

            @block.vector
            def _(dve):
                link = Link(dve, s_link)
                dve.sem_inc(s_val, U)
                dve.sem_inc(s_acc, 2)
                link(nc.vector.memset(E.acc0[:, :], 0.0))

                def values(tile0, u, par, loaded):
                    sl = bass.ds(tile0, G)
                    onehot(nc, E, oh[:, par], E.loS, tile0)
                    nc.vector.tensor_copy(val[:, par, :, B:], E.lg0[:, sl, :])
                    dve.wait_ge(s_in[u], loaded)
                    nc.vector.tensor_tensor(val[:, par, :, 0:B].rearrange("p t (h j) -> p t h j", h=H),
                                            rows[:, u, :, B:2 * B].rearrange("p t (h j) -> p t h j", h=H),
                                            bc(E.lg0[:, sl, :][:, :, :, None], [P, G, H, B // H]),
                                            ALU.mult).then_inc(s_val, 1)

                values(0, 0, 0, 16)
                with dve.Fori(0, n) as it:
                    link.loop(1, it, U * (G - 1))
                    blocks = blocks_of(nc, DVE, E.blkS, it, E.NB, U)
                    for u in range(U):
                        par, g1 = u % 2, it * U + u + 1
                        values(it * (U * G) + (u + 1) * G, (u + 1) % U, 1 - par, 16 * it + 16 * (1 + (u + 1) // U))
                        dve.wait_ge(s_sum, g1)
                        for j in range(G):
                            b = blocks[u * G + j]
                            a = E.acc0[:, bass.ds(b * B, B)]
                            ins = nc.vector.tensor_tensor(a, a, psA[par][:, j], ALU.add)
                            if j < G - 1:
                                link(ins)
                            else:
                                ins.then_inc(s_acc, 1)
                        dve.wait_ge(s_acc, g1 + 2)
                    assert link.n == U * (G - 1)


def row(v):
    return v.rearrange("(p c) -> p c", p=1)


def col(v, p):
    return v.rearrange("(c p) -> p c", p=p)


def phase_nodes1(nc, E, a, sem):
    N, NB = E.N, E.NB
    CW = NC * B
    H = 4
    H1 = 8
    with ExitStack() as st:
        def tmp(name, shape, dt=F32):
            return st.enter_context(nc.sbuf_tensor("n1_" + name, shape, dt))

        def pst(name, shape):
            return banks(nc, st, "n1_" + name, shape)

        sq = tmp("sq", [B, NB, B])
        h1 = tmp("h1", [B, NB, B + H1])
        s = tmp("s", [B, 2, NB])
        sel = tmp("sel", [B + H, B])
        cen = tmp("cen", [B, P])
        outw = tmp("outw", [B, B])
        rows = tmp("rows", [1, 2, B])
        lnrow = tmp("lnrow", [B, 2, B])
        cols = tmp("cols", [B, 2])
        fcw = tmp("fcw", [B, H1, B])
        attn = tmp("attn", [H1, 2, B])
        attnT = tmp("attnT", [B, 2, H1])
        WLR = tmp("WLR", [B, 2 * H1])
        Sb = tmp("Sb", [B, CW])
        r = tmp("r", [B, CW])
        Gn = tmp("Gn", [B, CW])
        z = tmp("z", [B, CW])
        net = tmp("net", [B, 3, CW])
        ssp = tmp("ssp", [B, CW])
        hs = tmp("hs", [B, NC, B])
        hTs = tmp("hTs", [B, CW])
        psS = pst("psS", [B, CW])
        psO = pst("psO", [P, CW])
        psY = pst("psY", [B, NC, B])
        psT = pst("psT", [B, CW])
        psA = pst("psA", [B, 2 * H1])
        psL = pst("psL", [B, 2 * H1])
        psE = pst("psE", [B, NC, 2 * H1])
        names = ("zero", "in", "link", "S", "G", "O", "z", "act", "soft", "ssp", "Y", "y", "var", "sd", "h", "at", "atc",
                 "L", "w", "hs", "T", "Tc", "E", "Ec", "b", "bc", "out", "taken", "x")
        (s_zero, s_in, s_link, s_S, s_G, s_O, s_z, s_act, s_soft, s_ssp, s_Y, s_y, s_var, s_sd, s_h, s_at, s_atc,
         s_L, s_w, s_hs, s_T, s_Tc, s_E, s_Ec, s_b, s_bc, s_out, s_taken, s_x) = (sem("n1_" + k) for k in names)
        s_fill = sem("n1_fill")
        loads = 1 + 1 + 1 + 2 + H + 1 + 1 + 2
        n = NB // NC
        with nc.Block() as block:
            @block.sync
            def _(sp):
                sp.wait_ge(s_fill, 1)
                load_nodes(sp, E.x1, a["x"], N, s_x)
                sp.dma_start(cen[:, 0:B], a["L0_gnn_cen_w"]).then_inc(s_in, 16)
                sp.dma_start(outw[:, :], a["L0_gnn_out_w"]).then_inc(s_in, 16)
                sp.dma_start(rows[:, 0], row(a["L0_gnn_out_b"])).then_inc(s_in, 16)
                for k, v in enumerate(("L0_gnn_ln_g", "L0_gnn_ln_b")):
                    sp.dma_start(lnrow[:, k], bc(row(a[v]), [B, B])).then_inc(s_in, 16)
                for h in range(H):
                    sp.dma_start(cols[16 * h:16 * h + 16, 0:1], col(a["L0_gnn_wvl_b"], 16)).then_inc(s_in, 16)
                sp.dma_start(cols[:, 1:2], col(a["L0_gnn_cen_b"], B)).then_inc(s_in, 16)
                sp.dma_start(fcw[:, :, :], a["L1_gnn_fc_w"].rearrange("(h o) c -> o h c", h=H1)).then_inc(s_in, 16)
                for k, v in enumerate(("L1_gnn_attn_l", "L1_gnn_attn_r")):
                    sp.dma_start(attn[:, k], a[v]).then_inc(s_in, 16)
                sp.wait_ge(s_in, 16 * loads)
                sp.wait_ge(s_h, 2)
                sp.dma_start(E.table1.rearrange("(b p) c -> p b c", p=B), h1[:, :, :]).then_inc(s_out, 16)
                sp.wait_ge(s_out, 16)
                sp.wait_ge(s_x, 32)

            @block.gpsimd
            def _(pool):
                nc.gpsimd.memset(sel[:, :], 0.0).then_inc(s_zero, 1)
                pool.wait_ge(s_zero, 1)
                nc.gpsimd.affine_select(out=sel[:, :].rearrange("p (h j) -> p h j", h=H),
                                        in_=sel[:, :].rearrange("p (h j) -> p h j", h=H),
                                        pattern=[[-1, H], [0, B // H]], compare_op=ALU.not_equal, fill=1.0,
                                        base=-B, channel_multiplier=1).then_inc(s_zero, 1)

            @block.tensor
            def _(pe):
                I = E.ident[0:B, 0:B]
                pe.wait_ge(s_zero, 2)
                pe.wait_ge(s_in, 16 * loads)
                nc.tensor.matmul(psA[0:1, 0:1], E.ones[:, 0:1], E.ones[:, 0:1], start=True, stop=True)
                for k in (0, 1):
                    last = nc.tensor.matmul(psA[:, k * H1:(k + 1) * H1], attn[:, k], E.ident[0:H1, 0:H1], start=True, stop=True)
                last.then_inc(s_at, 1)
                pe.wait_ge(s_atc, 1)
                for k in (0, 1):
                    for h in range(H1):
                        last = nc.tensor.matmul(psL[:, k * H1 + h:k * H1 + h + 1], fcw[:, h], attnT[:, k, h:h + 1],
                                                start=True, stop=True)
                last.then_inc(s_L, 1)
                nc.tensor.matmul(psY[0:1, 0, :], E.ones[0:B, 0:1], outw[:, :], start=True, stop=True).then_inc(s_b, 1)
                pe.wait_ge(s_bc, 1)
                with pe.Fori(0, n) as c:
                    ds = bass.ds(c * CW, CW)
                    pe.wait_ge(s_G, c + 1)
                    pe.sem_inc(s_taken, 1)
                    nc.tensor.matmul(psS[:, :], sel[:, :], E.acc0[:, ds], start=True, stop=True).then_inc(s_S, 1)
                    pe.wait_ge(s_G, c + 2)
                    pe.wait_ge(s_z, c + 1)
                    pe.sem_inc(s_taken, 1)
                    nc.tensor.matmul(psO[:, :], E.wvl[:, :], Gn[:, :], start=True, stop=False)
                    nc.tensor.matmul(psO[:, :], cen[:, :], E.h0T[:, ds], start=False, stop=True).then_inc(s_O, 1)
                    pe.wait_ge(s_ssp, c + 1)
                    pe.wait_ge(s_y, c + 1)
                    pe.sem_inc(s_taken, 1)
                    for j in range(NC):
                        nc.tensor.matmul(psY[:, j], ssp[:, j * B:(j + 1) * B], outw[:, :], start=True, stop=False)
                        last = nc.tensor.matmul(psY[:, j], E.ones[0:1, 0:B], rows[:, 1], start=False, stop=True)
                    last.then_inc(s_Y, 1)
                with pe.Fori(0, n) as c:
                    pe.wait_ge(s_hs, c + 1)
                    pe.sem_inc(s_taken, 1)
                    for j in range(NC):
                        last = nc.tensor.matmul(psT[:, j * B:(j + 1) * B], hs[:, j], I, start=True, stop=True)
                    last.then_inc(s_T, 1)
                    pe.wait_ge(s_Tc, c + 1)
                    pe.wait_ge(s_Ec, c + 1)
                    pe.sem_inc(s_taken, 1)
                    for j in range(NC):
                        last = nc.tensor.matmul(psE[:, j], hTs[:, j * B:(j + 1) * B], WLR[:, :], start=True, stop=True)
                    last.then_inc(s_E, 1)

            @block.scalar
            def _(act):
                act.wait_ge(s_in, 16 * loads)
                act.sem_inc(s_y, 1)
                with act.Fori(0, n) as c:
                    act.wait_ge(s_z, c + 2)
                    nc.scalar.activation(net[:, 0], z[:, :], ACT.Abs, bias=cols[:, 1:2]).then_inc(s_act, 1)
                    act.wait_ge(s_act, c * 2 + 1)
                    nc.scalar.activation(net[:, 1], net[:, 0], ACT.Exp, scale=-1.0).then_inc(s_act, 1)
                    act.wait_ge(s_act, c * 2 + 2)
                    nc.scalar.activation(net[:, 1], net[:, 1], ACT.Ln, bias=1.0)
                    nc.scalar.activation(net[:, 2], z[:, :], ACT.Relu, bias=cols[:, 1:2]).then_inc(s_soft, 1)
                    act.wait_ge(s_Y, c + 1)
                    nc.scalar.activation(h1[:, bass.ds(c * NC, NC), 0:B], psY[:, :, :], ACT.Copy).then_inc(s_y, 1)
                for k in (1, 2):
                    act.wait_ge(s_var, k)
                    nc.scalar.activation(s[:, 1], s[:, 1], ACT.Sqrt).then_inc(s_sd, 1)
                act.wait_ge(s_h, 1)
                with act.Fori(0, n) as c:
                    nc.scalar.activation(hs[:, :, :], h1[:, bass.ds(c * NC, NC), 0:B], ACT.Copy).then_inc(s_hs, 1)
                    act.wait_ge(s_T, c + 1)

            @block.vector
            def _(dve):
                link = Link(dve, s_link)
                nc.vector.memset(E.x1[:, NB - 1], 0.0)
                nc.vector.memset(cen[:, :], 0.0).then_inc(s_fill, 1)
                dve.wait_ge(s_at, 1)
                nc.vector.tensor_copy(attnT[:, :, :].rearrange("p k h -> p (k h)"), psA[:, :]).then_inc(s_atc, 1)
                dve.wait_ge(s_L, 1)
                nc.vector.tensor_copy(WLR[:, :], psL[:, :]).then_inc(s_w, 1)
                dve.wait_ge(s_b, 1)
                nc.vector.scalar_tensor_tensor(rows[:, 1], psY[0:1, 0, :], -float(np.log(2.0)), rows[:, 0],
                                               ALU.mult, ALU.add).then_inc(s_bc, 1)
                dve.sem_inc(s_G, 1)
                dve.sem_inc(s_z, 1)
                with dve.Fori(0, n) as c:
                    ds = bass.ds(c * CW, CW)
                    link.loop(0, c, 4)
                    dve.wait_ge(s_S, c + 1)
                    link(nc.vector.tensor_copy(Sb[:, :], psS[:, :]))
                    link(nc.vector.tensor_scalar(r[:, :], Sb[:, :], 1e-16, None, ALU.add))
                    link(nc.vector.reciprocal(r[:, :], r[:, :]))
                    nc.vector.tensor_tensor(Gn[:, :], E.acc0[0:B, ds], r[:, :], ALU.mult).then_inc(s_G, 1)
                    link(nc.vector.scalar_tensor_tensor(r[:, :], Sb[:, :], cols[:, 0:1], r[:, :], ALU.mult, ALU.mult))
                    dve.wait_ge(s_O, c + 1)
                    nc.vector.tensor_tensor(z[:, :], psO[0:B, :], r[:, :], ALU.add).then_inc(s_z, 1)
                    dve.wait_ge(s_soft, c + 1)
                    nc.vector.tensor_tensor(ssp[:, :], net[:, 1], net[:, 2], ALU.add).then_inc(s_ssp, 1)
                link.loop(0, n, 4)
                dve.wait_ge(s_y, n + 1)
                dve.wait_ge(s_x, 32)
                y = h1[:, :, 0:B]
                layernorm(nc, dve, None, link, y, s, sq[:, :, :], s_var, s_sd, 1)
                link(nc.vector.tensor_tensor(y, y, bc(lnrow[:, 0][:, None, :], [B, NB, B]), ALU.mult))
                link(nc.vector.tensor_tensor(y, y, bc(lnrow[:, 1][:, None, :], [B, NB, B]), ALU.add))
                link(nc.vector.tensor_tensor(E.x1[:, :, :], E.x1[:, :, :], y, ALU.add))
                link(nc.vector.tensor_copy(y, E.x1[:, :, :]))
                layernorm(nc, dve, None, link, y, s, sq[:, :, :], s_var, s_sd, 2)
                nc.vector.tensor_scalar(y, y, 0.0, None, ALU.max).then_inc(s_h, 1)
                dve.sem_inc(s_Ec, 1)
                with dve.Fori(0, n) as c:
                    dve.wait_ge(s_T, c + 1)
                    nc.vector.tensor_copy(hTs[:, :], psT[:, :]).then_inc(s_Tc, 1)
                    dve.wait_ge(s_E, c + 1)
                    nc.vector.tensor_copy(h1[:, bass.ds(c * NC, NC), B:B + H1], psE[:, :, 0:H1])
                    nc.vector.tensor_copy(E.ertab[:, bass.ds(c * NC, NC), :], psE[:, :, H1:]).then_inc(s_Ec, 1)
                dve.wait_ge(s_Ec, n + 1)
                dve.sem_inc(s_h, 1)


def phase_gather1(nc, E, sem):
    NT, H, W = E.NT, 8, B + 8
    with ExitStack() as st:
        def tmp(name, shape, dt=F32):
            return st.enter_context(nc.sbuf_tensor("g1_" + name, shape, dt))

        g = tmp("g", [P, 2, G, W])
        idx = tmp("idx", [P, 2, G], I32)
        oh = tmp("oh", [P, 2, G, B])
        ohT = tmp("ohT", [B, 2, G, P])
        sum_ = tmp("sum", [P, G, H])
        psT = banks(nc, st, "g1_psT", [B, G, P])
        psR = banks(nc, st, "g1_psR", [P, G, H])
        s_g = [sem("g1_g0"), sem("g1_g1")]
        s_st = [sem("g1_st0"), sem("g1_st1")]
        s_oh, s_T, s_ohT, s_r, s_lg, s_link, s_free, s_taken, s_taken2 = (
            sem("g1_" + k) for k in ("oh", "T", "ohT", "r", "lg", "link", "free", "taken", "taken2"))
        n = NT // (2 * G)
        hd = E.hg.rearrange("p (t f) -> p t f", f=W)
        with nc.Block() as block:
            @block.gpsimd
            def _(pool):
                with pool.Fori(0, n) as it:
                    for par in (0, 1):
                        pool.wait_ge(s_oh, upto(it, par))
                        pool.wait_ge(s_free, upto(it, par))
                        pool.wait_ge(s_lg, upto(it, par))
                        pool.sem_inc(s_taken2, 1)
                        for j in range(G):
                            nc.gpsimd.indirect_dma_start(
                                out=g[:, par, j, :], out_offset=None, in_=E.table1,
                                in_offset=bass.IndirectOffsetOnAxis(ap=idx[:, par, j:j + 1], axis=0)).then_inc(s_g[par], 16)
                for par in (0, 1):
                    pool.wait_ge(s_g[par], 64 * n)

            @block.sync
            def _(sp):
                sp.sem_inc(s_free, 1)
                sp.dma_start(E.hg[0:1, 0:W], E.table1[0:1, :]).then_inc(s_st[1], 16)
                with sp.Fori(0, n) as it:
                    for par in (0, 1):
                        sp.wait_ge(s_st[1 - par], it * 16 + 16)
                        sp.sem_inc(s_free, 1)
                        sp.wait_ge(s_g[par], it * 64 + 64)
                        sp.dma_start(hd[:, tiles(it, par), :], g[:, par]).then_inc(s_st[par], 16)
                sp.wait_ge(s_st[0], 16 * n)
                sp.wait_ge(s_st[1], 16 * n + 16)

            @block.tensor
            def _(pe):
                with pe.Fori(0, n) as it:
                    blocks = blocks_of(nc, PE, E.blkD, it, E.NB)
                    for par in (0, 1):
                        g1 = upto(it, par)
                        pe.wait_ge(s_oh, g1)
                        pe.wait_ge(s_ohT, g1)
                        for j in range(G):
                            last = nc.tensor.matmul(psT[:, j], oh[:, par, j], E.ident[:, :], start=True, stop=True)
                        last.then_inc(s_T, 1)
                        pe.wait_ge(s_ohT, g1 + 1)
                        pe.wait_ge(s_lg, g1 + 1)
                        pe.sem_inc(s_taken, 1)
                        for j in range(G):
                            b = blocks[par * G + j]
                            last = nc.tensor.matmul(psR[:, j], ohT[:, par, j], E.ertab[:, bass.ds(b, 1), :],
                                                    start=True, stop=True)
                        last.then_inc(s_r, 1)

            @block.scalar
            def _(act):
                act.sem_inc(s_ohT, 1)
                with act.Fori(0, n) as it:
                    for par in (0, 1):
                        act.wait_ge(s_T, upto(it, par))
                        nc.scalar.activation(ohT[:, par], psT[:, :, :], ACT.Copy).then_inc(s_ohT, 1)

            @block.vector
            def _(dve):
                link = Link(dve, s_link)
                dve.sem_inc(s_lg, 2)

                def onehots(tile0, par):
                    sl = bass.ds(tile0, G)
                    nc.vector.tensor_copy(idx[:, par], E.srcI[:, sl])
                    nc.vector.tensor_tensor(oh[:, par], bc(E.iota[:, None, 0:B], [P, G, B]),
                                            bc(E.loD[:, sl][:, :, None], [P, G, B]), ALU.is_equal).then_inc(s_oh, 1)

                nc.vector.memset(E.lg1[:, NT:], 0.0)
                onehots(0, 0)
                with dve.Fori(0, n) as it:
                    link.loop(0, it, 2)
                    for par in (0, 1):
                        if par == 1:
                            dve.wait_ge(s_g[0], it * 64 + 64)
                        else:
                            dve.wait_ge(s_oh, it * 2 + 1)
                        onehots(it * (2 * G) + (par + 1) * G, 1 - par)
                        dve.wait_ge(s_r, upto(it, par))
                        dve.wait_ge(s_g[par], it * 64 + 64)
                        link(nc.vector.tensor_tensor(sum_[:, :, :], g[:, par, :, B:], psR[:, :, :], ALU.add))
                        nc.vector.scalar_tensor_tensor(E.lg1[:, tiles(it, par), :], sum_[:, :, :], 0.2, sum_[:, :, :],
                                                       ALU.mult, ALU.max).then_inc(s_lg, 1)
                    assert link.n == 2


def phase_sum1(nc, E, sem):
    NT, H, W = E.NT, 8, B + 8
    with ExitStack() as st:
        def tmp(name, shape, dt=F32):
            return st.enter_context(nc.sbuf_tensor("a1_" + name, shape, dt))

        rows = tmp("rows", [P, 2, G, W])
        oh = tmp("oh", [P, 2, G, B])
        val = tmp("val", [P, 2, G, 5, P])
        psA = [[banks(nc, st, f"a1_ps{k}{j}", [P, 5, B]) for j in range(G)] for k in (0, 1)]
        s_in = [sem("a1_in0"), sem("a1_in1")]
        s_link, s_ez, s_val, s_valA, s_valP, s_sum, s_acc, s_taken, s_free = (
            sem("a1_" + k) for k in ("link", "ez", "val", "valA", "valP", "sum", "acc", "taken", "free"))
        n = NT // (2 * G)
        hd = E.hg.rearrange("p (t f) -> p t f", f=W)
        of_act, of_pool = (2,), (3,)
        of_dve = tuple(j for j in range(G) if j not in of_act + of_pool)

        def product(par, j):
            return (val[:, par, j, 0:4].rearrange("p k (h c) -> p (k h) c", h=2), bc(rows[:, par, j, None, 0:B], [P, H, B]),
                    bc(val[:, par, j, 4, 0:H][:, :, None], [P, H, B]))

        with nc.Block() as block:
            @block.sync
            def _(sp):
                with sp.Fori(0, n) as it:
                    for par in (0, 1):
                        sp.wait_ge(s_val, upto(it, par))
                        sp.wait_ge(s_valA, upto(it, par))
                        sp.wait_ge(s_valP, upto(it, par))
                        sp.dma_start(rows[:, par], hd[:, tiles(it, par), :]).then_inc(s_in[par], 16)
                for s in (s_val, s_valA, s_valP):
                    sp.wait_ge(s, 2 * n + 1)
                sp.dma_start(rows[:, 0], hd[:, 0:G, :]).then_inc(s_in[0], 16)
                sp.wait_ge(s_in[0], 16 * n + 16)
                sp.wait_ge(s_in[1], 16 * n)

            @block.tensor
            def _(pe):
                def sums(par, j):
                    for k in range(4):
                        nc.tensor.matmul(psA[par][j][:, k], val[:, par, j, k], oh[:, par, j], start=True, stop=True)
                    return nc.tensor.matmul(psA[par][j][0:H, 4], val[:, par, j, 4, 0:H], oh[:, par, j], start=True, stop=True)

                with pe.Fori(0, n) as it:
                    for par in (0, 1):
                        g1 = upto(it, par)
                        pe.wait_ge(s_val, g1 + 2)
                        pe.wait_ge(s_acc, g1)
                        for j in of_dve:
                            sums(par, j)
                        pe.wait_ge(s_valA, g1 + 2)
                        pe.wait_ge(s_valP, g1 + 2)
                        for j in of_act + of_pool:
                            last = sums(par, j)
                        last.then_inc(s_sum, 1)

            @block.scalar
            def _(act):
                def values(par, ez, loaded):
                    act.wait_ge(s_ez, ez)
                    act.wait_ge(s_in[par], loaded)
                    for j in of_act:
                        for h in range(H):
                            last = nc.scalar.activation(val[:, par, j, h // 2, (h % 2) * B:(h % 2 + 1) * B],
                                                        rows[:, par, j, 0:B], ACT.Copy,
                                                        scale=val[:, par, j, 4, h:h + 1])
                    last.then_inc(s_valA, 1)

                act.sem_inc(s_valA, 2)
                with act.Fori(0, n) as it:
                    for par in (0, 1):
                        values(par, upto(it, par), 16 * it + 16)
                values(0, 2 * n + 1, 16 * n + 16)

            @block.gpsimd
            def _(pool):
                def values(par, ez, loaded):
                    pool.wait_ge(s_ez, ez)
                    pool.wait_ge(s_in[par], loaded)
                    for j in of_pool:
                        out, h, e = product(par, j)
                        last = nc.gpsimd.tensor_tensor(out, h, e, ALU.mult)
                    last.then_inc(s_valP, 1)

                pool.sem_inc(s_valP, 2)
                with pool.Fori(0, n) as it:
                    for par in (0, 1):
                        values(par, upto(it, par), 16 * it + 16)
                values(0, 2 * n + 1, 16 * n + 16)

            @block.vector
            def _(dve):
                link = Link(dve, s_link)
                link(nc.vector.memset(E.acc1[:, :, :], 0.0))
                dve.sem_inc(s_val, 2)
                dve.sem_inc(s_acc, 2)

                def values(tile0, par, free, loaded):
                    if free is not None:
                        dve.wait_ge(s_sum, free)
                    sl = bass.ds(tile0, G)
                    nc.vector.tensor_copy(val[:, par, :, 4, 0:H], E.lg1[:, sl, :]).then_inc(s_ez, 1)
                    nc.vector.tensor_tensor(oh[:, par], bc(E.iota[:, None, 0:B], [P, G, B]),
                                            bc(E.loD[:, sl][:, :, None], [P, G, B]), ALU.is_equal)
                    dve.wait_ge(s_in[par], loaded)
                    dve.wait_ge(s_ez, free + 1 if free is not None else 1)
                    for j in of_dve:
                        out, h, e = product(par, j)
                        last = nc.vector.tensor_tensor(out, h, e, ALU.mult)
                    last.then_inc(s_val, 1)

                def add(it, par, blocks):
                    dve.wait_ge(s_sum, upto(it, par) + 1)
                    for j in range(G):
                        ds = bass.ds(blocks[par * G + j] * B, B)
                        v, d = E.acc1[:, 0:4, ds], E.acc1[0:H, 4, ds]
                        nc.vector.tensor_tensor(v, v, psA[par][j][:, 0:4], ALU.add)
                        ins = nc.vector.tensor_tensor(d, d, psA[par][j][0:H, 4], ALU.add)
                        if j < G - 1:
                            link(ins)
                        else:
                            ins.then_inc(s_acc, 1)
                    dve.wait_ge(s_acc, upto(it, par) + 2)

                dve.sem_inc(s_sum, 1)
                values(0, 0, None, 16)
                with dve.Fori(0, n) as it:
                    blocks = blocks_of(nc, DVE, E.blkD, it, E.NB)
                    link.loop(1, it, 2 * (G - 1))
                    for par in (0, 1):
                        values(it * (2 * G) + (par + 1) * G, 1 - par, upto(it, par), 16 * it + 16 * (par + 1))
                        add(it, par, blocks)
                    assert link.n == 2 * (G - 1)


def phase_dense1(nc, E, a, out, sem):
    N, NB = E.N, E.NB
    CW = NC * B
    n = NB // NC
    FM = a["L1_gnn_w1"].shape[0] // P
    with ExitStack() as st:
        def tmp(name, shape, dt=F32):
            return st.enter_context(nc.sbuf_tensor("d_" + name, shape, dt))

        def pst(name, shape):
            return banks(nc, st, "d_" + name, shape)

        fcs = tmp("fcs", [B, 8, B])
        FC = tmp("FC", [P, 4, P])
        selR = tmp("selR", [8, 4, P])
        rec = tmp("rec", [8, NB * B])
        rb = tmp("rb", [P, 2, CW])
        w1s = tmp("w1s", [P, 2, 4 * P])
        w1T = tmp("w1T", [P, 4, FM * P])
        w2s = tmp("w2s", [B, FM, P])
        w2T = tmp("w2T", [P, FM, B])
        c1 = tmp("c1", [P, 4, 3])
        bb1 = tmp("bb1", [P, FM])
        c2 = tmp("c2", [B, 3])
        st1 = tmp("st1", [P, 4, n, 6])
        mv1 = tmp("mv1", [P, 4, 2])
        sc1 = tmp("sc1", [P, 4, 3])
        st2 = tmp("st2", [B, n, 6])
        mv2 = tmp("mv2", [B, 2])
        sc2 = tmp("sc2", [B, 3])
        hn = tmp("hn", [P, 4, CW])
        h2 = tmp("h2", [P, 2, CW])
        yT = tmp("yT", [B, NB * B])
        yn = tmp("yn", [B, CW])
        fin = tmp("fin", [B, NC, B])
        pw = [pst(f"ps{k}", [P, BANK]) for k in range(4)]
        ps = [v[:, 0:CW] for v in pw]
        psY = pst("psY", [B, CW])
        psZ = pst("psZ", [B, NC, B])
        names = ("zero", "in", "link", "w1", "tp", "tpc", "R", "Rb", "rbc", "Rw", "bn", "sd", "sdd", "hn", "h", "h2",
                 "Y", "y", "yn", "Z", "fin", "out", "taken", "w1f", "rec", "hn1", "last", "fcc", "bn2")
        (s_zero, s_in, s_link, s_w1, s_tp, s_tpc, s_R, s_Rb, s_rbc, s_Rw, s_bn, s_sd, s_sdd, s_hn, s_h, s_h2,
         s_Y, s_y, s_yn, s_Z, s_fin, s_out, s_taken, s_w1f, s_rec, s_hn1, s_last, s_fcc, s_bn2) = (sem("d_" + k) for k in names)
        s_w1d = [sem("d_w1d0"), sem("d_w1d1")]
        s_outd = sem("d_outd")
        loads = 1 + 1 + 3 + 1 + 3
        ntp = FM + 2 + 4
        edge = [CW] * (n - 1) + [N - (n - 1) * CW]
        with nc.Block() as block:
            @block.sync
            def _(sp):
                sp.dma_start(fcs[:, :, :], a["L1_gnn_fc_w"].rearrange("(h o) c -> o h c", h=8)).then_inc(s_in, 16)
                sp.dma_start(w2s[:, :, :], a["L1_gnn_w2"].rearrange("o (m p) -> o m p", p=P)).then_inc(s_in, 16)
                for k, v in enumerate(("L1_gnn_gat_bias", "L1_gnn_bn1_gamma", "L1_gnn_bn1_beta")):
                    sp.dma_start(c1[:, :, k:k + 1], a[v].rearrange("(k p c) -> p k c", p=P, c=1),
                                 allow_slow_non_contiguous=True).then_inc(s_in, 16)
                sp.dma_start(bb1[:, :, None], a["L1_gnn_b1"].rearrange("(k p c) -> p k c", p=P, c=1),
                                 allow_slow_non_contiguous=True).then_inc(s_in, 16)
                for k, v in enumerate(("L1_gnn_b2", "L1_gnn_bn2_gamma", "L1_gnn_bn2_beta")):
                    sp.dma_start(c2[:, k:k + 1], col(a[v], B)).then_inc(s_in, 16)
                for m in range(FM):
                    if m >= 2:
                        sp.wait_ge(s_tp, m - 1)
                    sp.dma_start(w1s[:, m % 2], a["L1_gnn_w1"][m * P:(m + 1) * P]).then_inc(s_w1d[m % 2], 16)
                sp.wait_ge(s_in, 16 * loads)
                sp.sem_inc(s_out, 1)
                full = N // B
                ov = out[0:full * B].rearrange("(b p) c -> p b c", p=B)
                with sp.Fori(0, n - 1) as c:
                    sp.wait_ge(s_fin, c + 1)
                    sp.dma_start(ov[:, bass.ds(c * NC, NC), :], fin[:, :, :]).then_inc(s_outd, 16)
                    sp.wait_ge(s_outd, c * 16 + 16)
                    sp.sem_inc(s_out, 1)
                sp.wait_ge(s_fin, n)
                sp.dma_start(ov[:, (n - 1) * NC:full, :], fin[:, 0:full - (n - 1) * NC]).then_inc(s_outd, 16)
                sp.dma_start(out[full * B:N], fin[0:N - full * B, NC - 1]).then_inc(s_outd, 16)
                sp.wait_ge(s_outd, 16 * (n + 1))

            @block.gpsimd
            def _(pool):
                nc.gpsimd.memset(selR[:, :, :], 0.0).then_inc(s_zero, 1)
                pool.wait_ge(s_zero, 1)
                v = selR[:, :, :].rearrange("p k (h c) -> p (k h) c", h=2)
                nc.gpsimd.affine_select(out=v, in_=v, pattern=[[-1, 8], [0, B]], compare_op=ALU.not_equal, fill=1.0,
                                        base=0, channel_multiplier=1).then_inc(s_zero, 1)

            def second(pe, c, m):
                if m == 0:
                    pe.wait_ge(s_y, c + 1)
                pe.wait_ge(s_h, c * FM + m + 5)
                last = nc.tensor.matmul(psY[:, :], w2T[:, m], h2[:, m % 2], start=(m == 0), stop=(m == FM - 1))
                last.then_inc(s_Y, 1)

            @block.tensor
            def _(pe):
                I = E.ident[0:B, 0:B]
                pe.wait_ge(s_in, 16 * loads)
                pe.wait_ge(s_zero, 2)
                for m in range(ntp):
                    if m >= 4:
                        pe.wait_ge(s_tpc, m - 3)
                    b = pw[m % 4]
                    if m < FM:
                        pe.wait_ge(s_w1d[m % 2], 16 * (m // 2 + 1))
                        for k in range(4):
                            last = nc.tensor.matmul(b[:, k * P:(k + 1) * P], w1s[:, m % 2, k * P:(k + 1) * P], E.ident[:, :],
                                                    start=True, stop=True)
                    elif m < FM + 2:
                        for k in range(4):
                            last = nc.tensor.matmul(b[:, k * B:(k + 1) * B], w2s[:, (m - FM) * 4 + k], I, start=True, stop=True)
                    else:
                        for k in (0, 1):
                            last = nc.tensor.matmul(b[64 * k:64 * k + 64, 64 * k:64 * k + 64], fcs[:, 2 * (m - FM - 2) + k],
                                                    I, start=True, stop=True)
                    last.then_inc(s_tp, 1)
                pe.wait_ge(s_tpc, ntp)
                pe.wait_ge(s_rec, 1)
                with pe.Fori(0, n) as c:
                    ds = bass.ds(c * CW, CW)
                    for k in range(4):
                        q = k % 2
                        pe.wait_ge(s_Rw, c * 4 + k + 1)
                        pe.sem_inc(s_taken, 1)
                        nc.tensor.matmul(ps[2 + q][:, :], selR[:, k], rec[:, ds], start=True, stop=True).then_inc(s_Rb, 1)
                        nc.tensor.matmul(ps[q][:, :], FC[:, k], E.acc1[:, k, ds], start=True, stop=True).then_inc(s_R, 1)
                pe.sem_inc(s_Y, 2)
                with pe.Fori(0, n) as c:
                    pe.wait_ge(s_hn, c + 1)
                    for m in range(FM):
                        pe.wait_ge(s_h, c * FM + m + 1)
                        for k in range(4):
                            last = nc.tensor.matmul(ps[m % 4][:, :], w1T[:, k, m * P:(m + 1) * P], hn[:, k],
                                                    start=(k == 0), stop=(k == 3))
                        last.then_inc(s_h2, 1)
                        if m >= 1:
                            second(pe, c, m - 1)
                    second(pe, c, FM - 1)
                pe.wait_ge(s_bn2, 1)
                with pe.Fori(0, n) as c:
                    pe.wait_ge(s_yn, c + 1)
                    pe.sem_inc(s_taken, 1)
                    for j in range(NC):
                        last = nc.tensor.matmul(psZ[:, j], yn[:, j * B:(j + 1) * B], I, start=True, stop=True)
                    last.then_inc(s_Z, 1)

            @block.scalar
            def _(act):
                with act.Fori(0, n) as c:
                    for k in range(4):
                        act.wait_ge(s_Rb, c * 4 + k + 1)
                        act.wait_ge(s_Rw, c * 4 + k + 1)
                        nc.scalar.activation(rb[:, k % 2], ps[2 + k % 2][:, :], ACT.Copy).then_inc(s_rbc, 1)
                act.wait_ge(s_sd, 1)
                nc.scalar.activation(sc1[:, :, 0], sc1[:, :, 0], ACT.Sqrt).then_inc(s_sdd, 1)
                act.wait_ge(s_hn1, 1)
                act.sem_inc(s_h, 4)
                with act.Fori(0, n) as c:
                    for k in range(4):
                        last = nc.scalar.activation(hn[:, k], E.acc1[:, k, bass.ds(c * CW, CW)], ACT.Identity,
                                                    bias=sc1[:, k, 2:3], scale=sc1[:, k, 1:2])
                    last.then_inc(s_hn, 1)
                    for m in range(FM):
                        act.wait_ge(s_h2, c * FM + m + 1)
                        act.wait_ge(s_Y, c * FM + m + 1)
                        nc.scalar.activation(h2[:, m % 2], ps[m % 4][:, :], ACT.Relu, bias=bb1[:, m:m + 1]).then_inc(s_h, 1)
                act.wait_ge(s_sd, 2)
                nc.scalar.activation(sc2[:, 0:1], sc2[:, 0:1], ACT.Sqrt).then_inc(s_sdd, 1)
                act.wait_ge(s_bn2, 1)
                with act.Fori(0, n) as c:
                    nc.scalar.activation(yn[:, :], yT[:, bass.ds(c * CW, CW)], ACT.Identity, bias=sc2[:, 2:3],
                                         scale=sc2[:, 1:2]).then_inc(s_yn, 1)
                    act.wait_ge(s_fin, c + 1)

            @block.vector
            def _(dve):
                link = Link(dve, s_link)
                link(nc.vector.memset(FC[:, :, :], 0.0))
                for m in range(ntp):
                    dve.wait_ge(s_tp, m + 1)
                    b = pw[m % 4]
                    if m < FM:
                        nc.vector.tensor_copy(w1T[:, :, m * P:(m + 1) * P], b.rearrange("p (k c) -> p k c", k=4)).then_inc(s_tpc, 1)
                    elif m < FM + 2:
                        nc.vector.tensor_copy(w2T[:, (m - FM) * 4:(m - FM) * 4 + 4], b[:, 0:4 * B].rearrange("p (k c) -> p k c", k=4)).then_inc(s_tpc, 1)
                    else:
                        for k in (0, 1):
                            q = slice(64 * k, 64 * k + 64)
                            last = nc.vector.tensor_copy(FC[q, m - FM - 2, q], b[q, q])
                        last.then_inc(s_tpc, 1)
                link(nc.vector.tensor_scalar(rec[:, :], E.acc1[0:8, 4, :], 1e-30, None, ALU.max))
                nc.vector.reciprocal(rec[:, :], rec[:, :]).then_inc(s_rec, 1)
                dve.sem_inc(s_Rw, 2)
                with dve.Fori(0, n) as c:
                    link.loop(2, c, 4)
                    for k in range(4):
                        v = E.acc1[:, k, bass.ds(c * CW, CW)]
                        dve.wait_ge(s_R, c * 4 + k + 1)
                        dve.wait_ge(s_rbc, c * 4 + k + 1)
                        link(nc.vector.tensor_tensor(v, ps[k % 2][:, :], rb[:, k % 2], ALU.mult))
                        nc.vector.tensor_scalar(v, v, c1[:, k, 0:1], None, ALU.add).then_inc(s_Rw, 1)
                link.loop(2, n, 4)
                dve.wait_ge(s_Rw, 4 * n + 2)
                for k in range(4):
                    for c in range(n):
                        last = nc.vector.bn_stats(st1[:, k, c], E.acc1[:, k, c * CW:c * CW + edge[c]])
                link(last)
                for k in range(4):
                    last = nc.vector.bn_aggr(mv1[:, k], st1[:, k].rearrange("p a b -> p (a b)"))
                link(last)
                batchnorm_scale(nc, dve, link, mv1[:, :, 0], mv1[:, :, 1], sc1[:, :, 0], sc1[:, :, 1], sc1[:, :, 2],
                                c1[:, :, 1], c1[:, :, 2], s_sd, s_sdd, 1)
                dve.sem_inc(s_hn1, 1)
                dve.sem_inc(s_y, 1)
                with dve.Fori(0, n) as c:
                    dve.wait_ge(s_Y, c * FM + FM + 2)
                    nc.vector.tensor_scalar(yT[:, bass.ds(c * CW, CW)], psY[:, :], c2[:, 0:1], None, ALU.add).then_inc(s_y, 1)
                dve.wait_ge(s_y, n + 1)
                for c in range(n):
                    last = nc.vector.bn_stats(st2[:, c], yT[:, c * CW:c * CW + edge[c]])
                link(last)
                link(nc.vector.bn_aggr(mv2[:, :], st2[:, :, :].rearrange("p a b -> p (a b)")))
                batchnorm_scale(nc, dve, link, mv2[:, 0:1], mv2[:, 1:2], sc2[:, 0:1], sc2[:, 1:2], sc2[:, 2:3],
                                c2[:, 1:2], c2[:, 2:3], s_sd, s_sdd, 2)
                dve.sem_inc(s_bn2, 1)
                with dve.Fori(0, n) as c:
                    dve.wait_ge(s_Z, c + 1)
                    dve.wait_ge(s_out, c + 1)
                    nc.vector.tensor_tensor(fin[:, :, :], psZ[:, :, :], E.x1[:, bass.ds(c * NC, NC), :],
                                            ALU.add).then_inc(s_fin, 1)


def batchnorm_scale(nc, dve, link, mean, var, sd, scale, shift, gamma, beta, s_sd, s_sdd, n):
    nc.vector.tensor_scalar(sd, var, 1e-5, None, ALU.add).then_inc(s_sd, 1)
    dve.wait_ge(s_sdd, n)
    link(nc.vector.reciprocal(sd, sd))
    link(nc.vector.tensor_tensor(scale, sd, gamma, ALU.mult))
    link(nc.vector.tensor_tensor(shift, mean, scale, ALU.mult))
    link(nc.vector.tensor_tensor(shift, beta, shift, ALU.subtract))


def phase_setup(nc, E, a, sem):
    N, NT, NT0 = E.N, E.NT, E.NT0
    with ExitStack() as st:
        def tmp(name, shape, dt):
            return st.enter_context(nc.sbuf_tensor(name, shape, dt))

        def pst(name, shape, dt):
            return banks(nc, st, name, shape)

        H = Hist(nc, tmp, pst, sem, "D", NT0)
        HS = Hist(nc, tmp, pst, sem, "S", NT0)
        hiS = tmp("hiS0", [P, NT0], F32)
        loS = tmp("loS0_", [P, NT0], F32)
        idx = tmp("idx", [P, 2, NT0], I32)
        ti = tmp("ti", [P, NT0], I32)
        unset = tmp("unset", [P, 2 * max(E.RD, E.RS)], F32)
        s_ones, s_mask, s_fill, s_in, s_dve, s_low = (sem(n) for n in
                                                      ("s_ones", "s_mask", "s_fill", "s_in", "s_dve", "s_low"))
        s_hz, s_w, s_attr = sem("s_hz"), sem("s_w"), sem("s_attr")
        full = P - 1
        last = E.E - full * NT0
        with nc.Block() as block:
            @block.gpsimd
            def _(pool):
                masks_pool(nc, pool, E, s_ones, s_mask)
                pool.wait_ge(s_low, 1)
                for table, width, done in ((E.sd, E.RD, E.scatD), (E.ss, E.RS, E.scatS)):
                    w = NT * width // 8
                    for k in range(8):
                        pool.dma_start(table[:, k * w:(k + 1) * w].rearrange("p (n w) -> p n w", w=2 * width),
                                       bc(unset[:, None, 0:2 * width], [P, NT // 16, 2 * width])).then_inc(done[k % 2], 16)

            @block.sync
            def _(sp):
                sp.wait_ge(s_fill, 1)
                for k, v in enumerate((a["src"], a["dst"])):
                    sp.dma_start(idx[0:full, k], v[0:full * NT0].rearrange("(p t) -> p t", p=full)).then_inc(s_in, 16)
                    sp.dma_start(idx[full:P, k, 0:last], v[full * NT0:E.E].rearrange("(p t) -> p t", p=1)).then_inc(s_in, 16)
                for t in range(G):
                    for k, n in enumerate(("wk", "wv")):
                        o = 32 * t + 16 * k
                        sp.dma_start(E.W1[16 * t:16 * t + 16, o:o + 16], a[f"L0_gnn_{n}1_w"]).then_inc(s_w, 16)
                        sp.dma_start(E.W2[o:o + 16, o:o + 16], a[f"L0_gnn_{n}2_w"]).then_inc(s_w, 16)
                        sp.dma_start(E.b1[o:o + 16, :], a[f"L0_gnn_{n}1_b"].rearrange("(p c) -> p c", c=1)).then_inc(s_w, 16)
                        sp.dma_start(E.b2[:, o:o + 16], bc(a[f"L0_gnn_{n}2_b"].rearrange("(p c) -> p c", p=1),
                                                           [P, 16])).then_inc(s_w, 16)
                ea = a["edge_attr_16"]
                sp.dma_start(E.attr[0:full, 0:NT0], ea[0:full * NT0].rearrange("(p t) f -> p t f", p=full)).then_inc(s_attr, 16)
                sp.dma_start(E.attr[full:P, 0:last], ea[full * NT0:E.E].rearrange("(p t) f -> p t f", p=1)).then_inc(s_attr, 16)
                sp.wait_ge(s_w, 16 * 8 * G)
                sp.wait_ge(s_in, 64)
                sp.wait_ge(s_attr, 32)

            @block.vector
            def _(dve):
                link = Link(dve, s_dve)
                nc.vector.memset(E.attr[96:P, 0:NT0], 0.0)
                nc.vector.memset(E.attr[:, NT0:], 0.0)
                nc.vector.memset(E.W1[:, :], 0.0)
                nc.vector.memset(E.W2[:, :], 0.0)
                nc.vector.memset(idx[96:P], E.NB * B - 1).then_inc(s_fill, 1)
                nc.vector.memset(unset[:, :], -1.0).then_inc(s_low, 1)
                nc.vector.memset(H.zero[:, :], 0.0).then_inc(s_hz, 1)
                nc.vector.memset(HS.zero[:, :], 0.0).then_inc(s_hz, 1)
                link(nc.vector.memset(E.key0[:, :, NT0:], -1.0))
                link(nc.vector.memset(E.hi0[:, NT0:], -1.0))
                link(nc.vector.memset(E.lo0[:, NT0:], -1.0))
                dve.wait_ge(s_mask, 1)
                link(nc.vector.tensor_copy(E.iota[:, :], E.iota_i[:, :]))
                link(nc.vector.tensor_copy(E.identb[:, :], E.ident[:, :]))
                dve.wait_ge(s_in, 64)
                split_keys(nc, link, E.key0[:, 1, 0:NT0], idx[:, 1], E.hi0[:, 0:NT0], E.lo0[:, 0:NT0], ti[:, :])
                histogram_vector(nc, dve, E, H, E.hi0, E.lo0)
                split_keys(nc, link, E.key0[:, 0, 0:NT0], idx[:, 0], hiS[:, :], loS[:, :], ti[:, :])
                histogram_vector(nc, dve, E, HS, hiS, loS)
                base_vector(nc, dve, E, H, link, E.T0D[:, :], E.blkD[:, :])
                base_vector(nc, dve, E, HS, link, E.T0S[:, :], E.blkS[:, :])

            @block.tensor
            def _(pe):
                pe.wait_ge(s_hz, 2)
                for h in (H, HS):
                    pe.sem_inc(h.counted, 2)
                    histogram_tensor(nc, pe, E, h)
                for h in (H, HS):
                    base_tensor(nc, pe, E, h)


def phase_nets(nc, E, sem):
    NT0, EF = E.NT0, E.EF
    NG = 4
    CW = NG * P
    with ExitStack() as st:
        def tmp(name, shape):
            return st.enter_context(nc.sbuf_tensor("e_" + name, shape, F32))

        U = tmp("U", [P, NT0 // G * P])
        at = tmp("at", [P, 2, NG * G * EF])
        atT = tmp("atT", [G * EF, 2, CW])
        ssp = tmp("ssp", [P, 2, CW])
        psT = [banks(nc, st, f"e_psT{k}", [G * EF, CW]) for k in (0, 1)]
        psN = [banks(nc, st, f"e_psN{k}", [P, CW]) for k in (0, 1)]
        psW = [banks(nc, st, f"e_psW{k}", [P, CW]) for k in (0, 1)]
        s_at, s_T, s_Tc, s_N, s_Nc, s_abs, s_exp, s_ln, s_ssp, s_W, s_Wc, s_b, s_link, s_taken = (
            sem("e_" + k) for k in ("at", "T", "Tc", "N", "Nc", "abs", "exp", "ln", "ssp", "W", "Wc", "b", "link", "taken"))
        n = NT0 // (NG * G)
        half = n // 4 * 2
        assert NT0 % (NG * G) == 0 and n % 2 == 0
        cuts = (slice(0, half * CW), slice(half * CW, n * CW))

        def two(it, par, k=0):
            return it * 2 + par + 1 + k

        def at_chunk(it, par):
            return bass.ds(it * (2 * CW) + par * CW, CW)

        with nc.Block() as block:
            @block.tensor
            def _(pe):
                nc.tensor.matmul(psW[0][:, 0:P], E.ones[:, :], E.W2[:, :], start=True, stop=True).then_inc(s_b, 1)
                pe.sem_inc(s_N, 2)

                def transposed(par):
                    pe.sem_inc(s_taken, 1)
                    for q in range(NG):
                        last = nc.tensor.matmul(psT[par][:, q * P:(q + 1) * P], at[:, par, q * G * EF:(q + 1) * G * EF],
                                                E.ident[:, :], start=True, stop=True)
                    last.then_inc(s_T, 1)

                pe.wait_ge(s_at, 1)
                pe.wait_ge(s_Tc, 1)
                transposed(0)
                with pe.Fori(0, n // 2) as it:
                    for par in (0, 1):
                        c1 = two(it, par)
                        pe.wait_ge(s_at, c1 + 1)
                        pe.wait_ge(s_Tc, c1 + 1)
                        transposed(1 - par)
                        pe.wait_ge(s_Tc, c1 + 2)
                        pe.wait_ge(s_Nc, c1)
                        pe.sem_inc(s_taken, 1)
                        nc.tensor.matmul(psN[par][:, :], E.W1[:, :], atT[:, par], start=True, stop=True).then_inc(s_N, 1)
                with pe.Fori(0, n // 2) as it:
                    for par in (0, 1):
                        c1 = two(it, par)
                        pe.wait_ge(s_ssp, c1)
                        pe.wait_ge(s_Wc, c1)
                        pe.sem_inc(s_taken, 1)
                        for q in range(NG):
                            last = nc.tensor.matmul(psW[par][:, q * P:(q + 1) * P], ssp[:, par, q * P:(q + 1) * P],
                                                    E.W2[:, :], start=True, stop=True)
                        last.then_inc(s_W, 1)

            @block.scalar
            def _(act):
                def attrs(tile0, par):
                    nc.scalar.activation(at[:, par].rearrange("p (t f) -> p t f", f=EF),
                                         E.attr[:, bass.ds(tile0, NG * G), :], ACT.Copy).then_inc(s_at, 1)

                act.sem_inc(s_T, 2)
                attrs(0, 0)
                with act.Fori(0, n // 2) as it:
                    for par in (0, 1):
                        c1 = two(it, par)
                        act.wait_ge(s_T, c1 + 1)
                        attrs(it * (2 * NG * G) + (par + 1) * NG * G, 1 - par)
                        act.wait_ge(s_N, c1 + 2)
                        nc.scalar.activation(E.X[:, at_chunk(it, par)], psN[par][:, :], ACT.Identity, bias=E.b1[:, 0:1])
                        nc.scalar.activation(U[:, at_chunk(it, par)], psN[par][:, :], ACT.Abs,
                                             bias=E.b1[:, 0:1]).then_inc(s_Nc, 1)
                act.wait_ge(s_Nc, n + 2)
                for c in cuts:
                    nc.scalar.activation(U[:, c], U[:, c], ACT.Exp, scale=-1.0).then_inc(s_exp, 1)
                for k, c in enumerate(cuts):
                    act.wait_ge(s_exp, k + 1)
                    nc.scalar.activation(U[:, c], U[:, c], ACT.Ln, bias=1.0).then_inc(s_ln, 1)

            @block.vector
            def _(dve):
                link = Link(dve, s_link)
                dve.sem_inc(s_Tc, 2)
                dve.sem_inc(s_Nc, 2)
                dve.wait_ge(s_b, 1)
                link(nc.vector.scalar_tensor_tensor(E.b2[:, :], psW[0][:, 0:P], -float(np.log(2.0)), E.b2[:, :],
                                                    ALU.mult, ALU.add))
                dve.sem_inc(s_Wc, 2)
                with dve.Fori(0, n // 2) as it:
                    for par in (0, 1):
                        dve.wait_ge(s_T, two(it, par) + 2)
                        dve.wait_ge(s_N, two(it, par))
                        nc.vector.tensor_copy(atT[:, par], psT[par][:, :]).then_inc(s_Tc, 1)
                done = 0
                for k, pairs in enumerate((n // 4, n // 2)):
                    dve.wait_ge(s_ln, k + 1)
                    with dve.Fori(done, pairs) as it:
                        for par in (0, 1):
                            c = at_chunk(it, par)
                            dve.wait_ge(s_Wc, two(it, par))
                            nc.vector.scalar_tensor_tensor(ssp[:, par], E.X[:, c], 0.0, U[:, c], ALU.max,
                                                           ALU.add).then_inc(s_ssp, 1)
                        for par in (0, 1):
                            dve.wait_ge(s_W, two(it, par))
                            nc.vector.tensor_tensor(
                                E.X[:, at_chunk(it, par)].rearrange("p (q c) -> p q c", q=NG),
                                psW[par][:, :].rearrange("p (q c) -> p q c", q=NG),
                                bc(E.b2[:, None, :], [P, NG, P]), ALU.add).then_inc(s_Wc, 1)
                    done = pairs
                dve.wait_ge(s_Wc, n + 2)


def phase_sort_dst(nc, E, sem):
    NT, NT0 = E.NT, E.NT0
    W = 2 * E.EF
    with ExitStack() as st:
        def tmp(name, shape, dt):
            return st.enter_context(nc.sbuf_tensor(name, shape, dt))

        def pst(name, shape, dt):
            return banks(nc, st, name, shape)

        R = Rank(nc, tmp, pst, sem, "RD")
        pay = tmp("payD", [P, 2, G, E.RD], F32)
        s_link, s_pay, s_taken = sem("s_linkD"), sem("s_payD"), sem("s_takenD")
        n = NT0 // (2 * G)
        keys = (E.hi0, E.lo0)
        with nc.Block() as block:
            @block.tensor
            def _(pe):
                pe.sem_inc(R.look_ready, 2)
                pe.wait_ge(R.oh_ready, 1)
                pe.wait_ge(R.T_ready, 1)
                rank_tensor_hist(nc, pe, E, R, 0)
                with pe.Fori(0, n) as it:
                    for par in (0, 1):
                        rank_tensor_same(nc, pe, R, it, par)
                        rank_tensor_look(nc, pe, R, it, par)
                        rank_tensor_next(nc, pe, E, R, it, par)
                        rank_tensor_look_tile(nc, pe, R, it, par)

            @block.scalar
            def _(act):
                with act.Fori(0, n) as it:
                    for par in (0, 1):
                        rank_scalar(nc, act, R, it, par)
                        act.wait_ge(E.scatD[par], 64 * it + 64)
                        nc.scalar.activation(pay[:, par, :, 0:2],
                                             E.key0[:, :, tiles(it, par)].rearrange("p k t -> p t k"), ACT.Copy)
                        nc.scalar.activation(pay[:, par, :, 2:E.RD].rearrange("p t c -> p t c"),
                                             E.X[:, bass.ds(it * (2 * G * W) + par * G * W, G * W)].rearrange(
                                                 "p (t c) -> p t c", c=W), ACT.Copy).then_inc(s_pay, 1)

            @block.vector
            def _(dve):
                link = Link(dve, s_link)
                dve.sem_inc(R.M_ready, 1)
                dve.sem_inc(R.look_free, 1)
                rank_zero(nc, R, link)
                for par in (0, 1):
                    rank_onehots_hi(nc, E, R, keys, par * G, par)
                    rank_onehots_lo(nc, E, R, keys, par * G, par)
                    if par == 0:
                        rank_positions(nc, link, R, 0, E.T0D[:, :])
                dve.wait_ge(R.hist_ready, 1)
                rank_positions(nc, link, R, 1, R.psT[:, :])
                with dve.Fori(0, n) as it:
                    link.loop(3, it, 2 * RANK_LINKS)
                    for par in (0, 1):
                        rank_vector_same(nc, dve, E, R, it, par)
                        rank_onehots_hi(nc, E, R, keys, it * (2 * G) + (par + 2) * G, par)
                        rank_vector_next(nc, dve, R, link, it, par)
                        rank_rows(nc, dve, E, R, keys, link, it, par, NT, E.scatD)
                    assert link.n == 2 * RANK_LINKS, link.n

            @block.gpsimd
            def _(pool):
                with pool.Fori(0, n) as it:
                    for par in (0, 1):
                        pool.wait_ge(R.row_ready, upto(it, par))
                        pool.wait_ge(s_pay, upto(it, par))
                        pool.sem_inc(s_taken, 1)
                        for j in range(G):
                            nc.gpsimd.indirect_dma_start(
                                out=E.sd_rows, out_offset=bass.IndirectOffsetOnAxis(ap=R.row[:, par, j:j + 1], axis=0),
                                in_=pay[:, par, j, :], in_offset=None).then_inc(E.scatD[par], 16)
                for par in (0, 1):
                    pool.wait_ge(E.scatD[par], 64 * n + 64)


def build(nc, a, out, dbg=None):
    E = Env()
    E.N, E.E, E.EF = a["x"].shape[0], a["src"].shape[0], a["edge_attr_16"].shape[1]
    E.NB = -(-E.N // B)
    per = 2 * G * P
    E.NT0 = -(-E.E // per) * 2 * G
    most = (E.NT0 * P + E.NB * (P - 1)) // P
    E.NT = -(-most // (4 * G)) * 4 * G
    E.RD = 2 + 2 * E.EF
    E.RS = 2 * B + 2
    sdt = nc.dram_tensor("by_dst", (P, E.NT * E.RD), F32, kind="Internal").ap()
    E.sd = sdt
    sst = nc.dram_tensor("by_src", (P, E.NT * E.RS), F32, kind="Internal").ap()
    E.ss = sst
    E.ss_rows = sst.rearrange("p (t f) -> (p t) f", f=E.RS)
    E.table1 = nc.dram_tensor("table1", (E.NB * B, B + 8), F32, kind="Internal").ap()
    E.hg = nc.dram_tensor("by_dst_h", (P, E.NT * (B + 8)), F32, kind="Internal").ap()
    E.sd_rows = sdt.rearrange("p (t f) -> (p t) f", f=E.RD)
    with ExitStack() as top:
        def sb(name, shape, dt):
            return top.enter_context(nc.sbuf_tensor(name, shape, dt))

        taken = []

        def sem(name):
            taken.append(nc.alloc_semaphore(name))
            return taken[-1]

        masks(nc, E, sb, None)
        E.T0D = sb("T0D", [B, B], F32)
        E.blkD = sb("blkD", [1, E.NT], I32)
        E.T0S = sb("T0S", [B, B], F32)
        E.blkS = sb("blkS", [1, E.NT], I32)
        E.loD = sb("loD", [P, E.NT + 2 * G], F32)
        E.keyD = sb("keyD", [P, E.NT], F32)
        E.srcI = sb("srcI", [P, E.NT + G], I32)
        E.x1 = sb("x1", [B, E.NB, B], F32)
        E.ertab = sb("ertab", [B, E.NB, 8], F32)
        E.scatD = [sem("scatD0"), sem("scatD1")]
        E.scatS = [sem("scatS0"), sem("scatS1")]

        def stack(st):
            return lambda name, shape, dt: st.enter_context(nc.sbuf_tensor(name, shape, dt))

        with ExitStack() as st:
            sb2 = stack(st)
            E.key0 = sb2("key0", [P, 2, E.NT0 + 2 * G], F32)
            E.hi0 = sb2("hi0", [P, E.NT0 + 2 * G], F32)
            E.lo0 = sb2("lo0", [P, E.NT0 + 2 * G], F32)
            E.X = sb2("X", [P, E.NT0 * 2 * E.EF], F32)
            with ExitStack() as st2:
                sb3 = stack(st2)
                E.attr = sb3("attr", [P, E.NT0 + 4 * G, E.EF], F32)
                E.W1 = sb3("W1", [B, P], F32)
                E.W2 = sb3("W2", [P, P], F32)
                E.b1 = sb3("b1", [P, 1], F32)
                E.b2 = sb3("b2", [P, P], F32)
                phase_setup(nc, E, a, sem)
                phase_nets(nc, E, sem)
            phase_sort_dst(nc, E, sem)
        with ExitStack() as first:
            sb1 = stack(first)
            E.h0T = sb1("h0T", [B, E.NB * B], F32)
            E.wvl = sb1("wvl", [B, P], F32)
            E.qtab = sb1("qtab", [B, E.NB, B + 4], F32)
            with ExitStack() as st:
                E.kvtab = stack(st)("kvtab", [B, E.NB, 2 * B], F32)
                phase_nodes0(nc, E, a, sem)
                phase_sort_src(nc, E, sem)
            E.acc0 = sb1("acc0", [B + 4, E.NB * B], F32)
            with ExitStack() as st:
                sb2 = stack(st)
                E.lg0 = sb2("lg0", [P, E.NT + G, 4], F32)
                E.loS = sb2("loS0", [P, E.NT + 2 * G], F32)
                E.keyS = sb2("keyS0", [P, E.NT + 2 * G], F32)
                phase_logits0(nc, E, sem)
                phase_softmax(nc, E, sem, "m0_", E.lg0, E.keyS, 4)
                phase_sum0(nc, E, sem)
            phase_nodes1(nc, E, a, sem)
        nc.clear_and_free_semaphores(taken)
        nc.all_engine_barrier()
        with ExitStack() as second:
            sb1 = stack(second)
            E.acc1 = sb1("acc1", [P, 5, E.NB * B], F32)
            with ExitStack() as st:
                E.lg1 = stack(st)("lg1", [P, E.NT + G, 8], F32)
                phase_gather1(nc, E, sem)
                phase_softmax(nc, E, sem, "m1_", E.lg1, E.keyD, 8)
                phase_sum1(nc, E, sem)
            phase_dense1(nc, E, a, out, sem)


_OUTS = [((3125, 64), 'float32')]


def kernel(**inputs):
    import numpy as _np
    import concourse.bacc as _bacc
    from concourse import mybir as _mybir
    from concourse.bass_utils import run_bass_kernel_spmd as _run

    nc = _bacc.Bacc("TRN2", target_bir_lowering=False, num_devices=1)
    arrays, aps = {}, {}
    for name in inputs:
        a = _np.ascontiguousarray(inputs[name])
        arrays[f"in_{name}"] = a
        aps[name] = nc.dram_tensor(f"in_{name}", a.shape, _mybir.dt.from_np(a.dtype), kind="ExternalInput").ap()
    shape, dtype = _OUTS[0]
    out = nc.dram_tensor("out_0", shape, _mybir.dt.from_np(_np.dtype(dtype)), kind="ExternalOutput").ap()
    build(nc, aps, out)
    r = _run(nc, [arrays], core_ids=[0])
    return r.results[0]["out_0"]
```

```python
from contextlib import ExitStack

import numpy as np
import concourse.bass as bass
from concourse import mybir

F32 = mybir.dt.float32
BF16 = mybir.dt.bfloat16
BF16 = mybir.dt.bfloat16
I32 = mybir.dt.int32
ALU = mybir.AluOpType
ACT = mybir.ActivationFunctionType
AXX = mybir.AxisListType.X
PE = mybir.EngineType.PE
DVE = mybir.EngineType.DVE

P = 128
B = 64
G = 4
BIG = 3.0e38


def bc(ap, shape):
    return ap.to_broadcast(shape)


class Link:

    def __init__(self, eng, sem):
        self.eng, self.sem, self.base, self.n = eng, sem, 0, 0

    def __call__(self, ins):
        self.n += 1
        ins.then_inc(self.sem, 1)
        self.eng.wait_ge(self.sem, self.base + self.n)

    def loop(self, start, it, per):
        self.base, self.n = it * per + start, 0


def upto(it, par, k=1):
    return it * (2 * k) + k * (par + 1)


def tiles(it, par):
    return bass.ds(it * (2 * G) + par * G, G)


class Env:
    pass


def blocks_of(nc, engine, blk, it, NB, groups=2):
    _, v = nc.values_load_multi_w_load_instructions(
        blk[0:1, bass.ds(it * (groups * G), groups * G)], engines=[engine], min_val=0, max_val=NB - 1,
        skip_runtime_bounds_check_because="base_vector cuts them off at the last block")
    return v


BANK = 512


def banks(nc, st, name, shape):
    size = int(np.prod(shape[1:]))
    full = -(-size // BANK) * BANK
    t = st.enter_context(nc.psum_tensor(name, [P, full], F32))
    v = t[0:shape[0], 0:size]
    if len(shape) == 3:
        v = v.rearrange("p (a b) -> p a b", a=shape[1])
    return v


def masks(E, sb):
    E.ones = sb("ones", [P, P], F32)
    E.ident = sb("ident", [P, P], F32)
    E.identb = sb("identb", [P, P], BF16)
    E.notafter = sb("notafter", [P, P], BF16)
    E.after = sb("after", [P, P], F32)
    E.iota_i = sb("iota_i", [P, E.NT], I32)
    E.iota = sb("iota", [P, E.NT], F32)


def masks_pool(nc, pool, E, s_ones, s_mask):
    nc.gpsimd.memset(E.ones[:, :], 1.0).then_inc(s_ones, 1)
    pool.wait_ge(s_ones, 1)
    for out, cmp, way in ((E.ident, ALU.is_equal, 1), (E.after, ALU.is_gt, -1)):
        nc.gpsimd.affine_select(out=out[:, :], in_=E.ones[:, :], pattern=[[-way, P]], compare_op=cmp, fill=0.0,
                                base=0, channel_multiplier=way)
    nc.gpsimd.iota(E.iota_i[:, :], pattern=[[1, E.NT]], base=0, channel_multiplier=0).then_inc(s_mask, 1)


class Rank:

    def __init__(self, nc, sb, ps, sem, n):
        self.oh = sb(n + "_oh", [P, 2, 2, G, B], BF16)
        self.ohT = sb(n + "_ohT", [B, 2, G, P], BF16)
        self.Hb = sb(n + "_Hb", [B, 2, G, B], BF16)
        self.T = sb(n + "_T", [B, 2, 2, B], BF16)
        self.M = sb(n + "_M", [P, G, P], BF16)
        self.zero = sb(n + "_zero", [1, G * B], BF16)
        self.tmp = sb(n + "_tmp", [P, G, B], F32)
        self.posf = sb(n + "_posf", [P, G], F32)
        self.posi = sb(n + "_posi", [P, 3, G], I32)
        self.row = sb(n + "_row", [P, 2, G], I32)
        self.psH = ps(n + "_psH", [B, G, B], F32)
        self.psT = ps(n + "_psT", [B, B], F32)
        self.psHT = ps(n + "_psHT", [B, G, P], F32)
        self.psE = ps(n + "_psE", [P, G, P], F32)
        self.psL = ps(n + "_psL", [P, G, B], F32)
        self.oh_ready = sem(n + "_oh_ready")
        self.hist_ready = sem(n + "_hist_ready")
        self.T_ready = sem(n + "_T_ready")
        self.hT_ready = sem(n + "_hT_ready")
        self.ohT_ready = sem(n + "_ohT_ready")
        self.same_ready = sem(n + "_same_ready")
        self.M_ready = sem(n + "_M_ready")
        self.look_ready = sem(n + "_look_ready")
        self.look_free = sem(n + "_look_free")
        self.row_ready = sem(n + "_row_ready")
        self.taken = sem(n + "_taken")


def onehot(nc, E, out, part, tile0, n=B):
    return nc.vector.tensor_tensor(out, bc(E.iota[:, None, 0:n], [P, G, n]),
                                   bc(part[:, bass.ds(tile0, G)][:, :, None], [P, G, n]), ALU.is_equal)


def rank_onehots_hi(nc, E, R, keys, tile0, par):
    onehot(nc, E, R.oh[:, par, 0], keys[0], tile0)


def rank_zero(nc, R, link):
    link(nc.vector.memset(R.zero[:, :], 0.0))


def rank_onehots_lo(nc, E, R, keys, tile0, par):
    onehot(nc, E, R.oh[:, par, 1], keys[1], tile0).then_inc(R.oh_ready, 1)


def rank_tensor_hist(nc, pe, E, R, par):
    I = E.identb[0:B, 0:B]
    pe.sem_inc(R.taken, 1)
    for k in (0, 1):
        nc.tensor.matmul(R.psT[:, :], I, R.T[:, par, k], start=(k == 0), stop=False)
    for j in range(G):
        nc.tensor.matmul(R.psH[:, j, :], R.oh[:, par, 0, j, :], R.oh[:, par, 1, j, :], start=True, stop=True)
        last = nc.tensor.matmul(R.psT[:, :], R.oh[:, par, 0, j, :], R.oh[:, par, 1, j, :], start=False, stop=(j == G - 1))
    last.then_inc(R.hist_ready, 1)
    for j in range(G):
        last = nc.tensor.matmul(R.psHT[:, j, :], R.oh[:, par, 0, j, :], E.identb[:, :], start=True, stop=True)
    last.then_inc(R.hT_ready, 1)


def rank_tensor_same(nc, pe, E, R, it, par):
    g1 = upto(it, par)
    pe.wait_ge(R.ohT_ready, g1)
    pe.wait_ge(R.M_ready, g1)
    for j in range(G):
        nc.tensor.matmul(R.psE[:, j, :], R.ohT[:, par, j, :], R.ohT[:, par, j, :], start=True, stop=False)
        last = nc.tensor.matmul(R.psE[:, j, :], E.identb[:, :], E.notafter[:, :], start=False, stop=True)
    last.then_inc(R.same_ready, 1)


def rank_tensor_next(nc, pe, E, R, it, par):
    g1 = upto(it, par)
    pe.wait_ge(R.oh_ready, g1 + 1)
    pe.wait_ge(R.T_ready, g1 + 1)
    rank_tensor_hist(nc, pe, E, R, 1 - par)


def rank_tensor_look(nc, pe, R, it, par):
    pe.wait_ge(R.look_free, upto(it, par))
    nc.tensor.matmul(R.psL[:, :, :], R.zero[0:1, 0:P], R.zero[0:1, :], start=True, stop=False)
    for j in range(G):
        nc.tensor.matmul(R.psL[:, j, :], R.ohT[:, par, j, :], R.T[:, par, 0, :], start=False, stop=False)
        nc.tensor.matmul(R.psL[:, j, :], R.ohT[:, par, j, :], R.T[:, par, 1, :], start=False, stop=False)
        for i in range(j):
            nc.tensor.matmul(R.psL[:, j, :], R.ohT[:, par, j, :], R.Hb[:, par, i, :], start=False, stop=False)


def rank_tensor_look_tile(nc, pe, R, it, par):
    pe.wait_ge(R.M_ready, upto(it, par) + 1)
    for j in range(G):
        last = nc.tensor.matmul(R.psL[:, j, :], R.M[:, j, :], R.oh[:, par, 1, j, :], start=False,
                                stop=(j == G - 1))
    last.then_inc(R.look_ready, 1)


def rank_scalar(nc, act, R, par, g1):
    act.wait_ge(R.hist_ready, g1)
    act.wait_ge(R.look_ready, g1)
    nc.scalar.activation(R.Hb[:, par], R.psH[:, :, :], ACT.Copy)
    act.wait_ge(R.hT_ready, g1)
    nc.scalar.activation(R.ohT[:, par], R.psHT[:, :, :], ACT.Copy).then_inc(R.ohT_ready, 1)


def rank_scalar_same(nc, act, R, it, par):
    g1 = upto(it, par)
    act.wait_ge(R.same_ready, g1)
    act.wait_ge(R.look_ready, g1 + 1)
    nc.scalar.activation(R.M[:, :, :], R.psE[:, :, :], ACT.Relu).then_inc(R.M_ready, 1)


def rank_positions(nc, link, R, par, pos):
    link(nc.vector.tensor_copy(R.T[:, par, 0], pos))
    nc.vector.tensor_tensor(R.T[:, par, 1], pos, R.T[:, par, 0], ALU.subtract).then_inc(R.T_ready, 1)


def rank_vector_next(nc, dve, R, link, it, par):
    dve.wait_ge(R.hist_ready, upto(it, par) + 1)
    rank_positions(nc, link, R, par, R.psT[:, :])


RANK_LINKS = 1 + 4


def rank_rows(nc, dve, E, R, keys, link, it, par, NT, scattered, padoff=None):
    g1 = upto(it, par)
    dve.wait_ge(R.look_ready, g1 + 2)
    nc.vector.tensor_tensor(R.tmp[:, :, :], R.psL[:, :, :], R.oh[:, par, 1], ALU.mult).then_inc(R.look_free, 1)
    dve.wait_ge(R.look_free, g1 + 1)
    rank_onehots_lo(nc, E, R, keys, it * (2 * G) + (par + 2) * G, par)
    link(nc.vector.tensor_reduce(R.posf[:, :], R.tmp[:, :, :], AXX, ALU.add))
    if padoff is not None:
        link(nc.vector.tensor_tensor(R.posi[:, 0], R.posf[:, :], padoff[:, tiles(it, par)], ALU.add))
    else:
        link(nc.vector.tensor_copy(R.posi[:, 0], R.posf[:, :]))
    link(nc.vector.tensor_scalar(R.posi[:, 1], R.posi[:, 0], 127, None, ALU.bitwise_and))
    link(nc.vector.tensor_scalar(R.posi[:, 2], R.posi[:, 0], 7, None, ALU.arith_shift_right))
    dve.wait_ge(scattered[par], 64 * it + 64)
    nc.vector.scalar_tensor_tensor(R.row[:, par], R.posi[:, 1], float(NT), R.posi[:, 2],
                                   ALU.mult, ALU.add).then_inc(R.row_ready, 1)


def twice(nc, out, oh, E):
    return nc.tensor.matmul(out, oh.rearrange("p k c -> p (k c)"), E.identb[:, :], start=True, stop=True)


def onehot_twice(nc, E, out, part):
    return nc.vector.tensor_tensor(out, bc(E.iota[:, None, None, 0:B], [P, G, 2, B]),
                                   bc(part[:, :, None, None], [P, G, 2, B]), ALU.is_equal)


def look_up(nc, out, ohT, A, C, b):
    nc.tensor.matmul(out, ohT, A[:, bass.ds(b, 1), :], start=True, stop=False)
    return nc.tensor.matmul(out, ohT[0:B], C[:, bass.ds(b, 1), :], start=False, stop=True)


def split_keys(nc, link, keyf, keyi, hi, lo, ti):
    link(nc.vector.tensor_copy(keyf, keyi))
    link(nc.vector.tensor_scalar(ti, keyi, 6, None, ALU.arith_shift_right))
    link(nc.vector.tensor_copy(hi, ti))
    link(nc.vector.tensor_scalar(ti, keyi, B - 1, None, ALU.bitwise_and))
    link(nc.vector.tensor_copy(lo, ti))


def histogram_vector(nc, dve, E, H, hi, lo):
    def group(it, par):
        dve.wait_ge(H.counted, upto(it, par))
        for k, part in enumerate((hi, lo)):
            last = nc.vector.tensor_tensor(H.oh[:, par, k], bc(E.iota[:, None, 0:B], [P, G, B]),
                                           bc(part[:, tiles(it, par)][:, :, None], [P, G, B]), ALU.is_equal)
        last.then_inc(H.oh_ready, 1)
    with dve.Fori(0, H.n // (2 * G)) as it:
        for par in (0, 1):
            group(it, par)


def histogram_tensor(nc, pe, E, H):
    nc.tensor.matmul(H.ps[:, :], H.zero[:, 0:B], H.zero[:, 0:B], start=True, stop=False)
    with pe.Fori(0, H.n // (2 * G)) as it:
        for par in (0, 1):
            pe.wait_ge(H.oh_ready, upto(it, par))
            for j in range(G):
                last = nc.tensor.matmul(H.ps[:, :], H.oh[:, par, 0, j], H.oh[:, par, 1, j], start=False, stop=False)
            last.then_inc(H.counted, 1)
    nc.tensor.matmul(H.ps[:, :], H.zero[:, 0:B], H.zero[:, 0:B], start=False, stop=True).then_inc(H.done, 1)


class Hist:
    def __init__(self, nc, sb, ps, sem, n, tiles_n):
        self.n = tiles_n
        self.oh = sb(n + "_hoh", [P, 2, 2, G, B], BF16)
        self.zero = sb(n + "_hzero", [P, B], BF16)
        self.c = sb(n + "_hc", [B, 4, B], F32)
        self.i = sb(n + "_hi", [B, 2], I32)
        self.nt = sb(n + "_hnt", [B, 4], F32)
        self.M = sb(n + "_hM", [B, 512], F32)
        self.ps = ps(n + "_hps", [B, B], F32)
        self.psb = ps(n + "_hpsb", [B, 512], F32)
        self.oh_ready = sem(n + "_hoh_ready")
        self.counted = sem(n + "_hcounted")
        self.done = sem(n + "_hdone")
        self.s_nt = sem(n + "_hs_nt")
        self.s_first = sem(n + "_hs_first")
        self.s_M = sem(n + "_hs_M")
        self.s_blk = sem(n + "_hs_blk")


def base_vector(nc, dve, E, H, link, T0, blk):
    dve.wait_ge(H.done, 1)
    link(nc.vector.tensor_copy(H.c[:, 0], H.ps[:, :]))
    link(nc.vector.tensor_tensor_scan(H.c[:, 1], E.ones[0:B, 0:B], H.c[:, 0], 0.0, ALU.mult, ALU.add))
    link(nc.vector.tensor_scalar(H.nt[:, 0:1], H.c[:, 1, B - 1:B], float(P - 1), None, ALU.add))
    link(nc.vector.tensor_copy(H.i[:, 0:1], H.nt[:, 0:1]))
    link(nc.vector.tensor_scalar(H.i[:, 1:2], H.i[:, 0:1], 7, None, ALU.arith_shift_right))
    nc.vector.tensor_copy(H.nt[:, 1:2], H.i[:, 1:2]).then_inc(H.s_nt, 1)
    dve.wait_ge(H.s_first, 1)
    link(nc.vector.tensor_tensor(H.nt[:, 2:3], H.psb[:, 0:1], H.nt[:, 1:2], ALU.add))
    link(nc.vector.tensor_scalar(H.nt[:, 3:4], H.psb[:, 0:1], float(P), None, ALU.mult))
    link(nc.vector.tensor_tensor(H.c[:, 2], H.c[:, 1], H.c[:, 0], ALU.subtract))
    link(nc.vector.tensor_scalar(T0, H.c[:, 2], H.nt[:, 3:4], None, ALU.add))
    nc.vector.tensor_scalar(H.M[:, 0:E.NT], E.iota[0:B, :], H.nt[:, 2:3], None, ALU.is_ge).then_inc(H.s_M, 1)
    dve.wait_ge(H.s_blk, 1)
    link(nc.vector.tensor_scalar(blk, H.psb[0:1, 0:E.NT], float(E.NB - 1), None, ALU.min))


def base_tensor(nc, pe, E, H):
    pe.wait_ge(H.s_nt, 1)
    nc.tensor.matmul(H.psb[:, 0:1], E.after[0:B, 0:B], H.nt[:, 1:2], start=True, stop=True).then_inc(H.s_first, 1)
    pe.wait_ge(H.s_M, 1)
    nc.tensor.matmul(H.psb[0:1, 0:E.NT], E.ones[0:B, 0:1], H.M[:, 0:E.NT], start=True, stop=True).then_inc(H.s_blk, 1)


NC = 7


def load_nodes(sp, dst, x, N, sem):
    full = N // B
    sp.dma_start(dst[:, 0:full], x[0:full * B].rearrange("(b p) c -> p b c", p=B)).then_inc(sem, 16)
    sp.dma_start(dst[0:N - full * B, full:full + 1],
                 x[full * B:N].rearrange("(b p) c -> p b c", b=1)).then_inc(sem, 16)


def layernorm(nc, dve, link, x, s, sq, s_var, s_sd, n):
    D = x.shape[-1]
    mean, r = s[:, 0], s[:, 1]
    sh = list(x.shape)
    link(nc.vector.tensor_reduce(mean, x, AXX, ALU.add))
    link(nc.vector.tensor_scalar(mean, mean, 1.0 / D, None, ALU.mult))
    link(nc.vector.tensor_tensor(x, x, bc(mean[:, :, None], sh), ALU.subtract))
    link(nc.vector.tensor_tensor(sq, x, x, ALU.mult))
    link(nc.vector.tensor_reduce(r, sq, AXX, ALU.add))
    nc.vector.tensor_scalar(r, r, 1.0 / D, 1e-5, ALU.mult, ALU.add).then_inc(s_var, 1)
    dve.wait_ge(s_sd, n)
    link(nc.vector.reciprocal(r, r))
    link(nc.vector.tensor_tensor(x, x, bc(r[:, :, None], sh), ALU.mult))


def phase_nodes0(nc, E, a, sem):
    N, NB = E.N, E.NB
    CW = NC * B
    with ExitStack() as st:
        def tmp(name, shape, dt):
            return st.enter_context(nc.sbuf_tensor(name, shape, dt))

        def pst(name, shape, dt):
            return banks(nc, st, name, shape)

        TW = 2 * B + B + 4
        xs = tmp("n0_x", [B, NB + NC, B], F32)
        x = xs[:, 0:NB]
        sq = tmp("n0_sq", [B, NB, B], F32)
        s = tmp("n0_s", [B, 2, NB], F32)
        hs = tmp("n0_hs", [B, NC, B], F32)
        hT2 = tmp("n0_hT2", [B, NC, 2, B], F32)
        t1 = tmp("n0_t1", [P, NC, TW], BF16)
        t2 = tmp("n0_t2", [P, NC, TW], BF16)
        rest = tmp("n0_rest", [P, NC, TW], F32)
        bd = tmp("n0_bd", [B, 4, B], F32)
        M = tmp("n0_M", [B, 68], F32)
        WKV = tmp("n0_WKV", [B, 2 * B], F32)
        WQ = tmp("n0_WQ", [B, 68], F32)
        psW = pst("n0_psW", [B, 4, B], F32)
        psT = pst("n0_psT", [B, CW], F32)
        psKV = pst("n0_psKV", [P, 8, 2 * B], F32)
        psQ = pst("n0_psQ", [P, NC, 68], F32)
        s_in, s_x, s_zero, s_link, s_var, s_sd, s_w, s_wc, s_M, s_q = (
            sem("n0_" + n) for n in ("in", "x", "zero", "link", "var", "sd", "w", "wc", "M", "q"))
        s_h, s_hs, s_T, s_Tc, s_tab, s_t1, s_rest, s_t2, s_third = (
            sem("n0_" + n) for n in ("h", "hs", "T", "Tc", "tab", "t1", "rest", "t2", "third"))
        s_taken = sem("n0_taken")
        H, D = 4, 16
        with nc.Block() as block:
            @block.sync
            def _(sp):
                sp.wait_ge(s_zero, 1)
                load_nodes(sp, x, a["x"], N, s_x)
                for h in range(H):
                    hd = slice(h * D, h * D + D)
                    for k, w in enumerate(("L0_gnn_Wk", "L0_gnn_Wv", "L0_gnn_Wq")):
                        sp.dma_start(bd[hd, k, hd], a[w][h]).then_inc(s_in, 16)
                    sp.dma_start(bd[hd, 3, hd], a["L0_gnn_wkl_w"]).then_inc(s_in, 16)
                    sp.dma_start(M[hd, B + h:B + h + 1], a["L0_gnn_wkl_b"].rearrange("(p c) -> p c", c=1)).then_inc(s_in, 16)
                    sp.dma_start(E.wvl[hd, hd], a["L0_gnn_wvl_w"]).then_inc(s_in, 16)
                sp.wait_ge(s_in, 16 * (6 * H))
                sp.wait_ge(s_x, 32)

            @block.vector
            def _(dve):
                link = Link(dve, s_link)
                for t in (E.wvl, M):
                    nc.vector.memset(t[:, :], 0.0)
                nc.vector.memset(xs[:, NB - 1:], 0.0)
                nc.vector.memset(bd[:, :, :], 0.0).then_inc(s_zero, 1)
                dve.wait_ge(s_x, 32)
                layernorm(nc, dve, link, x[:, :, :], s, sq[:, :, :], s_var, s_sd, 1)
                nc.vector.tensor_scalar(x[:, :, :], x[:, :, :], 0.0, None, ALU.max).then_inc(s_h, 1)
                dve.wait_ge(s_w, 1)
                nc.vector.tensor_copy(WKV[:, 0:2 * B], psW[:, 0:2].rearrange("p k c -> p (k c)"))
                nc.vector.tensor_copy(M[:, 0:B], psW[:, 2]).then_inc(s_wc, 1)
                dve.wait_ge(s_q, 1)
                nc.vector.tensor_scalar(WQ[:, :], psQ[0:B, 0, :], 0.25, None, ALU.mult).then_inc(s_M, 1)
                dve.sem_inc(s_rest, 1)
                dve.sem_inc(s_third, 1)

                def transposed():
                    nc.vector.tensor_copy(hT2[:, :, :, :], bc(psT[:, :].rearrange("p (j c) -> p j c", c=B)[:, :, None, :],
                                                              [B, NC, 2, B])).then_inc(s_Tc, 1)

                dve.wait_ge(s_T, 1)
                transposed()
                with dve.Fori(0, NB // NC) as c:
                    ds = bass.ds(c * NC, NC)
                    dve.wait_ge(s_third, c + 1)
                    dve.wait_ge(s_t1, c + 1)
                    nc.vector.tensor_tensor(rest[:, :, 0:2 * B], psKV[:, 0:NC, :], t1[:, :, 0:2 * B], ALU.subtract)
                    nc.vector.tensor_tensor(rest[:, :, 2 * B:], psQ[:, :, :], t1[:, :, 2 * B:],
                                            ALU.subtract).then_inc(s_rest, 1)
                    dve.wait_ge(s_T, c + 2)
                    transposed()
                    dve.wait_ge(s_rest, c + 2)
                    dve.wait_ge(s_t2, c + 1)
                    nc.vector.tensor_tensor(E.kvC[:, ds, :], rest[0:B, :, 0:2 * B], t2[0:B, :, 0:2 * B], ALU.subtract)
                    nc.vector.tensor_tensor(E.qC[:, ds, :], rest[0:B, :, 2 * B:], t2[0:B, :, 2 * B:],
                                            ALU.subtract).then_inc(s_third, 1)

            @block.scalar
            def _(act):
                act.wait_ge(s_var, 1)
                nc.scalar.activation(s[:, 1], s[:, 1], ACT.Sqrt).then_inc(s_sd, 1)
                act.wait_ge(s_h, 1)
                nc.scalar.activation(hs[:, :, :], x[:, 0:NC, :], ACT.Copy).then_inc(s_hs, 1)
                with act.Fori(0, NB // NC) as c:
                    ds = bass.ds(c * NC, NC)
                    act.wait_ge(s_Tc, c + 1)
                    nc.scalar.activation(hs[:, :, :], xs[:, bass.ds(c * NC + NC, NC), :], ACT.Copy).then_inc(s_hs, 1)
                    nc.scalar.activation(E.h0T[:, bass.ds(c * CW, CW)].rearrange("p (j c) -> p j c", c=B), hT2[:, :, 0],
                                         ACT.Copy)
                    act.wait_ge(s_tab, c + 1)
                    nc.scalar.activation(t1[:, :, 0:2 * B], psKV[:, 0:NC, :], ACT.Copy)
                    nc.scalar.activation(t1[:, :, 2 * B:], psQ[:, :, :], ACT.Copy).then_inc(s_t1, 1)
                    act.wait_ge(s_t1, c + 1)
                    nc.scalar.activation(E.kvA[0:B, ds, :], t1[0:B, :, 0:2 * B], ACT.Copy)
                    nc.scalar.activation(E.qA[0:B, ds, :], t1[0:B, :, 2 * B:], ACT.Copy)
                    act.wait_ge(s_rest, c + 2)
                    act.wait_ge(s_third, c + 1)
                    nc.scalar.activation(t2[:, :, :], rest[:, :, :], ACT.Copy).then_inc(s_t2, 1)
                    act.wait_ge(s_t2, c + 1)
                    nc.scalar.activation(E.kvA[B:P, ds, :], t2[B:P, :, 0:2 * B], ACT.Copy)
                    nc.scalar.activation(E.qA[B:P, ds, :], t2[B:P, :, 2 * B:], ACT.Copy)

            @block.tensor
            def _(pe):
                pe.wait_ge(s_in, 16 * (6 * H))
                I = E.ident[0:B, 0:B]
                for k, w in enumerate((0, 1, 3)):
                    last = nc.tensor.matmul(psW[:, k], bd[:, w], I, start=True, stop=True)
                last.then_inc(s_w, 1)
                pe.wait_ge(s_wc, 1)
                nc.tensor.matmul(psQ[0:B, 0, :], bd[:, 2], M[:, :], start=True, stop=True).then_inc(s_q, 1)
                pe.wait_ge(s_M, 1)

                def transpose():
                    pe.sem_inc(s_taken, 1)
                    for j in range(NC):
                        last = nc.tensor.matmul(psT[:, j * B:j * B + B], hs[:, j], I, start=True, stop=True)
                    last.then_inc(s_T, 1)

                pe.wait_ge(s_hs, 1)
                transpose()
                with pe.Fori(0, NB // NC) as c:
                    pe.wait_ge(s_Tc, c + 1)
                    pe.wait_ge(s_rest, c + 1)
                    pe.sem_inc(s_taken, 1)
                    for j in range(NC):
                        lhs = hT2[:, j].rearrange("p k c -> p (k c)")
                        nc.tensor.matmul(psKV[:, j, :], lhs, WKV[:, :], start=True, stop=True)
                        last = nc.tensor.matmul(psQ[:, j, :], lhs, WQ[:, :], start=True, stop=True)
                    last.then_inc(s_tab, 1)
                    pe.wait_ge(s_hs, c + 2)
                    transpose()


def phase_sort_src(nc, E, sem):
    NT, EF = E.NT, E.EF
    with ExitStack() as st:
        def tmp(name, shape, dt):
            return st.enter_context(nc.sbuf_tensor(name, shape, dt))

        def pst(name, shape, dt):
            return banks(nc, st, name, shape)

        sd = tmp("sd", [P, NT, E.RD], F32)
        KL = tmp("KL", [P, 2, NT + 2 * G], F32)
        hiS = tmp("hiS", [P, NT + 2 * G], F32)
        keyS, loS = KL[:, 0], KL[:, 1]
        pad = tmp("pad", [P, NT], F32)
        n = NT // (2 * G)
        with ExitStack() as st2:
            ki = st2.enter_context(nc.sbuf_tensor("ki", [P, NT], I32))
            ti = st2.enter_context(nc.sbuf_tensor("tiS", [P, NT], I32))
            s_sd, s_link = sem("s_sd"), sem("s_linkHS")
            with nc.Block() as block:
                @block.sync
                def _(sp):
                    sp.dma_start(sd[:, :, :], E.sd.rearrange("p (t f) -> p t f", f=E.RD)).then_inc(s_sd, 16)
                    sp.wait_ge(s_sd, 16)

                @block.vector
                def _(dve):
                    link = Link(dve, s_link)
                    link(nc.vector.memset(keyS[:, NT:], -1.0))
                    link(nc.vector.memset(hiS[:, NT:], -1.0))
                    link(nc.vector.memset(loS[:, NT:], -1.0))
                    link(nc.vector.memset(E.loD[:, NT:], -1.0))
                    link(nc.vector.memset(E.srcI[:, NT:], 0))
                    dve.wait_ge(s_sd, 16)
                    link(nc.vector.tensor_copy(ki[:, :], sd[:, :, 1]))
                    split_keys(nc, link, E.keyD[:, :], ki[:, :], hiS[:, 0:NT], E.loD[:, 0:NT], ti[:, :])
                    link(nc.vector.tensor_scalar(pad[:, :], E.keyD[:, :], 0.0, 8388608.0, ALU.is_lt, ALU.mult))
                    link(nc.vector.tensor_tensor(E.loD[:, 0:NT], E.loD[:, 0:NT], pad[:, :], ALU.max))
                    link(nc.vector.tensor_copy(ki[:, :], sd[:, :, 0]))
                    split_keys(nc, link, keyS[:, 0:NT], ki[:, :], hiS[:, 0:NT], loS[:, 0:NT], ti[:, :])
                    link(nc.vector.tensor_scalar(E.srcI[:, 0:NT], keyS[:, 0:NT], 0.0, None, ALU.max))

        R = Rank(nc, tmp, pst, sem, "RS")
        ohD = tmp("ohD", [P, 2, G, 2, B], BF16)
        ohDT = tmp("ohDT", [P, 2, G, P], BF16)
        pay = tmp("payS", [P, 2, G, E.RS], F32)
        psDT = pst("psDT", [P, G, P], F32)
        psKV = pst("psKV", [P, G, 2 * B], F32)
        s_DT, s_ohDT, s_kv, s_pay, s_link, s_taken, s_taken2 = (
            sem("es_" + k) for k in ("DT", "ohDT", "kv", "pay", "link", "taken", "taken2"))
        keys = (hiS, loS)

        def dst_transposed(par):
            for j in range(G):
                last = twice(nc, psDT[:, j], ohD[:, par, j], E)
            last.then_inc(s_DT, 1)

        with nc.Block() as block:
            @block.tensor
            def _(pe):
                pe.sem_inc(R.look_ready, 2)
                pe.wait_ge(R.oh_ready, 1)
                pe.wait_ge(R.T_ready, 1)
                rank_tensor_hist(nc, pe, E, R, 0)
                dst_transposed(0)
                with pe.Fori(0, n) as it:
                    blocks = blocks_of(nc, PE, E.blkD, it, E.NB)
                    for par in (0, 1):
                        g1 = upto(it, par)
                        rank_tensor_same(nc, pe, E, R, it, par)
                        rank_tensor_look(nc, pe, R, it, par)
                        rank_tensor_next(nc, pe, E, R, it, par)
                        pe.wait_ge(s_ohDT, g1)
                        dst_transposed(1 - par)
                        pe.wait_ge(s_pay, g1)
                        pe.sem_inc(s_taken, 1)
                        for j in range(G):
                            b = blocks[par * G + j]
                            last = look_up(nc, psKV[:, j], ohDT[:, par, j], E.kvA, E.kvC, b)
                        last.then_inc(s_kv, 1)
                        rank_tensor_look_tile(nc, pe, R, it, par)

            @block.scalar
            def _(act):
                def group(par, g1):
                    rank_scalar(nc, act, R, par, g1)
                    act.wait_ge(s_DT, g1)
                    nc.scalar.activation(ohDT[:, par], psDT[:, :, :], ACT.Copy).then_inc(s_ohDT, 1)

                act.sem_inc(R.M_ready, 1)
                group(0, 1)
                with act.Fori(0, n) as it:
                    for par in (0, 1):
                        rank_scalar_same(nc, act, R, it, par)
                        group(1 - par, upto(it, par) + 1)

            @block.vector
            def _(dve):
                link = Link(dve, s_link)
                dve.sem_inc(R.look_free, 1)
                dve.sem_inc(s_pay, 1)

                def onehots(tile0, par):
                    onehot_twice(nc, E, ohD[:, par], E.loD[:, bass.ds(tile0, G)])
                    rank_onehots_hi(nc, E, R, keys, tile0, par)

                rank_zero(nc, R, link)
                onehots(0, 0)
                rank_onehots_lo(nc, E, R, keys, 0, 0)
                rank_positions(nc, link, R, 0, E.T0S[:, :])
                onehots(G, 1)
                rank_onehots_lo(nc, E, R, keys, G, 1)
                dve.wait_ge(s_DT, 1)
                rank_positions(nc, link, R, 1, R.psT[:, :])
                with dve.Fori(0, n) as it:
                    link.loop(3, it, 2 * RANK_LINKS)
                    for par in (0, 1):
                        g1 = upto(it, par)
                        onehots(it * (2 * G) + (par + 2) * G, par)
                        rank_vector_next(nc, dve, R, link, it, par)
                        dve.wait_ge(E.scatS[par], 64 * it + 64)
                        nc.vector.tensor_copy(pay[:, par, :, 2 * B:], KL[:, :, tiles(it, par)].rearrange("p k t -> p t k"))
                        dve.wait_ge(s_kv, g1)
                        for k in (0, 1):
                            w = sd[:, tiles(it, par), 2 + k * EF:2 + (k + 1) * EF]
                            last = nc.vector.tensor_tensor(
                                pay[:, par, :, k * B:(k + 1) * B].rearrange("p t (h j) -> p t h j", h=4),
                                psKV[:, :, k * B:(k + 1) * B].rearrange("p t (h j) -> p t h j", h=4),
                                bc(w[:, :, None, :], [P, G, 4, EF]), ALU.mult)
                        last.then_inc(s_pay, 1)
                        rank_rows(nc, dve, E, R, keys, link, it, par, NT, E.scatS, pad)
                    assert link.n == 2 * RANK_LINKS, link.n

            @block.gpsimd
            def _(pool):
                limit = pool.to_reg(P * NT - 1)
                with pool.Fori(0, n) as it:
                    for par in (0, 1):
                        pool.wait_ge(R.row_ready, upto(it, par))
                        pool.wait_ge(s_pay, upto(it, par) + 1)
                        pool.sem_inc(s_taken2, 1)
                        for j in range(G):
                            nc.gpsimd.indirect_dma_start(
                                out=E.ss_rows, out_offset=bass.IndirectOffsetOnAxis(ap=R.row[:, par, j:j + 1], axis=0),
                                in_=pay[:, par, j, :], in_offset=None,
                                bounds_check=limit, oob_is_err=False).then_inc(E.scatS[par], 16)
                for par in (0, 1):
                    pool.wait_ge(E.scatS[par], 64 * n + 64)


U = 4
FAR = 1.0e30


def phase_logits0(nc, E, sem):
    NT, RS, H = E.NT, E.RS, 4
    with ExitStack() as st:
        def tmp(name, shape, dt):
            return st.enter_context(nc.sbuf_tensor(name, shape, dt))

        def pst(name, shape):
            return banks(nc, st, name, shape)

        rows = tmp("l0_rows", [P, U, G, RS], F32)
        oh = tmp("l0_oh", [P, 2, G, 2, B], BF16)
        ohT = tmp("l0_ohT", [P, 2, G, P], BF16)
        prod = tmp("l0_prod", [P, 2, G, B], F32)
        dot = tmp("l0_dot", [P, 2, G, H], F32)
        psT = pst("l0_psT", [P, G, P])
        psQ = [pst(f"l0_psQ{k}", [P, G, B + H]) for k in (0, 1)]
        s_in = [sem(f"l0_in{u}") for u in range(U)]
        s_used, s_keys, s_oh, s_T, s_ohT, s_q, s_link, s_taken = (
            sem("l0_" + k) for k in ("used", "keys", "oh", "T", "ohT", "q", "link", "taken"))
        n = NT // (U * G)
        assert NT % (U * G) == 0
        ss = E.ss.rearrange("p (t f) -> p t f", f=RS)

        def group(it, u):
            return bass.ds(it * (U * G) + u * G, G)

        with nc.Block() as block:
            @block.sync
            def _(sp):
                with sp.Fori(0, n) as it:
                    for u in range(U):
                        sp.wait_ge(s_used, it * U + u + 1)
                        sp.wait_ge(s_keys, it * U + u + 1)
                        sp.dma_start(rows[:, u], ss[:, group(it, u), :]).then_inc(s_in[u], 16)
                sp.wait_ge(s_used, U * (n - 1) + 1 + U)
                sp.wait_ge(s_keys, U * (n - 1) + 1 + U)
                sp.dma_start(rows[:, 0], ss[:, 0:G, :]).then_inc(s_in[0], 16)
                sp.wait_ge(s_used, U * (n - 1) + 2 + U)
                sp.wait_ge(s_keys, U * (n - 1) + 2 + U)
                sp.dma_start(rows[:, 1], ss[:, G:2 * G, :]).then_inc(s_in[1], 16)
                for u in range(U):
                    sp.wait_ge(s_in[u], 16 * n + 16 * (u < 2))

            @block.tensor
            def _(pe):
                def transposed(par):
                    for j in range(G):
                        last = twice(nc, psT[:, j], oh[:, par, j], E)
                    last.then_inc(s_T, 1)

                pe.sem_inc(s_q, 2)
                pe.wait_ge(s_oh, 1)
                transposed(0)
                with pe.Fori(0, n) as it:
                    blocks = blocks_of(nc, PE, E.blkS, it, E.NB, U)
                    for u in range(U):
                        par, g1 = u % 2, it * U + u + 1
                        pe.wait_ge(s_oh, g1 + 1)
                        pe.wait_ge(s_ohT, g1)
                        transposed(1 - par)
                        pe.wait_ge(s_used, g1 + U - 2)
                        pe.sem_inc(s_taken, 1)
                        for j in range(G):
                            b = blocks[u * G + j]
                            last = look_up(nc, psQ[par][:, j], ohT[:, par, j], E.qA, E.qC, b)
                        last.then_inc(s_q, 1)

            @block.scalar
            def _(act):
                act.sem_inc(s_keys, U)
                with act.Fori(0, n) as it:
                    for u in range(U):
                        par, g1 = u % 2, it * U + u + 1
                        act.wait_ge(s_T, g1)
                        act.wait_ge(s_q, g1)
                        nc.scalar.activation(ohT[:, par], psT[:, :, :], ACT.Copy).then_inc(s_ohT, 1)
                        act.wait_ge(s_in[u], 16 * it + 16)
                        nc.scalar.activation(E.keyS[:, group(it, u)], rows[:, u, :, 2 * B], ACT.Copy)
                        nc.scalar.activation(E.loS[:, group(it, u)], rows[:, u, :, 2 * B + 1], ACT.Copy).then_inc(s_keys, 1)

            @block.vector
            def _(dve):
                link = Link(dve, s_link)

                def onehots(u, par):
                    onehot_twice(nc, E, oh[:, par], rows[:, u, :, 2 * B + 1]).then_inc(s_oh, 1)

                dve.sem_inc(s_used, U)
                nc.vector.memset(E.loS[:, NT:], -1.0)
                link(nc.vector.memset(E.lg0[:, NT:], 0.0))
                for u in (0, 1):
                    dve.wait_ge(s_in[u], 16)
                    onehots(u, u)
                dve.wait_ge(s_T, 1)
                with dve.Fori(0, n) as it:
                    link.loop(1, it, 2 * U)
                    for u in range(U):
                        par, g1 = u % 2, it * U + u + 1
                        dve.wait_ge(s_in[(u + 2) % U], 16 * it + 16 * (1 + (u + 2) // U))
                        onehots((u + 2) % U, par)
                        dve.wait_ge(s_q, g1 + 2)
                        link(nc.vector.tensor_tensor(prod[:, par], rows[:, u, :, 0:B], psQ[par][:, :, 0:B], ALU.mult))
                        link(nc.vector.tensor_reduce(dot[:, par], prod[:, par].rearrange("p t (h j) -> p t h j", h=H),
                                                     AXX, ALU.add))
                        nc.vector.tensor_tensor(E.lg0[:, group(it, u), :], dot[:, par], psQ[par][:, :, B:],
                                                ALU.add).then_inc(s_used, 1)
                    assert link.n == 2 * U, link.n


def phase_softmax(nc, E, sem, n, lg, key, H, sums):
    NT = E.NT
    Q = NT // 4
    with ExitStack() as st:
        def tmp(name, shape, dt=F32):
            return st.enter_context(nc.sbuf_tensor(n + name, shape, dt))

        def pst(name, shape):
            return banks(nc, st, n + name, shape)

        X = tmp("X", [Q, 4, H, P])
        up = tmp("up", [Q, 4, H, P])
        down = tmp("down", [Q, 4, H, P])
        K = tmp("K", [Q, 4, P])
        Rup = tmp("Rup", [Q, 4, P])
        Rdown = tmp("Rdown", [Q, 4, P])
        ends = tmp("ends", [H, 4, NT])
        same = tmp("same", [H, 4, NT])
        run = tmp("run", [H, 2, NT])
        carry = tmp("carry", [H, 2, NT])
        cq = tmp("cq", [Q, 2, 4, H])
        psX = [pst("psX0", [Q, P * 4]), pst("psX1", [Q, P * 4])]
        psE = [pst(f"psE{k}", [H, NT]) for k in range(4)]
        psMt = [pst("psMt0", [P, 4 * Q]), pst("psMt1", [P, 4 * Q])]
        psC = psMt[1][0:Q, 0:2 * 4 * H]
        s_X, s_Xc, s_link, s_ends, s_E, s_carry, s_C, s_M, s_Mt, s_sub = (
            sem(n + k) for k in ("X", "Xc", "link", "ends", "E", "carry", "C", "M", "Mt", "sub"))
        HX = -(-H // 4)
        steps = [(c, k) for c in range(4) for k in range(HX + 1)]
        with nc.Block() as block:
            @block.tensor
            def _(pe):
                for i, (c, k) in enumerate(steps):
                    if i >= 2:
                        pe.wait_ge(s_Xc, i - 1)
                    if k < HX:
                        for h in range(4):
                            last = nc.tensor.matmul(psX[i % 2][:, h * P:(h + 1) * P], lg[:, c * Q:(c + 1) * Q, 4 * k + h],
                                                    E.ident[:, :], start=True, stop=True)
                    else:
                        last = nc.tensor.matmul(psX[i % 2][:, 0:P], key[:, c * Q:(c + 1) * Q], E.ident[:, :],
                                                start=True, stop=True)
                    last.then_inc(s_X, 1)
                pe.wait_ge(s_ends, 1)
                I = E.ident[0:Q, 0:Q]
                for c in range(4):
                    for k, src in enumerate((up[:, c, :, P - 1], down[:, c, :, 0], bc(K[:, c, 0:1], [Q, H]),
                                             bc(K[:, c, P - 1:P], [Q, H]))):
                        last = nc.tensor.matmul(psE[k][:, c * Q:(c + 1) * Q], src, I, start=True, stop=True)
                last.then_inc(s_E, 1)
                pe.wait_ge(s_carry, 1)
                for k in (0, 1):
                    for c in range(4):
                        last = nc.tensor.matmul(psC[:, (k * 4 + c) * H:(k * 4 + c + 1) * H], carry[:, k, c * Q:(c + 1) * Q],
                                                E.ident[0:H, 0:H], start=True, stop=True)
                last.then_inc(s_C, 1)
                pe.wait_ge(s_M, 1)
                for i, (c, k) in enumerate((c, k) for c in range(4) for k in range(HX)):
                    if i >= 2:
                        pe.wait_ge(s_sub, i - 1)
                    for h in range(4):
                        last = nc.tensor.matmul(psMt[i % 2][:, h * Q:(h + 1) * Q], up[:, c, 4 * k + h], I,
                                                start=True, stop=True)
                    last.then_inc(s_Mt, 1)

            @block.vector
            def _(dve):
                link = Link(dve, s_link)
                for i, (c, k) in enumerate(steps):
                    dve.wait_ge(s_X, i + 1)
                    if k < HX:
                        nc.vector.tensor_copy(X[:, c, 4 * k:4 * k + 4], psX[i % 2].rearrange("p (h e) -> p h e", h=4)).then_inc(s_Xc, 1)
                    else:
                        nc.vector.tensor_copy(K[:, c], psX[i % 2][:, 0:P]).then_inc(s_Xc, 1)
                dve.wait_ge(s_Xc, len(steps))
                nc.vector.memset(Rup[:, :, 0:1], 0.0)
                nc.vector.memset(Rdown[:, :, P - 1:P], 0.0)
                for c in range(4):
                    last = nc.vector.tensor_tensor(Rup[:, c, 1:P], K[:, c, 1:P], K[:, c, 0:P - 1], ALU.is_equal)
                link(last)
                link(nc.vector.tensor_scalar(Rup[:, :, 1:P], Rup[:, :, 1:P], FAR, -FAR, ALU.mult, ALU.add))
                link(nc.vector.tensor_copy(Rdown[:, :, 0:P - 1], Rup[:, :, 1:P]))
                for c in range(4):
                    for h in range(H):
                        nc.vector.tensor_tensor_scan(up[:, c, h], Rup[:, c], X[:, c, h], -FAR, ALU.add, ALU.max)
                        last = nc.vector.tensor_tensor_scan(down[:, c, h, ::-1], Rdown[:, c, ::-1], X[:, c, h, ::-1],
                                                            -FAR, ALU.add, ALU.max)
                last.then_inc(s_ends, 1)
                dve.wait_ge(s_E, 1)
                for k in range(4):
                    nc.vector.tensor_copy(ends[:, k], psE[k][:, :])
                link(nc.vector.memset(carry[:, :, :], -FAR))
                first, final = ends[:, 2], ends[:, 3]
                link(nc.vector.tensor_tensor(same[:, 0, 1:NT], first[:, 1:NT], final[:, 0:NT - 1], ALU.is_equal))
                link(nc.vector.tensor_tensor(same[:, 1], first, final, ALU.is_equal))
                link(nc.vector.memset(same[:, 2:4], -FAR))
                link(nc.vector.memset(same[:, 0, 0:1], 0.0))
                link(nc.vector.tensor_tensor(same[:, 2, 1:NT], same[:, 0, 1:NT], same[:, 1, 1:NT], ALU.mult))
                link(nc.vector.tensor_tensor(same[:, 3, 0:NT - 1], same[:, 0, 1:NT], same[:, 1, 0:NT - 1], ALU.mult))
                link(nc.vector.tensor_scalar(same[:, 0], same[:, 0], FAR, -FAR, ALU.mult, ALU.add))
                link(nc.vector.tensor_scalar(same[:, 2, 1:NT], same[:, 2, 1:NT], FAR, -FAR, ALU.mult, ALU.add))
                link(nc.vector.tensor_scalar(same[:, 3, 0:NT - 1], same[:, 3, 0:NT - 1], FAR, -FAR, ALU.mult, ALU.add))
                link(nc.vector.tensor_tensor_scan(run[:, 0], same[:, 2], ends[:, 0], -FAR, ALU.add, ALU.max))
                link(nc.vector.tensor_tensor_scan(run[:, 1, ::-1], same[:, 3, ::-1], ends[:, 1, ::-1], -FAR, ALU.add, ALU.max))
                nc.vector.tensor_tensor(carry[:, 0, 1:NT], run[:, 0, 0:NT - 1], same[:, 0, 1:NT], ALU.add)
                nc.vector.tensor_tensor(carry[:, 1, 0:NT - 1], run[:, 1, 1:NT], same[:, 0, 1:NT], ALU.add).then_inc(s_carry, 1)
                dve.wait_ge(s_C, 1)
                link(nc.vector.tensor_copy(cq[:, :, :, :].rearrange("p k c h -> p (k c h)"), psC))
                for c in range(4):
                    nc.vector.tensor_scalar(Rup[:, c], K[:, c], K[:, c, 0:1], None, ALU.is_equal)
                    link(nc.vector.tensor_scalar(Rdown[:, c], K[:, c], K[:, c, P - 1:P], None, ALU.is_equal))
                link(nc.vector.tensor_scalar(Rup[:, :, :], Rup[:, :, :], FAR, -FAR, ALU.mult, ALU.add))
                link(nc.vector.tensor_scalar(Rdown[:, :, :], Rdown[:, :, :], FAR, -FAR, ALU.mult, ALU.add))
                for k, (R, m) in enumerate(((Rup, up), (Rdown, down))):
                    for c in range(4):
                        for h in range(H):
                            last = nc.vector.scalar_tensor_tensor(m[:, c, h], R[:, c], cq[:, k, c, h:h + 1], m[:, c, h],
                                                                  ALU.add, ALU.max)
                link(last)
                nc.vector.tensor_tensor(up[:, :, :, :], up[:, :, :, :], down[:, :, :, :], ALU.max).then_inc(s_M, 1)
                for i, (c, k) in enumerate((c, k) for c in range(4) for k in range(HX)):
                    dve.wait_ge(s_Mt, i + 1)
                    v = lg[:, c * Q:(c + 1) * Q, 4 * k:4 * k + 4]
                    nc.vector.tensor_tensor(v, v, psMt[i % 2].rearrange("p (h q) -> p q h", h=4), ALU.subtract).then_inc(s_sub, 1)

            @block.scalar
            def _(act):
                act.wait_ge(s_sub, 4 * HX)
                nc.scalar.activation(lg[:, 0:NT, :], lg[:, 0:NT, :], ACT.Exp)

            @block.gpsimd
            def _(pool):
                nc.gpsimd.memset(sums, 0.0)


def phase_sum0(nc, E, sem):
    NT, RS, H = E.NT, E.RS, 4
    V = B + H
    with ExitStack() as st:
        def tmp(name, shape, dt):
            return st.enter_context(nc.sbuf_tensor(name, shape, dt))

        rows = tmp("a0_rows", [P, U, G, RS], F32)
        oh = tmp("a0_oh", [P, 2, G, B], F32)
        val = tmp("a0_val", [P, 2, G, V], F32)
        psA = [banks(nc, st, f"a0_ps{k}", [V, G, B]) for k in (0, 1)]
        s_in = [sem(f"a0_in{u}") for u in range(U)]
        s_link, s_val, s_sum, s_acc = (sem("a0_" + k) for k in ("link", "val", "sum", "acc"))
        n = NT // (U * G)
        ss = E.ss.rearrange("p (t f) -> p t f", f=RS)
        with nc.Block() as block:
            @block.sync
            def _(sp):
                with sp.Fori(0, n) as it:
                    for u in range(U):
                        sp.wait_ge(s_val, it * U + u + 1)
                        sp.dma_start(rows[:, u], ss[:, bass.ds(it * (U * G) + u * G, G), :]).then_inc(s_in[u], 16)
                sp.wait_ge(s_val, U * (n - 1) + 1 + U)
                sp.dma_start(rows[:, 0], ss[:, 0:G, :]).then_inc(s_in[0], 16)
                sp.wait_ge(s_val, U * (n - 1) + 2 + U)
                sp.dma_start(rows[:, 1], ss[:, G:2 * G, :]).then_inc(s_in[1], 16)
                for u in range(U):
                    sp.wait_ge(s_in[u], 16 * n + 16 * (u < 2))

            @block.tensor
            def _(pe):
                with pe.Fori(0, n) as it:
                    for u in range(U):
                        par, g1 = u % 2, it * U + u + 1
                        pe.wait_ge(s_val, g1 + U)
                        pe.wait_ge(s_acc, g1)
                        for j in range(G):
                            last = nc.tensor.matmul(psA[par][:, j], val[:, par, j], oh[:, par, j], start=True, stop=True)
                        last.then_inc(s_sum, 1)

            @block.vector
            def _(dve):
                dve.sem_inc(s_val, U)
                dve.sem_inc(s_acc, 2)

                def products(tile0, u, par, loaded):
                    dve.wait_ge(s_in[u], loaded)
                    nc.vector.tensor_tensor(val[:, par, :, 0:B].rearrange("p t (h j) -> p t h j", h=H),
                                            rows[:, u, :, B:2 * B].rearrange("p t (h j) -> p t h j", h=H),
                                            bc(E.lg0[:, bass.ds(tile0, G), :][:, :, :, None], [P, G, H, B // H]),
                                            ALU.mult).then_inc(s_val, 1)

                for u in (0, 1):
                    onehot(nc, E, oh[:, u], E.loS, u * G)
                    nc.vector.tensor_copy(val[:, u, :, B:], E.lg0[:, u * G:(u + 1) * G, :])
                    products(u * G, u, u, 16)
                with dve.Fori(0, n) as it:
                    blocks = blocks_of(nc, DVE, E.blkS, it, E.NB, U)
                    for u in range(U):
                        par, g1 = u % 2, it * U + u + 1
                        dve.wait_ge(s_sum, g1)
                        ahead = it * (U * G) + (u + 2) * G
                        for j in range(G):
                            b = blocks[u * G + j]
                            a = E.acc0[:, bass.ds(b * B, B)]
                            ins = nc.vector.tensor_tensor(a, a, psA[par][:, j], ALU.add)
                            if j == G - 1:
                                ins.then_inc(s_acc, 1)
                                continue
                            ins.then_inc(s_link, 1)
                            if j == 0:
                                onehot(nc, E, oh[:, par], E.loS, ahead)
                            elif j == 1:
                                nc.vector.tensor_copy(val[:, par, :, B:], E.lg0[:, bass.ds(ahead, G), :])
                            else:
                                products(ahead, (u + 2) % U, par, 16 * it + 16 * (1 + (u + 2) // U))
                            dve.wait_ge(s_link, (it * U + u) * (G - 1) + j + 1)
                        dve.wait_ge(s_acc, g1 + 2)


def row(v):
    return v.rearrange("(p c) -> p c", p=1)


def col(v, p):
    return v.rearrange("(c p) -> p c", p=p)


def phase_nodes1(nc, E, a, sem):
    N, NB = E.N, E.NB
    CW = NC * B
    H = 4
    H1 = 8
    with ExitStack() as st:
        def tmp(name, shape, dt=F32):
            return st.enter_context(nc.sbuf_tensor("n1_" + name, shape, dt))

        def pst(name, shape):
            return banks(nc, st, "n1_" + name, shape)

        sq = tmp("sq", [B, NB, B])
        h1 = tmp("h1", [B, NB, B + H1])
        s = tmp("s", [B, 2, NB])
        sel = tmp("sel", [B + H, B])
        cen = tmp("cen", [B, P])
        outw = tmp("outw", [B, B])
        rows = tmp("rows", [1, 2, B])
        lnrow = tmp("lnrow", [B, 2, B])
        cols = tmp("cols", [B, 2])
        fcw = tmp("fcw", [B, H1, B])
        attn = tmp("attn", [H1, 2, B])
        attnT = tmp("attnT", [B, 2, H1])
        WLR = tmp("WLR", [B, 2 * H1])
        Sb = tmp("Sb", [B, CW])
        r = tmp("r", [B, CW])
        z = tmp("z", [B, NB * B])
        soft = tmp("soft", [B, NB * B])
        ssp = tmp("ssp", [B, CW])
        hs = tmp("hs", [B, NC, B])
        hTs = tmp("hTs", [B, CW])
        psS = pst("psS", [B, CW])
        psO = pst("psO", [P, CW])
        psY = pst("psY", [B, NC, B])
        psT = pst("psT", [B, CW])
        psA = pst("psA", [B, 2 * H1])
        psL = pst("psL", [B, 2 * H1])
        psE = pst("psE", [B, NC, 2 * H1])
        names = ("zero", "in", "link", "S", "G", "O", "z", "act", "soft", "ssp", "Y", "y", "var", "sd", "h", "at", "atc",
                 "L", "w", "hs", "T", "Tc", "E", "Ec", "b", "bc", "out", "taken", "x")
        (s_zero, s_in, s_link, s_S, s_G, s_O, s_z, s_act, s_soft, s_ssp, s_Y, s_y, s_var, s_sd, s_h, s_at, s_atc,
         s_L, s_w, s_hs, s_T, s_Tc, s_E, s_Ec, s_b, s_bc, s_out, s_taken, s_x) = (sem("n1_" + k) for k in names)
        s_fill, s_Sb = sem("n1_fill"), sem("n1_Sb")
        loads = 1 + 1 + 1 + 2 + H + 1 + 1 + 2
        n = NB // NC
        with nc.Block() as block:
            @block.sync
            def _(sp):
                sp.wait_ge(s_fill, 1)
                load_nodes(sp, E.x1, a["x"], N, s_x)
                sp.dma_start(cen[:, 0:B], a["L0_gnn_cen_w"]).then_inc(s_in, 16)
                sp.dma_start(outw[:, :], a["L0_gnn_out_w"]).then_inc(s_in, 16)
                sp.dma_start(rows[:, 0], row(a["L0_gnn_out_b"])).then_inc(s_in, 16)
                for k, v in enumerate(("L0_gnn_ln_g", "L0_gnn_ln_b")):
                    sp.dma_start(lnrow[:, k], bc(row(a[v]), [B, B])).then_inc(s_in, 16)
                for h in range(H):
                    sp.dma_start(cols[16 * h:16 * h + 16, 0:1], col(a["L0_gnn_wvl_b"], 16)).then_inc(s_in, 16)
                sp.dma_start(cols[:, 1:2], col(a["L0_gnn_cen_b"], B)).then_inc(s_in, 16)
                sp.dma_start(fcw[:, :, :], a["L1_gnn_fc_w"].rearrange("(h o) c -> o h c", h=H1)).then_inc(s_in, 16)
                for k, v in enumerate(("L1_gnn_attn_l", "L1_gnn_attn_r")):
                    sp.dma_start(attn[:, k], a[v]).then_inc(s_in, 16)
                sp.wait_ge(s_in, 16 * loads)
                sp.wait_ge(s_h, 2)
                sp.dma_start(E.table1.rearrange("(b p) c -> p b c", p=B), h1[:, :, :]).then_inc(s_out, 16)
                sp.wait_ge(s_out, 16)
                sp.wait_ge(s_x, 32)

            @block.gpsimd
            def _(pool):
                nc.gpsimd.memset(sel[:, :], 0.0).then_inc(s_zero, 1)
                pool.wait_ge(s_zero, 1)
                nc.gpsimd.affine_select(out=sel[:, :].rearrange("p (h j) -> p h j", h=H),
                                        in_=sel[:, :].rearrange("p (h j) -> p h j", h=H),
                                        pattern=[[-1, H], [0, B // H]], compare_op=ALU.not_equal, fill=1.0,
                                        base=-B, channel_multiplier=1).then_inc(s_zero, 1)

            @block.tensor
            def _(pe):
                I = E.ident[0:B, 0:B]
                pe.wait_ge(s_zero, 2)
                pe.wait_ge(s_in, 16 * loads)
                nc.tensor.matmul(psA[0:1, 0:1], E.ones[:, 0:1], E.ones[:, 0:1], start=True, stop=True)
                for k in (0, 1):
                    last = nc.tensor.matmul(psA[:, k * H1:(k + 1) * H1], attn[:, k], E.ident[0:H1, 0:H1], start=True, stop=True)
                last.then_inc(s_at, 1)
                pe.wait_ge(s_atc, 1)
                for k in (0, 1):
                    for h in range(H1):
                        last = nc.tensor.matmul(psL[:, k * H1 + h:k * H1 + h + 1], fcw[:, h], attnT[:, k, h:h + 1],
                                                start=True, stop=True)
                last.then_inc(s_L, 1)
                nc.tensor.matmul(psY[0:1, 0, :], E.ones[0:B, 0:1], outw[:, :], start=True, stop=True).then_inc(s_b, 1)
                pe.wait_ge(s_bc, 1)

                def denominators(ds):
                    nc.tensor.matmul(psS[:, :], sel[:, :], E.acc0[:, ds], start=True, stop=True).then_inc(s_S, 1)

                def outputs(c):
                    ds = bass.ds(c * CW, CW)
                    pe.wait_ge(s_G, c + 1)
                    pe.wait_ge(s_z, c + 1)
                    pe.sem_inc(s_taken, 1)
                    nc.tensor.matmul(psO[:, :], E.wvl[:, :], E.acc0[0:B, ds], start=True, stop=False)
                    nc.tensor.matmul(psO[:, :], cen[:, :], E.h0T[:, ds], start=False, stop=True).then_inc(s_O, 1)

                denominators(bass.ds(0, CW))
                with pe.Fori(0, n - 1) as c:
                    pe.wait_ge(s_Sb, c + 1)
                    pe.sem_inc(s_taken, 1)
                    denominators(bass.ds(c * CW + CW, CW))
                    outputs(c)
                outputs(n - 1)
                with pe.Fori(0, n) as c:
                    pe.wait_ge(s_ssp, c + 1)
                    pe.wait_ge(s_y, c + 1)
                    pe.sem_inc(s_taken, 1)
                    for j in range(NC):
                        nc.tensor.matmul(psY[:, j], ssp[:, j * B:(j + 1) * B], outw[:, :], start=True, stop=False)
                        last = nc.tensor.matmul(psY[:, j], E.ones[0:1, 0:B], rows[:, 1], start=False, stop=True)
                    last.then_inc(s_Y, 1)
                with pe.Fori(0, n) as c:
                    pe.wait_ge(s_hs, c + 1)
                    pe.sem_inc(s_taken, 1)
                    for j in range(NC):
                        last = nc.tensor.matmul(psT[:, j * B:(j + 1) * B], hs[:, j], I, start=True, stop=True)
                    last.then_inc(s_T, 1)
                    pe.wait_ge(s_Tc, c + 1)
                    pe.wait_ge(s_Ec, c + 1)
                    pe.sem_inc(s_taken, 1)
                    for j in range(NC):
                        last = nc.tensor.matmul(psE[:, j], hTs[:, j * B:(j + 1) * B], WLR[:, :], start=True, stop=True)
                    last.then_inc(s_E, 1)

            @block.scalar
            def _(act):
                act.wait_ge(s_in, 16 * loads)
                act.sem_inc(s_y, 1)
                act.wait_ge(s_z, n + 1)
                nc.scalar.activation(soft[:, :], z[:, :], ACT.Abs, bias=cols[:, 1:2]).then_inc(s_act, 1)
                act.wait_ge(s_act, 1)
                nc.scalar.activation(soft[:, :], soft[:, :], ACT.Exp, scale=-1.0).then_inc(s_act, 1)
                nc.scalar.activation(z[:, :], z[:, :], ACT.Relu, bias=cols[:, 1:2])
                act.wait_ge(s_act, 2)
                nc.scalar.activation(soft[:, :], soft[:, :], ACT.Ln, bias=1.0).then_inc(s_soft, 1)
                with act.Fori(0, n) as c:
                    act.wait_ge(s_Y, c + 2)
                    nc.scalar.activation(h1[:, bass.ds(c * NC, NC), 0:B], psY[:, :, :], ACT.Copy).then_inc(s_y, 1)
                for k in (1, 2):
                    act.wait_ge(s_var, k)
                    nc.scalar.activation(s[:, 1], s[:, 1], ACT.Sqrt).then_inc(s_sd, 1)
                act.wait_ge(s_h, 1)
                with act.Fori(0, n) as c:
                    nc.scalar.activation(hs[:, :, :], h1[:, bass.ds(c * NC, NC), 0:B], ACT.Copy).then_inc(s_hs, 1)
                    act.wait_ge(s_T, c + 1)

            @block.vector
            def _(dve):
                link = Link(dve, s_link)
                nc.vector.memset(E.x1[:, NB - 1], 0.0)
                nc.vector.memset(cen[:, :], 0.0).then_inc(s_fill, 1)
                dve.wait_ge(s_at, 1)
                nc.vector.tensor_copy(attnT[:, :, :].rearrange("p k h -> p (k h)"), psA[:, :]).then_inc(s_atc, 1)
                dve.wait_ge(s_L, 1)
                nc.vector.tensor_copy(WLR[:, :], psL[:, :]).then_inc(s_w, 1)
                dve.wait_ge(s_b, 1)
                nc.vector.scalar_tensor_tensor(rows[:, 1], psY[0:1, 0, :], -float(np.log(2.0)), rows[:, 0],
                                               ALU.mult, ALU.add).then_inc(s_bc, 1)
                dve.sem_inc(s_z, 1)

                def normal(c):
                    ds = bass.ds(c * CW, CW)
                    dve.wait_ge(s_S, c + 1)
                    nc.vector.tensor_copy(Sb[:, :], psS[:, :]).then_inc(s_Sb, 1)
                    dve.wait_ge(s_Sb, c + 1)
                    link(nc.vector.tensor_scalar(r[:, :], Sb[:, :], 1e-16, None, ALU.add))
                    link(nc.vector.reciprocal(r[:, :], r[:, :]))
                    nc.vector.tensor_tensor(E.acc0[0:B, ds], E.acc0[0:B, ds], r[:, :], ALU.mult).then_inc(s_G, 1)
                    link(nc.vector.scalar_tensor_tensor(z[:, ds], Sb[:, :], cols[:, 0:1], r[:, :], ALU.mult, ALU.mult))

                def add(c):
                    ds = bass.ds(c * CW, CW)
                    dve.wait_ge(s_O, c + 1)
                    nc.vector.tensor_tensor(z[:, ds], z[:, ds], psO[0:B, :], ALU.add).then_inc(s_z, 1)

                normal(0)
                with dve.Fori(0, n - 1) as c:
                    link.loop(3, c, 3)
                    normal(c + 1)
                    add(c)
                link.loop(3, n - 1, 3)
                add(n - 1)
                dve.wait_ge(s_soft, 1)
                dve.sem_inc(s_Y, 1)
                with dve.Fori(0, n) as c:
                    ds = bass.ds(c * CW, CW)
                    dve.wait_ge(s_Y, c + 1)
                    nc.vector.tensor_tensor(ssp[:, :], soft[:, ds], z[:, ds], ALU.add).then_inc(s_ssp, 1)
                dve.wait_ge(s_y, n + 1)
                dve.wait_ge(s_x, 32)
                y = h1[:, :, 0:B]
                layernorm(nc, dve, link, y, s, sq[:, :, :], s_var, s_sd, 1)
                link(nc.vector.tensor_tensor(y, y, bc(lnrow[:, 0][:, None, :], [B, NB, B]), ALU.mult))
                link(nc.vector.tensor_tensor(y, y, bc(lnrow[:, 1][:, None, :], [B, NB, B]), ALU.add))
                link(nc.vector.tensor_tensor(E.x1[:, :, :], E.x1[:, :, :], y, ALU.add))
                link(nc.vector.tensor_copy(y, E.x1[:, :, :]))
                layernorm(nc, dve, link, y, s, sq[:, :, :], s_var, s_sd, 2)
                nc.vector.tensor_scalar(y, y, 0.0, None, ALU.max).then_inc(s_h, 1)
                dve.sem_inc(s_Ec, 1)
                with dve.Fori(0, n) as c:
                    dve.wait_ge(s_T, c + 1)
                    nc.vector.tensor_copy(hTs[:, :], psT[:, :]).then_inc(s_Tc, 1)
                    dve.wait_ge(s_E, c + 1)
                    nc.vector.tensor_copy(h1[:, bass.ds(c * NC, NC), B:B + H1], psE[:, :, 0:H1])
                    nc.vector.tensor_copy(E.ertab[:, bass.ds(c * NC, NC), :], psE[:, :, H1:]).then_inc(s_Ec, 1)
                dve.wait_ge(s_Ec, n + 1)
                dve.sem_inc(s_h, 1)


def phase_gather1(nc, E, sem):
    NT, H, W = E.NT, 8, B + 8
    with ExitStack() as st:
        def tmp(name, shape, dt=F32):
            return st.enter_context(nc.sbuf_tensor("g1_" + name, shape, dt))

        g = tmp("g", [P, 2, G, W])
        idx = tmp("idx", [P, 2, G], I32)
        oh = tmp("oh", [P, 2, G, B])
        ohT = tmp("ohT", [B, 2, G, P])
        sum_ = tmp("sum", [P, G, H])
        psT = banks(nc, st, "g1_psT", [B, G, P])
        psR = banks(nc, st, "g1_psR", [P, G, H])
        s_g = [sem("g1_g0"), sem("g1_g1")]
        s_st = [sem("g1_st0"), sem("g1_st1")]
        s_oh, s_T, s_ohT, s_r, s_lg, s_link, s_free, s_taken, s_taken2 = (
            sem("g1_" + k) for k in ("oh", "T", "ohT", "r", "lg", "link", "free", "taken", "taken2"))
        n = NT // (2 * G)
        hd = E.hg.rearrange("p (t f) -> p t f", f=W)
        with nc.Block() as block:
            @block.gpsimd
            def _(pool):
                with pool.Fori(0, n) as it:
                    for par in (0, 1):
                        pool.wait_ge(s_oh, upto(it, par))
                        pool.wait_ge(s_free, upto(it, par))
                        pool.wait_ge(s_lg, upto(it, par))
                        pool.sem_inc(s_taken2, 1)
                        for j in range(G):
                            nc.gpsimd.indirect_dma_start(
                                out=g[:, par, j, :], out_offset=None, in_=E.table1,
                                in_offset=bass.IndirectOffsetOnAxis(ap=idx[:, par, j:j + 1], axis=0)).then_inc(s_g[par], 16)
                for par in (0, 1):
                    pool.wait_ge(s_g[par], 64 * n)

            @block.sync
            def _(sp):
                sp.sem_inc(s_free, 1)
                sp.dma_start(E.hg[0:1, 0:W], E.table1[0:1, :]).then_inc(s_st[1], 16)
                with sp.Fori(0, n) as it:
                    for par in (0, 1):
                        sp.wait_ge(s_st[1 - par], it * 16 + 16)
                        sp.sem_inc(s_free, 1)
                        sp.wait_ge(s_g[par], it * 64 + 64)
                        sp.dma_start(hd[:, tiles(it, par), :], g[:, par]).then_inc(s_st[par], 16)
                sp.wait_ge(s_st[0], 16 * n)
                sp.wait_ge(s_st[1], 16 * n + 16)

            @block.tensor
            def _(pe):
                with pe.Fori(0, n) as it:
                    blocks = blocks_of(nc, PE, E.blkD, it, E.NB)
                    for par in (0, 1):
                        g1 = upto(it, par)
                        pe.wait_ge(s_oh, g1)
                        pe.wait_ge(s_ohT, g1)
                        for j in range(G):
                            last = nc.tensor.matmul(psT[:, j], oh[:, par, j], E.ident[:, :], start=True, stop=True)
                        last.then_inc(s_T, 1)
                        pe.wait_ge(s_ohT, g1 + 1)
                        pe.wait_ge(s_lg, g1 + 1)
                        pe.sem_inc(s_taken, 1)
                        for j in range(G):
                            b = blocks[par * G + j]
                            last = nc.tensor.matmul(psR[:, j], ohT[:, par, j], E.ertab[:, bass.ds(b, 1), :],
                                                    start=True, stop=True)
                        last.then_inc(s_r, 1)

            @block.scalar
            def _(act):
                act.sem_inc(s_ohT, 1)
                with act.Fori(0, n) as it:
                    for par in (0, 1):
                        act.wait_ge(s_T, upto(it, par))
                        nc.scalar.activation(ohT[:, par], psT[:, :, :], ACT.Copy).then_inc(s_ohT, 1)

            @block.vector
            def _(dve):
                link = Link(dve, s_link)
                dve.sem_inc(s_lg, 2)

                def onehots(tile0, par):
                    sl = bass.ds(tile0, G)
                    nc.vector.tensor_copy(idx[:, par], E.srcI[:, sl])
                    nc.vector.tensor_tensor(oh[:, par], bc(E.iota[:, None, 0:B], [P, G, B]),
                                            bc(E.loD[:, sl][:, :, None], [P, G, B]), ALU.is_equal).then_inc(s_oh, 1)

                nc.vector.memset(E.lg1[:, NT:], 0.0)
                onehots(0, 0)
                with dve.Fori(0, n) as it:
                    link.loop(0, it, 2)
                    for par in (0, 1):
                        if par == 1:
                            dve.wait_ge(s_g[0], it * 64 + 64)
                        else:
                            dve.wait_ge(s_oh, it * 2 + 1)
                        onehots(it * (2 * G) + (par + 1) * G, 1 - par)
                        dve.wait_ge(s_r, upto(it, par))
                        dve.wait_ge(s_g[par], it * 64 + 64)
                        link(nc.vector.tensor_tensor(sum_[:, :, :], g[:, par, :, B:], psR[:, :, :], ALU.add))
                        nc.vector.scalar_tensor_tensor(E.lg1[:, tiles(it, par), :], sum_[:, :, :], 0.2, sum_[:, :, :],
                                                       ALU.mult, ALU.max).then_inc(s_lg, 1)
                    assert link.n == 2


def phase_sum1(nc, E, sem):
    NT, H, W = E.NT, 8, B + 8
    with ExitStack() as st:
        def tmp(name, shape, dt=F32):
            return st.enter_context(nc.sbuf_tensor("a1_" + name, shape, dt))

        rows = tmp("rows", [P, 2, G, W])
        oh = tmp("oh", [P, 2, G, B])
        val = tmp("val", [P, 2, G, 5, P])
        psA = [[banks(nc, st, f"a1_ps{k}{j}", [P, 5, B]) for j in range(G)] for k in (0, 1)]
        s_in = [sem("a1_in0"), sem("a1_in1")]
        s_link, s_ez, s_val, s_valA, s_valP, s_sum, s_acc = (
            sem("a1_" + k) for k in ("link", "ez", "val", "valA", "valP", "sum", "acc"))
        n = NT // (2 * G)
        hd = E.hg.rearrange("p (t f) -> p t f", f=W)
        of_act, of_pool = (2,), (3,)
        of_dve = tuple(j for j in range(G) if j not in of_act + of_pool)

        def product(par, j):
            return (val[:, par, j, 0:4].rearrange("p k (h c) -> p (k h) c", h=2), bc(rows[:, par, j, None, 0:B], [P, H, B]),
                    bc(val[:, par, j, 4, 0:H][:, :, None], [P, H, B]))

        with nc.Block() as block:
            @block.sync
            def _(sp):
                with sp.Fori(0, n) as it:
                    for par in (0, 1):
                        sp.wait_ge(s_val, upto(it, par))
                        sp.wait_ge(s_valA, upto(it, par))
                        sp.wait_ge(s_valP, upto(it, par))
                        sp.dma_start(rows[:, par], hd[:, tiles(it, par), :]).then_inc(s_in[par], 16)
                for s in (s_val, s_valA, s_valP):
                    sp.wait_ge(s, 2 * n + 1)
                sp.dma_start(rows[:, 0], hd[:, 0:G, :]).then_inc(s_in[0], 16)
                sp.wait_ge(s_in[0], 16 * n + 16)
                sp.wait_ge(s_in[1], 16 * n)

            @block.tensor
            def _(pe):
                def sums(par, j):
                    for k in range(4):
                        nc.tensor.matmul(psA[par][j][:, k], val[:, par, j, k], oh[:, par, j], start=True, stop=True)
                    return nc.tensor.matmul(psA[par][j][0:H, 4], val[:, par, j, 4, 0:H], oh[:, par, j], start=True, stop=True)

                with pe.Fori(0, n) as it:
                    for par in (0, 1):
                        g1 = upto(it, par)
                        pe.wait_ge(s_val, g1 + 2)
                        pe.wait_ge(s_acc, g1)
                        for j in of_dve:
                            sums(par, j)
                        pe.wait_ge(s_valA, g1 + 2)
                        pe.wait_ge(s_valP, g1 + 2)
                        for j in of_act + of_pool:
                            last = sums(par, j)
                        last.then_inc(s_sum, 1)

            @block.scalar
            def _(act):
                def values(par, ez, loaded):
                    act.wait_ge(s_ez, ez)
                    act.wait_ge(s_in[par], loaded)
                    for j in of_act:
                        for h in range(H):
                            last = nc.scalar.activation(val[:, par, j, h // 2, (h % 2) * B:(h % 2 + 1) * B],
                                                        rows[:, par, j, 0:B], ACT.Copy,
                                                        scale=val[:, par, j, 4, h:h + 1])
                    last.then_inc(s_valA, 1)

                act.sem_inc(s_valA, 2)
                with act.Fori(0, n) as it:
                    for par in (0, 1):
                        values(par, upto(it, par), 16 * it + 16)
                values(0, 2 * n + 1, 16 * n + 16)

            @block.gpsimd
            def _(pool):
                def values(par, ez, loaded):
                    pool.wait_ge(s_ez, ez)
                    pool.wait_ge(s_in[par], loaded)
                    for j in of_pool:
                        out, h, e = product(par, j)
                        last = nc.gpsimd.tensor_tensor(out, h, e, ALU.mult)
                    last.then_inc(s_valP, 1)

                pool.sem_inc(s_valP, 2)
                with pool.Fori(0, n) as it:
                    for par in (0, 1):
                        values(par, upto(it, par), 16 * it + 16)
                values(0, 2 * n + 1, 16 * n + 16)

            @block.vector
            def _(dve):
                link = Link(dve, s_link)
                dve.sem_inc(s_val, 2)
                dve.sem_inc(s_acc, 2)

                def values(tile0, par, free, loaded):
                    if free is not None:
                        dve.wait_ge(s_sum, free)
                    sl = bass.ds(tile0, G)
                    nc.vector.tensor_copy(val[:, par, :, 4, 0:H], E.lg1[:, sl, :]).then_inc(s_ez, 1)
                    nc.vector.tensor_tensor(oh[:, par], bc(E.iota[:, None, 0:B], [P, G, B]),
                                            bc(E.loD[:, sl][:, :, None], [P, G, B]), ALU.is_equal)
                    dve.wait_ge(s_in[par], loaded)
                    dve.wait_ge(s_ez, free + 1 if free is not None else 1)
                    for j in of_dve:
                        out, h, e = product(par, j)
                        last = nc.vector.tensor_tensor(out, h, e, ALU.mult)
                    last.then_inc(s_val, 1)

                def add(it, par, blocks):
                    dve.wait_ge(s_sum, upto(it, par) + 1)
                    for j in range(G):
                        ds = bass.ds(blocks[par * G + j] * B, B)
                        v, d = E.acc1[:, 0:4, ds], E.acc1[0:H, 4, ds]
                        nc.vector.tensor_tensor(v, v, psA[par][j][:, 0:4], ALU.add)
                        ins = nc.vector.tensor_tensor(d, d, psA[par][j][0:H, 4], ALU.add)
                        if j < G - 1:
                            link(ins)
                        else:
                            ins.then_inc(s_acc, 1)
                    dve.wait_ge(s_acc, upto(it, par) + 2)

                dve.sem_inc(s_sum, 1)
                values(0, 0, None, 16)
                with dve.Fori(0, n) as it:
                    blocks = blocks_of(nc, DVE, E.blkD, it, E.NB)
                    link.loop(0, it, 2 * (G - 1))
                    for par in (0, 1):
                        values(it * (2 * G) + (par + 1) * G, 1 - par, upto(it, par), 16 * it + 16 * (par + 1))
                        add(it, par, blocks)
                    assert link.n == 2 * (G - 1)


def phase_dense1(nc, E, a, out, sem):
    N, NB = E.N, E.NB
    CW = NC * B
    n = NB // NC
    FM = a["L1_gnn_w1"].shape[0] // P
    with ExitStack() as st:
        def tmp(name, shape, dt=F32):
            return st.enter_context(nc.sbuf_tensor("d_" + name, shape, dt))

        def pst(name, shape):
            return banks(nc, st, "d_" + name, shape)

        fcs = tmp("fcs", [B, 8, B])
        FC = tmp("FC", [P, 4, P])
        selR = tmp("selR", [8, 4, P])
        rec = tmp("rec", [8, NB * B])
        rb = tmp("rb", [P, 2, CW])
        w1s = tmp("w1s", [P, 2, 4 * P])
        w1T = tmp("w1T", [P, 4, FM * P])
        w2s = tmp("w2s", [B, FM, P])
        w2T = tmp("w2T", [P, FM, B])
        c1 = tmp("c1", [P, 4, 3])
        bb1 = tmp("bb1", [P, FM])
        c2 = tmp("c2", [B, 3])
        st1 = tmp("st1", [P, 4, n, 6])
        mv1 = tmp("mv1", [P, 4, 2])
        sc1 = tmp("sc1", [P, 4, 3])
        st2 = tmp("st2", [B, n, 6])
        mv2 = tmp("mv2", [B, 2])
        sc2 = tmp("sc2", [B, 3])
        hn = tmp("hn", [P, 4, CW])
        h2 = tmp("h2", [P, 2, CW])
        yT = tmp("yT", [B, NB * B])
        yn = tmp("yn", [B, CW])
        fin = tmp("fin", [B, NC, B])
        pw = [pst(f"ps{k}", [P, BANK]) for k in range(4)]
        ps = [v[:, 0:CW] for v in pw]
        psY = pst("psY", [B, CW])
        psZ = pst("psZ", [B, NC, B])
        names = ("zero", "in", "link", "tp", "tpc", "R", "Rb", "rbc", "Rw", "sd", "sdd", "hn", "h", "h2",
                 "Y", "y", "yn", "Z", "fin", "out", "taken", "rec", "hn1", "bn2")
        (s_zero, s_in, s_link, s_tp, s_tpc, s_R, s_Rb, s_rbc, s_Rw, s_sd, s_sdd, s_hn, s_h, s_h2,
         s_Y, s_y, s_yn, s_Z, s_fin, s_out, s_taken, s_rec, s_hn1, s_bn2) = (sem("d_" + k) for k in names)
        s_w1d = [sem("d_w1d0"), sem("d_w1d1")]
        s_outd, s_fcz = sem("d_outd"), sem("d_fcz")
        loads = 1 + 1 + 3 + 1 + 3
        ntp = FM + 2 + 4
        edge = [CW] * (n - 1) + [N - (n - 1) * CW]
        with nc.Block() as block:
            @block.sync
            def _(sp):
                sp.dma_start(fcs[:, :, :], a["L1_gnn_fc_w"].rearrange("(h o) c -> o h c", h=8)).then_inc(s_in, 16)
                sp.dma_start(w2s[:, :, :], a["L1_gnn_w2"].rearrange("o (m p) -> o m p", p=P)).then_inc(s_in, 16)
                for k, v in enumerate(("L1_gnn_gat_bias", "L1_gnn_bn1_gamma", "L1_gnn_bn1_beta")):
                    sp.dma_start(c1[:, :, k:k + 1], a[v].rearrange("(k p c) -> p k c", p=P, c=1),
                                 allow_slow_non_contiguous=True).then_inc(s_in, 16)
                sp.dma_start(bb1[:, :, None], a["L1_gnn_b1"].rearrange("(k p c) -> p k c", p=P, c=1),
                                 allow_slow_non_contiguous=True).then_inc(s_in, 16)
                for k, v in enumerate(("L1_gnn_b2", "L1_gnn_bn2_gamma", "L1_gnn_bn2_beta")):
                    sp.dma_start(c2[:, k:k + 1], col(a[v], B)).then_inc(s_in, 16)
                for m in range(FM):
                    if m >= 2:
                        sp.wait_ge(s_tp, m - 1)
                    sp.dma_start(w1s[:, m % 2], a["L1_gnn_w1"][m * P:(m + 1) * P]).then_inc(s_w1d[m % 2], 16)
                sp.wait_ge(s_in, 16 * loads)
                sp.sem_inc(s_out, 1)
                full = N // B
                ov = out[0:full * B].rearrange("(b p) c -> p b c", p=B)
                with sp.Fori(0, n - 1) as c:
                    sp.wait_ge(s_fin, c + 1)
                    sp.dma_start(ov[:, bass.ds(c * NC, NC), :], fin[:, :, :]).then_inc(s_outd, 16)
                    sp.wait_ge(s_outd, c * 16 + 16)
                    sp.sem_inc(s_out, 1)
                sp.wait_ge(s_fin, n)
                sp.dma_start(ov[:, (n - 1) * NC:full, :], fin[:, 0:full - (n - 1) * NC]).then_inc(s_outd, 16)
                sp.dma_start(out[full * B:N], fin[0:N - full * B, NC - 1]).then_inc(s_outd, 16)
                sp.wait_ge(s_outd, 16 * (n + 1))

            @block.gpsimd
            def _(pool):
                nc.gpsimd.memset(selR[:, :, :], 0.0).then_inc(s_zero, 1)
                pool.wait_ge(s_zero, 1)
                v = selR[:, :, :].rearrange("p k (h c) -> p (k h) c", h=2)
                nc.gpsimd.affine_select(out=v, in_=v, pattern=[[-1, 8], [0, B]], compare_op=ALU.not_equal, fill=1.0,
                                        base=0, channel_multiplier=1).then_inc(s_zero, 1)

            def second(pe, c, m):
                if m == 0:
                    pe.wait_ge(s_y, c + 1)
                pe.wait_ge(s_h, c * FM + m + 5)
                last = nc.tensor.matmul(psY[:, :], w2T[:, m], h2[:, m % 2], start=(m == 0), stop=(m == FM - 1))
                last.then_inc(s_Y, 1)

            @block.tensor
            def _(pe):
                I = E.ident[0:B, 0:B]
                pe.wait_ge(s_in, 16 * loads)
                pe.wait_ge(s_zero, 2)
                for m in range(ntp):
                    if m >= 4:
                        pe.wait_ge(s_tpc, m - 3)
                    b = pw[m % 4]
                    if m < FM:
                        pe.wait_ge(s_w1d[m % 2], 16 * (m // 2 + 1))
                        for k in range(4):
                            last = nc.tensor.matmul(b[:, k * P:(k + 1) * P], w1s[:, m % 2, k * P:(k + 1) * P], E.ident[:, :],
                                                    start=True, stop=True)
                    elif m < FM + 2:
                        for k in range(4):
                            last = nc.tensor.matmul(b[:, k * B:(k + 1) * B], w2s[:, (m - FM) * 4 + k], I, start=True, stop=True)
                    else:
                        for k in (0, 1):
                            last = nc.tensor.matmul(b[64 * k:64 * k + 64, 64 * k:64 * k + 64], fcs[:, 2 * (m - FM - 2) + k],
                                                    I, start=True, stop=True)
                    last.then_inc(s_tp, 1)
                pe.wait_ge(s_tpc, ntp)
                pe.wait_ge(s_rec, 1)
                with pe.Fori(0, n) as c:
                    ds = bass.ds(c * CW, CW)
                    for k in range(4):
                        q = k % 2
                        pe.wait_ge(s_Rw, c * 4 + k + 1)
                        pe.sem_inc(s_taken, 1)
                        nc.tensor.matmul(ps[2 + q][:, :], selR[:, k], rec[:, ds], start=True, stop=True).then_inc(s_Rb, 1)
                        nc.tensor.matmul(ps[q][:, :], FC[:, k], E.acc1[:, k, ds], start=True, stop=True).then_inc(s_R, 1)
                pe.sem_inc(s_Y, 2)
                with pe.Fori(0, n) as c:
                    pe.wait_ge(s_hn, c + 1)
                    for m in range(FM):
                        pe.wait_ge(s_h, c * FM + m + 1)
                        for k in range(4):
                            last = nc.tensor.matmul(ps[m % 4][:, :], w1T[:, k, m * P:(m + 1) * P], hn[:, k],
                                                    start=(k == 0), stop=(k == 3))
                        last.then_inc(s_h2, 1)
                        if m >= 1:
                            second(pe, c, m - 1)
                    second(pe, c, FM - 1)
                pe.wait_ge(s_bn2, 1)
                with pe.Fori(0, n) as c:
                    pe.wait_ge(s_yn, c + 1)
                    pe.sem_inc(s_taken, 1)
                    for j in range(NC):
                        last = nc.tensor.matmul(psZ[:, j], yn[:, j * B:(j + 1) * B], I, start=True, stop=True)
                    last.then_inc(s_Z, 1)

            @block.scalar
            def _(act):
                act.wait_ge(s_fcz, 1)
                for m in range(ntp):
                    act.wait_ge(s_tp, m + 1)
                    b = pw[m % 4]
                    if m < FM:
                        nc.scalar.activation(w1T[:, :, m * P:(m + 1) * P], b.rearrange("p (k c) -> p k c", k=4), ACT.Copy).then_inc(s_tpc, 1)
                    elif m < FM + 2:
                        nc.scalar.activation(w2T[:, (m - FM) * 4:(m - FM) * 4 + 4],
                                             b[:, 0:4 * B].rearrange("p (k c) -> p k c", k=4), ACT.Copy).then_inc(s_tpc, 1)
                    else:
                        for k in (0, 1):
                            q = slice(64 * k, 64 * k + 64)
                            last = nc.scalar.activation(FC[q, m - FM - 2, q], b[q, q], ACT.Copy)
                        last.then_inc(s_tpc, 1)
                with act.Fori(0, n) as c:
                    for k in range(4):
                        act.wait_ge(s_Rb, c * 4 + k + 1)
                        act.wait_ge(s_Rw, c * 4 + k + 1)
                        nc.scalar.activation(rb[:, k % 2], ps[2 + k % 2][:, :], ACT.Copy).then_inc(s_rbc, 1)
                act.wait_ge(s_sd, 1)
                nc.scalar.activation(sc1[:, :, 0], sc1[:, :, 0], ACT.Sqrt).then_inc(s_sdd, 1)
                act.wait_ge(s_hn1, 1)
                act.sem_inc(s_h, 4)
                with act.Fori(0, n) as c:
                    for k in range(4):
                        last = nc.scalar.activation(hn[:, k], E.acc1[:, k, bass.ds(c * CW, CW)], ACT.Identity,
                                                    bias=sc1[:, k, 2:3], scale=sc1[:, k, 1:2])
                    last.then_inc(s_hn, 1)
                    for m in range(FM):
                        act.wait_ge(s_h2, c * FM + m + 1)
                        act.wait_ge(s_Y, c * FM + m + 1)
                        nc.scalar.activation(h2[:, m % 2], ps[m % 4][:, :], ACT.Relu, bias=bb1[:, m:m + 1]).then_inc(s_h, 1)
                act.wait_ge(s_sd, 2)
                nc.scalar.activation(sc2[:, 0:1], sc2[:, 0:1], ACT.Sqrt).then_inc(s_sdd, 1)
                act.wait_ge(s_bn2, 1)
                with act.Fori(0, n) as c:
                    nc.scalar.activation(yn[:, :], yT[:, bass.ds(c * CW, CW)], ACT.Identity, bias=sc2[:, 2:3],
                                         scale=sc2[:, 1:2]).then_inc(s_yn, 1)
                    act.wait_ge(s_fin, c + 1)

            @block.vector
            def _(dve):
                link = Link(dve, s_link)
                link(nc.vector.memset(FC[:, :, :], 0.0))
                dve.sem_inc(s_fcz, 1)
                link(nc.vector.tensor_scalar(rec[:, :], E.acc1[0:8, 4, :], 1e-30, None, ALU.max))
                nc.vector.reciprocal(rec[:, :], rec[:, :]).then_inc(s_rec, 1)
                dve.sem_inc(s_Rw, 2)

                def normalized(c, chunk, width):
                    for k in range(4):
                        v = E.acc1[:, k, bass.ds(c * CW, CW)]
                        dve.wait_ge(s_R, c * 4 + k + 1)
                        dve.wait_ge(s_rbc, c * 4 + k + 1)
                        link(nc.vector.tensor_tensor(v, ps[k % 2][:, :], rb[:, k % 2], ALU.mult))
                        nc.vector.tensor_scalar(v, v, c1[:, k, 0:1], None, ALU.add).then_inc(s_Rw, 1)
                        dve.wait_ge(s_Rw, c * 4 + k + 3)
                        last = nc.vector.bn_stats(st1[:, k, chunk], E.acc1[:, k, bass.ds(c * CW, width)])
                    return last

                with dve.Fori(0, n - 1) as c:
                    link.loop(2, c, 4)
                    normalized(c, bass.ds(c, 1), CW)
                link.loop(2, n - 1, 4)
                last = normalized(n - 1, n - 1, edge[n - 1])
                link(last)
                for k in range(4):
                    last = nc.vector.bn_aggr(mv1[:, k], st1[:, k].rearrange("p a b -> p (a b)"))
                link(last)
                batchnorm_scale(nc, dve, link, mv1[:, :, 0], mv1[:, :, 1], sc1[:, :, 0], sc1[:, :, 1], sc1[:, :, 2],
                                c1[:, :, 1], c1[:, :, 2], s_sd, s_sdd, 1)
                dve.sem_inc(s_hn1, 1)
                dve.sem_inc(s_y, 1)
                with dve.Fori(0, n) as c:
                    dve.wait_ge(s_Y, c * FM + FM + 2)
                    nc.vector.tensor_scalar(yT[:, bass.ds(c * CW, CW)], psY[:, :], c2[:, 0:1], None, ALU.add).then_inc(s_y, 1)
                dve.wait_ge(s_y, n + 1)
                for c in range(n):
                    last = nc.vector.bn_stats(st2[:, c], yT[:, c * CW:c * CW + edge[c]])
                link(last)
                link(nc.vector.bn_aggr(mv2[:, :], st2[:, :, :].rearrange("p a b -> p (a b)")))
                batchnorm_scale(nc, dve, link, mv2[:, 0:1], mv2[:, 1:2], sc2[:, 0:1], sc2[:, 1:2], sc2[:, 2:3],
                                c2[:, 1:2], c2[:, 2:3], s_sd, s_sdd, 2)
                dve.sem_inc(s_bn2, 1)
                with dve.Fori(0, n) as c:
                    dve.wait_ge(s_Z, c + 1)
                    dve.wait_ge(s_out, c + 1)
                    nc.vector.tensor_tensor(fin[:, :, :], psZ[:, :, :], E.x1[:, bass.ds(c * NC, NC), :],
                                            ALU.add).then_inc(s_fin, 1)


def batchnorm_scale(nc, dve, link, mean, var, sd, scale, shift, gamma, beta, s_sd, s_sdd, n):
    nc.vector.tensor_scalar(sd, var, 1e-5, None, ALU.add).then_inc(s_sd, 1)
    dve.wait_ge(s_sdd, n)
    link(nc.vector.reciprocal(sd, sd))
    link(nc.vector.tensor_tensor(scale, sd, gamma, ALU.mult))
    link(nc.vector.tensor_tensor(shift, mean, scale, ALU.mult))
    link(nc.vector.tensor_tensor(shift, beta, shift, ALU.subtract))


def phase_setup(nc, E, a, sem):
    NT, NT0 = E.NT, E.NT0
    with ExitStack() as st:
        def tmp(name, shape, dt):
            return st.enter_context(nc.sbuf_tensor(name, shape, dt))

        def pst(name, shape, dt):
            return banks(nc, st, name, shape)

        H = Hist(nc, tmp, pst, sem, "D", NT0)
        HS = Hist(nc, tmp, pst, sem, "S", NT0)
        hiS = tmp("hiS0", [P, NT0], F32)
        loS = tmp("loS0_", [P, NT0], F32)
        idx = tmp("idx", [P, 2, NT0], I32)
        ti = tmp("ti", [P, NT0], I32)
        unset = tmp("unset", [P, 2 * max(E.RD, E.RS)], F32)
        s_ones, s_mask, s_fill, s_in, s_dve, s_low = (sem(n) for n in
                                                      ("s_ones", "s_mask", "s_fill", "s_in", "s_dve", "s_low"))
        s_hz, s_w, s_attr = sem("s_hz"), sem("s_w"), sem("s_attr")
        full = P - 1
        last = E.E - full * NT0
        with nc.Block() as block:
            @block.gpsimd
            def _(pool):
                masks_pool(nc, pool, E, s_ones, s_mask)
                pool.wait_ge(s_low, 1)
                for table, width, done in ((E.sd, E.RD, E.scatD), (E.ss, E.RS, E.scatS)):
                    w = NT * width // 8
                    for k in range(8):
                        pool.dma_start(table[:, k * w:(k + 1) * w].rearrange("p (n w) -> p n w", w=2 * width),
                                       bc(unset[:, None, 0:2 * width], [P, NT // 16, 2 * width])).then_inc(done[k % 2], 16)

            @block.sync
            def _(sp):
                sp.wait_ge(s_fill, 1)
                for k, v in enumerate((a["src"], a["dst"])):
                    sp.dma_start(idx[0:full, k], v[0:full * NT0].rearrange("(p t) -> p t", p=full)).then_inc(s_in, 16)
                    sp.dma_start(idx[full:P, k, 0:last], v[full * NT0:E.E].rearrange("(p t) -> p t", p=1)).then_inc(s_in, 16)
                for t in range(G):
                    for k, n in enumerate(("wk", "wv")):
                        o = 32 * t + 16 * k
                        sp.dma_start(E.W1[16 * t:16 * t + 16, o:o + 16], a[f"L0_gnn_{n}1_w"]).then_inc(s_w, 16)
                        sp.dma_start(E.W2[o:o + 16, o:o + 16], a[f"L0_gnn_{n}2_w"]).then_inc(s_w, 16)
                        sp.dma_start(E.b1[o:o + 16, :], a[f"L0_gnn_{n}1_b"].rearrange("(p c) -> p c", c=1)).then_inc(s_w, 16)
                        sp.dma_start(E.b2[:, o:o + 16], bc(a[f"L0_gnn_{n}2_b"].rearrange("(p c) -> p c", p=1),
                                                           [P, 16])).then_inc(s_w, 16)
                ea = a["edge_attr_16"]
                sp.dma_start(E.attr[0:full, 0:NT0], ea[0:full * NT0].rearrange("(p t) f -> p t f", p=full)).then_inc(s_attr, 16)
                sp.dma_start(E.attr[full:P, 0:last], ea[full * NT0:E.E].rearrange("(p t) f -> p t f", p=1)).then_inc(s_attr, 16)
                sp.wait_ge(s_w, 16 * 8 * G)
                sp.wait_ge(s_in, 64)
                sp.wait_ge(s_attr, 32)

            @block.vector
            def _(dve):
                link = Link(dve, s_dve)
                nc.vector.memset(E.attr[96:P, 0:NT0], 0.0)
                nc.vector.memset(E.attr[:, NT0:], 0.0)
                nc.vector.memset(E.W1[:, :], 0.0)
                nc.vector.memset(E.W2[:, :], 0.0)
                nc.vector.memset(idx[96:P], E.NB * B - 1).then_inc(s_fill, 1)
                nc.vector.memset(unset[:, :], -1.0).then_inc(s_low, 1)
                nc.vector.memset(H.zero[:, :], 0.0).then_inc(s_hz, 1)
                nc.vector.memset(HS.zero[:, :], 0.0).then_inc(s_hz, 1)
                link(nc.vector.memset(E.key0[:, :, NT0:], -1.0))
                link(nc.vector.memset(E.hi0[:, NT0:], -1.0))
                link(nc.vector.memset(E.lo0[:, NT0:], -1.0))
                dve.wait_ge(s_mask, 1)
                link(nc.vector.tensor_copy(E.iota[:, :], E.iota_i[:, :]))
                link(nc.vector.tensor_copy(E.identb[:, :], E.ident[:, :]))
                link(nc.vector.tensor_scalar(E.notafter[:, :], E.after[:, :], -1.0, None, ALU.add))
                dve.wait_ge(s_in, 64)
                split_keys(nc, link, E.key0[:, 1, 0:NT0], idx[:, 1], E.hi0[:, 0:NT0], E.lo0[:, 0:NT0], ti[:, :])
                histogram_vector(nc, dve, E, H, E.hi0, E.lo0)
                split_keys(nc, link, E.key0[:, 0, 0:NT0], idx[:, 0], hiS[:, :], loS[:, :], ti[:, :])
                histogram_vector(nc, dve, E, HS, hiS, loS)
                base_vector(nc, dve, E, H, link, E.T0D[:, :], E.blkD[:, :])
                base_vector(nc, dve, E, HS, link, E.T0S[:, :], E.blkS[:, :])

            @block.tensor
            def _(pe):
                pe.wait_ge(s_hz, 2)
                for h in (H, HS):
                    pe.sem_inc(h.counted, 2)
                    histogram_tensor(nc, pe, E, h)
                for h in (H, HS):
                    base_tensor(nc, pe, E, h)


def phase_nets(nc, E, sem):
    NT0, EF = E.NT0, E.EF
    NG = 4
    CW = NG * P
    with ExitStack() as st:
        def tmp(name, shape):
            return st.enter_context(nc.sbuf_tensor("e_" + name, shape, F32))

        U = tmp("U", [P, NT0 // G * P])
        at = tmp("at", [P, 2, NG * G * EF])
        atT = tmp("atT", [G * EF, 2, CW])
        ssp = tmp("ssp", [P, 2, CW])
        psT = [banks(nc, st, f"e_psT{k}", [G * EF, CW]) for k in (0, 1)]
        psN = [banks(nc, st, f"e_psN{k}", [P, CW]) for k in (0, 1)]
        psW = [banks(nc, st, f"e_psW{k}", [P, CW]) for k in (0, 1)]
        s_at, s_T, s_Tc, s_N, s_Nc, s_exp, s_ln, s_ssp, s_W, s_Wc, s_b, s_link, s_taken = (
            sem("e_" + k) for k in ("at", "T", "Tc", "N", "Nc", "exp", "ln", "ssp", "W", "Wc", "b", "link", "taken"))
        n = NT0 // (NG * G)
        half = n // 4 * 2
        assert NT0 % (NG * G) == 0 and n % 2 == 0
        cuts = (slice(0, half * CW), slice(half * CW, n * CW))

        def two(it, par, k=0):
            return it * 2 + par + 1 + k

        def at_chunk(it, par):
            return bass.ds(it * (2 * CW) + par * CW, CW)

        with nc.Block() as block:
            @block.tensor
            def _(pe):
                nc.tensor.matmul(psW[0][:, 0:P], E.ones[:, :], E.W2[:, :], start=True, stop=True).then_inc(s_b, 1)
                pe.sem_inc(s_N, 2)

                def transposed(par):
                    pe.sem_inc(s_taken, 1)
                    for q in range(NG):
                        last = nc.tensor.matmul(psT[par][:, q * P:(q + 1) * P], at[:, par, q * G * EF:(q + 1) * G * EF],
                                                E.ident[:, :], start=True, stop=True)
                    last.then_inc(s_T, 1)

                pe.wait_ge(s_at, 1)
                pe.wait_ge(s_Tc, 1)
                transposed(0)
                with pe.Fori(0, n // 2) as it:
                    for par in (0, 1):
                        c1 = two(it, par)
                        pe.wait_ge(s_at, c1 + 1)
                        pe.wait_ge(s_Tc, c1 + 1)
                        transposed(1 - par)
                        pe.wait_ge(s_Tc, c1 + 2)
                        pe.wait_ge(s_Nc, c1)
                        pe.sem_inc(s_taken, 1)
                        nc.tensor.matmul(psN[par][:, :], E.W1[:, :], atT[:, par], start=True, stop=True).then_inc(s_N, 1)
                with pe.Fori(0, n // 2) as it:
                    for par in (0, 1):
                        c1 = two(it, par)
                        pe.wait_ge(s_ssp, c1)
                        pe.wait_ge(s_Wc, c1)
                        pe.sem_inc(s_taken, 1)
                        for q in range(NG):
                            last = nc.tensor.matmul(psW[par][:, q * P:(q + 1) * P], ssp[:, par, q * P:(q + 1) * P],
                                                    E.W2[:, :], start=True, stop=True)
                        last.then_inc(s_W, 1)

            @block.scalar
            def _(act):
                def attrs(tile0, par):
                    nc.scalar.activation(at[:, par].rearrange("p (t f) -> p t f", f=EF),
                                         E.attr[:, bass.ds(tile0, NG * G), :], ACT.Copy).then_inc(s_at, 1)

                act.sem_inc(s_T, 2)
                attrs(0, 0)
                attrs(NG * G, 1)
                with act.Fori(0, n // 2) as it:
                    for par in (0, 1):
                        c1 = two(it, par)
                        act.wait_ge(s_T, c1 + 2)
                        attrs(it * (2 * NG * G) + (par + 2) * NG * G, par)
                        act.wait_ge(s_N, c1 + 2)
                        nc.scalar.activation(E.X[:, at_chunk(it, par)], psN[par][:, :], ACT.Identity, bias=E.b1[:, 0:1])
                        nc.scalar.activation(U[:, at_chunk(it, par)], psN[par][:, :], ACT.Abs,
                                             bias=E.b1[:, 0:1]).then_inc(s_Nc, 1)
                act.wait_ge(s_Nc, n + 2)
                for c in cuts:
                    nc.scalar.activation(U[:, c], U[:, c], ACT.Exp, scale=-1.0).then_inc(s_exp, 1)
                for k, c in enumerate(cuts):
                    act.wait_ge(s_exp, k + 1)
                    nc.scalar.activation(U[:, c], U[:, c], ACT.Ln, bias=1.0).then_inc(s_ln, 1)

            @block.vector
            def _(dve):
                link = Link(dve, s_link)
                dve.sem_inc(s_Tc, 2)
                dve.sem_inc(s_Nc, 2)
                dve.wait_ge(s_b, 1)
                link(nc.vector.scalar_tensor_tensor(E.b2[:, :], psW[0][:, 0:P], -float(np.log(2.0)), E.b2[:, :],
                                                    ALU.mult, ALU.add))
                dve.sem_inc(s_Wc, 2)
                with dve.Fori(0, n // 2) as it:
                    for par in (0, 1):
                        dve.wait_ge(s_T, two(it, par) + 2)
                        dve.wait_ge(s_N, two(it, par))
                        nc.vector.tensor_copy(atT[:, par], psT[par][:, :]).then_inc(s_Tc, 1)
                done = 0
                for k, pairs in enumerate((n // 4, n // 2)):
                    dve.wait_ge(s_ln, k + 1)
                    with dve.Fori(done, pairs) as it:
                        for par in (0, 1):
                            c = at_chunk(it, par)
                            dve.wait_ge(s_Wc, two(it, par))
                            nc.vector.scalar_tensor_tensor(ssp[:, par], E.X[:, c], 0.0, U[:, c], ALU.max,
                                                           ALU.add).then_inc(s_ssp, 1)
                        for par in (0, 1):
                            dve.wait_ge(s_W, two(it, par))
                            nc.vector.tensor_tensor(
                                E.X[:, at_chunk(it, par)].rearrange("p (q c) -> p q c", q=NG),
                                psW[par][:, :].rearrange("p (q c) -> p q c", q=NG),
                                bc(E.b2[:, None, :], [P, NG, P]), ALU.add).then_inc(s_Wc, 1)
                    done = pairs
                dve.wait_ge(s_Wc, n + 2)


def phase_sort_dst(nc, E, sem):
    NT, NT0 = E.NT, E.NT0
    W = 2 * E.EF
    with ExitStack() as st:
        def tmp(name, shape, dt):
            return st.enter_context(nc.sbuf_tensor(name, shape, dt))

        def pst(name, shape, dt):
            return banks(nc, st, name, shape)

        R = Rank(nc, tmp, pst, sem, "RD")
        pay = tmp("payD", [P, 2, G, E.RD], F32)
        s_link, s_pay, s_taken = sem("s_linkD"), sem("s_payD"), sem("s_takenD")
        n = NT0 // (2 * G)
        keys = (E.hi0, E.lo0)
        with nc.Block() as block:
            @block.tensor
            def _(pe):
                pe.sem_inc(R.look_ready, 2)
                pe.wait_ge(R.oh_ready, 1)
                pe.wait_ge(R.T_ready, 1)
                rank_tensor_hist(nc, pe, E, R, 0)
                with pe.Fori(0, n) as it:
                    for par in (0, 1):
                        rank_tensor_same(nc, pe, E, R, it, par)
                        rank_tensor_look(nc, pe, R, it, par)
                        rank_tensor_next(nc, pe, E, R, it, par)
                        rank_tensor_look_tile(nc, pe, R, it, par)

            @block.scalar
            def _(act):
                act.sem_inc(R.M_ready, 1)
                rank_scalar(nc, act, R, 0, 1)
                with act.Fori(0, n) as it:
                    for par in (0, 1):
                        rank_scalar_same(nc, act, R, it, par)
                        rank_scalar(nc, act, R, 1 - par, upto(it, par) + 1)
                        act.wait_ge(E.scatD[par], 64 * it + 64)
                        nc.scalar.activation(pay[:, par, :, 0:2],
                                             E.key0[:, :, tiles(it, par)].rearrange("p k t -> p t k"), ACT.Copy)
                        nc.scalar.activation(pay[:, par, :, 2:E.RD],
                                             E.X[:, bass.ds(it * (2 * G * W) + par * G * W, G * W)].rearrange(
                                                 "p (t c) -> p t c", c=W), ACT.Copy).then_inc(s_pay, 1)

            @block.vector
            def _(dve):
                link = Link(dve, s_link)
                dve.sem_inc(R.look_free, 1)
                rank_zero(nc, R, link)
                for par in (0, 1):
                    rank_onehots_hi(nc, E, R, keys, par * G, par)
                    rank_onehots_lo(nc, E, R, keys, par * G, par)
                    if par == 0:
                        rank_positions(nc, link, R, 0, E.T0D[:, :])
                dve.wait_ge(R.hT_ready, 1)
                rank_positions(nc, link, R, 1, R.psT[:, :])
                with dve.Fori(0, n) as it:
                    link.loop(3, it, 2 * RANK_LINKS)
                    for par in (0, 1):
                        rank_onehots_hi(nc, E, R, keys, it * (2 * G) + (par + 2) * G, par)
                        rank_vector_next(nc, dve, R, link, it, par)
                        rank_rows(nc, dve, E, R, keys, link, it, par, NT, E.scatD)
                    assert link.n == 2 * RANK_LINKS, link.n

            @block.gpsimd
            def _(pool):
                with pool.Fori(0, n) as it:
                    for par in (0, 1):
                        pool.wait_ge(R.row_ready, upto(it, par))
                        pool.wait_ge(s_pay, upto(it, par))
                        pool.sem_inc(s_taken, 1)
                        for j in range(G):
                            nc.gpsimd.indirect_dma_start(
                                out=E.sd_rows, out_offset=bass.IndirectOffsetOnAxis(ap=R.row[:, par, j:j + 1], axis=0),
                                in_=pay[:, par, j, :], in_offset=None).then_inc(E.scatD[par], 16)
                for par in (0, 1):
                    pool.wait_ge(E.scatD[par], 64 * n + 64)


def build(nc, a, out):
    E = Env()
    E.N, E.E, E.EF = a["x"].shape[0], a["src"].shape[0], a["edge_attr_16"].shape[1]
    E.NB = -(-E.N // B)
    per = 2 * G * P
    E.NT0 = -(-E.E // per) * 2 * G
    most = (E.NT0 * P + E.NB * (P - 1)) // P
    E.NT = -(-most // (4 * G)) * 4 * G
    E.RD = 2 + 2 * E.EF
    E.RS = 2 * B + 2
    sdt = nc.dram_tensor("by_dst", (P, E.NT * E.RD), F32, kind="Internal").ap()
    E.sd = sdt
    sst = nc.dram_tensor("by_src", (P, E.NT * E.RS), F32, kind="Internal").ap()
    E.ss = sst
    E.ss_rows = sst.rearrange("p (t f) -> (p t) f", f=E.RS)
    E.table1 = nc.dram_tensor("table1", (E.NB * B, B + 8), F32, kind="Internal").ap()
    E.hg = nc.dram_tensor("by_dst_h", (P, E.NT * (B + 8)), F32, kind="Internal").ap()
    E.sd_rows = sdt.rearrange("p (t f) -> (p t) f", f=E.RD)
    with ExitStack() as top:
        def sb(name, shape, dt):
            return top.enter_context(nc.sbuf_tensor(name, shape, dt))

        taken = []

        def sem(name):
            taken.append(nc.alloc_semaphore(name))
            return taken[-1]

        masks(E, sb)
        E.T0D = sb("T0D", [B, B], F32)
        E.blkD = sb("blkD", [1, E.NT], I32)
        E.T0S = sb("T0S", [B, B], F32)
        E.blkS = sb("blkS", [1, E.NT], I32)
        E.loD = sb("loD", [P, E.NT + 2 * G], F32)
        E.keyD = sb("keyD", [P, E.NT], F32)
        E.srcI = sb("srcI", [P, E.NT + G], I32)
        E.x1 = sb("x1", [B, E.NB, B], F32)
        E.ertab = sb("ertab", [B, E.NB, 8], F32)
        E.scatD = [sem("scatD0"), sem("scatD1")]
        E.scatS = [sem("scatS0"), sem("scatS1")]

        def hand_over():
            nc.clear_and_free_semaphores(taken)
            taken.clear()
            nc.all_engine_barrier()

        def stack(st):
            return lambda name, shape, dt: st.enter_context(nc.sbuf_tensor(name, shape, dt))

        with ExitStack() as st:
            sb2 = stack(st)
            E.key0 = sb2("key0", [P, 2, E.NT0 + 2 * G], F32)
            E.hi0 = sb2("hi0", [P, E.NT0 + 2 * G], F32)
            E.lo0 = sb2("lo0", [P, E.NT0 + 2 * G], F32)
            E.X = sb2("X", [P, E.NT0 * 2 * E.EF], F32)
            with ExitStack() as st2:
                sb3 = stack(st2)
                E.attr = sb3("attr", [P, E.NT0 + 8 * G, E.EF], F32)
                E.W1 = sb3("W1", [B, P], F32)
                E.W2 = sb3("W2", [P, P], F32)
                E.b1 = sb3("b1", [P, 1], F32)
                E.b2 = sb3("b2", [P, P], F32)
                phase_setup(nc, E, a, sem)
                phase_nets(nc, E, sem)
            phase_sort_dst(nc, E, sem)
        with ExitStack() as first:
            sb1 = stack(first)
            E.h0T = sb1("h0T", [B, E.NB * B], F32)
            E.wvl = sb1("wvl", [B, P], F32)
            E.qA = sb1("qA", [P, E.NB, B + 4], BF16)
            E.qC = sb1("qC", [B, E.NB, B + 4], BF16)
            with ExitStack() as st:
                E.kvA = stack(st)("kvA", [P, E.NB, 2 * B], BF16)
                E.kvC = stack(st)("kvC", [B, E.NB, 2 * B], BF16)
                phase_nodes0(nc, E, a, sem)
                phase_sort_src(nc, E, sem)
            hand_over()
            E.acc0 = sb1("acc0", [B + 4, E.NB * B], F32)
            with ExitStack() as st:
                sb2 = stack(st)
                E.lg0 = sb2("lg0", [P, E.NT + 2 * G, 4], F32)
                E.loS = sb2("loS0", [P, E.NT + 2 * G], F32)
                E.keyS = sb2("keyS0", [P, E.NT + 2 * G], F32)
                phase_logits0(nc, E, sem)
                phase_softmax(nc, E, sem, "m0_", E.lg0, E.keyS, 4, E.acc0[:, :])
                phase_sum0(nc, E, sem)
            phase_nodes1(nc, E, a, sem)
        hand_over()
        with ExitStack() as second:
            sb1 = stack(second)
            E.acc1 = sb1("acc1", [P, 5, E.NB * B], F32)
            with ExitStack() as st:
                E.lg1 = stack(st)("lg1", [P, E.NT + G, 8], F32)
                phase_gather1(nc, E, sem)
                phase_softmax(nc, E, sem, "m1_", E.lg1, E.keyD, 8, E.acc1[:, :, :])
                phase_sum1(nc, E, sem)
            phase_dense1(nc, E, a, out, sem)


_OUTS = [((3125, 64), 'float32')]


def kernel(**inputs):
    import numpy as _np
    import concourse.bacc as _bacc
    from concourse import mybir as _mybir
    from concourse.bass_utils import run_bass_kernel_spmd as _run

    nc = _bacc.Bacc("TRN2", target_bir_lowering=False, num_devices=1)
    arrays, aps = {}, {}
    for name in inputs:
        a = _np.ascontiguousarray(inputs[name])
        arrays[f"in_{name}"] = a
        aps[name] = nc.dram_tensor(f"in_{name}", a.shape, _mybir.dt.from_np(a.dtype), kind="ExternalInput").ap()
    shape, dtype = _OUTS[0]
    out = nc.dram_tensor("out_0", shape, _mybir.dt.from_np(_np.dtype(dtype)), kind="ExternalOutput").ap()
    build(nc, aps, out)
    r = _run(nc, [arrays], core_ids=[0])
    return r.results[0]["out_0"]
```
